# Optimizing a Trainium2 kernel written in Bass

```python
import numpy as np
import jax
import jax.numpy as jnp

def _softmax(x, axis=-1):
    return jax.nn.softmax(x, axis=axis)

def _gelu(x):
    return jax.nn.gelu(x, approximate=True)

def _silu(x):
    return jax.nn.silu(x)

def _sigmoid(x):
    return jax.nn.sigmoid(x)

def _layernorm(x, axis=-1, eps=1e-05):
    m = jnp.mean(x, axis=axis, keepdims=True)
    v = jnp.var(x, axis=axis, keepdims=True)
    return (x - m) / jnp.sqrt(v + eps)

def _scatter_add(tgt, idx, src, axis=0):
    return tgt.at[idx].add(src)

def _segment_sum(src, seg, n):
    return jax.ops.segment_sum(src, seg, n)
kernel_name = 'mk_conv_preact_d2_conv_nhwc192_r2_d35baf'

def setup_inputs(seed: int=0):
    np.random.seed(seed)
    _w = jnp.asarray

    def _rec_inputs():
        import jax
        import jax.numpy as jnp
        _gk = jax.random.key(seed)
        x = -0.0002221 + 1 * jax.random.normal(jax.random.fold_in(_gk, 1), (2, 128, 128, 96), jnp.float32)
        return x
    x = _rec_inputs()

    def _L0_conv_setup():
        import jax, jax.numpy as jnp
        import numpy as np
        DN = ('NHWC', 'HWIO', 'NHWC')

        def _mdta(x, w_qkv, b_qkv, w_dw, b_dw, temperature, w_out, b_out):
            B, H, W, C = x.shape
            heads = temperature.shape[1]
            c = C // heads
            qkv = jax.lax.conv_general_dilated(x, w_qkv, (1, 1), 'SAME', dimension_numbers=DN) + b_qkv
            qkv = jax.lax.conv_general_dilated(qkv, w_dw, (1, 1), 'SAME', dimension_numbers=DN, feature_group_count=3 * C) + b_dw
            q, k, v = jnp.split(qkv, 3, axis=-1)

            def to_heads(t):
                return t.reshape(B, H * W, heads, c).transpose(0, 2, 3, 1)
            q, k, v = (to_heads(q), to_heads(k), to_heads(v))
            q = q / jnp.maximum(jnp.linalg.norm(q, axis=-1, keepdims=True), 1e-12)
            k = k / jnp.maximum(jnp.linalg.norm(k, axis=-1, keepdims=True), 1e-12)
            attn = jnp.einsum('bhcn,bhdn->bhcd', q, k) * temperature
            attn = jax.nn.softmax(attn, axis=-1)
            out = jnp.einsum('bhcd,bhdn->bhcn', attn, v)
            out = out.transpose(0, 3, 1, 2).reshape(B, H, W, C)
            out = jax.lax.conv_general_dilated(out, w_out, (1, 1), 'SAME', dimension_numbers=DN) + b_out
            return out
        key = jax.random.key(seed)
        ks = jax.random.split(key, 5)
        B, H, W, C = (2, 128, 128, 96)
        heads = 4
        x = jax.random.normal(ks[0], (B, H, W, C), dtype=jnp.float32)
        w_qkv = jax.random.normal(ks[1], (1, 1, C, 3 * C), dtype=jnp.float32) * 0.05
        b_qkv = jnp.zeros((3 * C,), dtype=jnp.float32)
        w_dw = jax.random.normal(ks[2], (3, 3, 1, 3 * C), dtype=jnp.float32) * 0.05
        b_dw = jnp.zeros((3 * C,), dtype=jnp.float32)
        temperature = jnp.ones((1, heads, 1, 1), dtype=jnp.float32)
        w_out = jax.random.normal(ks[3], (1, 1, C, C), dtype=jnp.float32) * 0.05
        b_out = jnp.zeros((C,), dtype=jnp.float32)
        return {'x': x, 'w_qkv': w_qkv, 'b_qkv': b_qkv, 'w_dw': w_dw, 'b_dw': b_dw, 'temperature': temperature, 'w_out': w_out, 'b_out': b_out}
    _L0_conv_all = _L0_conv_setup()
    _L0_conv_in = {k: v for k, v in _L0_conv_all.items() if k in ('w_qkv', 'b_qkv', 'w_dw', 'b_dw', 'temperature', 'w_out', 'b_out')}
    del _L0_conv_all

    def _L1_conv_setup():
        import jax, jax.numpy as jnp
        import numpy as np
        G = 16
        K = 3
        key = jax.random.key(seed)
        feature = jax.random.normal(key, (2, 64, 96, 96), dtype=jnp.float32)
        return {'feature': feature}
    _L1_conv_all = _L1_conv_setup()
    _L1_conv_in = {k: v for k, v in _L1_conv_all.items() if k in ()}
    del _L1_conv_all
    return {'x': x, 'L0_conv_w_qkv': _L0_conv_in['w_qkv'], 'L0_conv_b_qkv': _L0_conv_in['b_qkv'], 'L0_conv_w_dw': _L0_conv_in['w_dw'], 'L0_conv_b_dw': _L0_conv_in['b_dw'], 'L0_conv_temperature': _L0_conv_in['temperature'], 'L0_conv_w_out': _L0_conv_in['w_out'], 'L0_conv_b_out': _L0_conv_in['b_out']}

def reference(x, L0_conv_w_qkv, L0_conv_b_qkv, L0_conv_w_dw, L0_conv_b_dw, L0_conv_temperature, L0_conv_w_out, L0_conv_b_out):
    import jax
    import jax.numpy as jnp

    def _L0_conv_ref(x, w_qkv, b_qkv, w_dw, b_dw, temperature, w_out, b_out):
        import jax, jax.numpy as jnp
        import numpy as np
        DN = ('NHWC', 'HWIO', 'NHWC')

        def _mdta(x, w_qkv, b_qkv, w_dw, b_dw, temperature, w_out, b_out):
            B, H, W, C = x.shape
            heads = temperature.shape[1]
            c = C // heads
            qkv = jax.lax.conv_general_dilated(x, w_qkv, (1, 1), 'SAME', dimension_numbers=DN) + b_qkv
            qkv = jax.lax.conv_general_dilated(qkv, w_dw, (1, 1), 'SAME', dimension_numbers=DN, feature_group_count=3 * C) + b_dw
            q, k, v = jnp.split(qkv, 3, axis=-1)

            def to_heads(t):
                return t.reshape(B, H * W, heads, c).transpose(0, 2, 3, 1)
            q, k, v = (to_heads(q), to_heads(k), to_heads(v))
            q = q / jnp.maximum(jnp.linalg.norm(q, axis=-1, keepdims=True), 1e-12)
            k = k / jnp.maximum(jnp.linalg.norm(k, axis=-1, keepdims=True), 1e-12)
            attn = jnp.einsum('bhcn,bhdn->bhcd', q, k) * temperature
            attn = jax.nn.softmax(attn, axis=-1)
            out = jnp.einsum('bhcd,bhdn->bhcn', attn, v)
            out = out.transpose(0, 3, 1, 2).reshape(B, H, W, C)
            out = jax.lax.conv_general_dilated(out, w_out, (1, 1), 'SAME', dimension_numbers=DN) + b_out
            return out
        return _mdta(x, w_qkv, b_qkv, w_dw, b_dw, temperature, w_out, b_out)

    def _L1_conv_ref(feature):
        import jax, jax.numpy as jnp
        import numpy as np
        G = 16
        K = 3
        B, C, H, W = feature.shape
        Cg = C // G
        Hm, Wm = (H - K + 1, W - K + 1)
        L = Hm * Wm
        slices = [feature[:, :, ki:ki + Hm, kj:kj + Wm] for ki in range(K) for kj in range(K)]
        patches = jnp.stack(slices, axis=2)
        motif = patches.reshape(B, G, Cg * 9, L).reshape(B, G, 9, Cg, L)
        gram = jnp.einsum('bgjcl,bgjdl->bgjcd', motif, motif)
        sq = jnp.einsum('bgjcl,bgjcl->bgjc', motif, motif)
        d2 = sq[..., :, None] + sq[..., None, :] - 2.0 * gram
        eye = jnp.eye(Cg, dtype=bool)
        d2 = jnp.where(eye, jnp.inf, d2)
        nn_idx = jnp.argmin(d2, axis=-1)
        u_max = jnp.max(nn_idx, axis=-1)
        c_max = jnp.sum(nn_idx == u_max[..., None], axis=-1).astype(feature.dtype)
        motif_nn = jnp.take_along_axis(motif, u_max[..., None, None], axis=3)
        term = jnp.floor(motif * motif_nn * c_max[..., None, None] / Cg)
        batch_mask = (jnp.arange(B) != 0).astype(feature.dtype).reshape(B, 1, 1, 1, 1)
        out_ser = motif * batch_mask + term
        ser2 = out_ser.reshape(B, G, 9 * Cg, L).reshape(B, G, Cg, 9, Hm, Wm)
        out = jnp.zeros((B, G, Cg, H, W), feature.dtype)
        for k in range(K * K):
            ki, kj = (k // K, k % K)
            out = out.at[:, :, :, ki:ki + Hm, kj:kj + Wm].add(ser2[:, :, :, k])
        return out.reshape(B, C, H, W)

    def _gn(v, G=32, eps=1e-05):
        B_, H_, W_, C_ = v.shape
        g = v.reshape(B_, H_, W_, G, C_ // G)
        m = jnp.mean(g, axis=(1, 2, 4), keepdims=True)
        s = jnp.var(g, axis=(1, 2, 4), keepdims=True)
        return ((g - m) / jnp.sqrt(s + eps)).reshape(v.shape)

    def _ln_c(v, eps=1e-06):
        m = jnp.mean(v, axis=-1, keepdims=True)
        s = jnp.var(v, axis=-1, keepdims=True)
        return (v - m) / jnp.sqrt(s + eps)

    def _ln_t(v, eps=1e-05):
        m = jnp.mean(v, axis=-1, keepdims=True)
        s = jnp.var(v, axis=-1, keepdims=True)
        return (v - m) / jnp.sqrt(s + eps)

    def _to_tokens(v):
        B_, H_, W_, C_ = v.shape
        return v.reshape(B_, H_ * W_, C_)

    def _from_tokens(t, like):
        return t.reshape(like.shape)
    x = x + _L0_conv_ref(_gn(x), L0_conv_w_qkv, L0_conv_b_qkv, L0_conv_w_dw, L0_conv_b_dw, L0_conv_temperature, L0_conv_w_out, L0_conv_b_out)
    x = x + _L1_conv_ref(_gn(x))
    return x

_drawn_inputs = setup_inputs


def setup_inputs(seed=0):
    import zlib

    import numpy as np

    out = dict(_drawn_inputs(seed))
    spreads = {'L0_conv_b_qkv': (0.0, 0.289),
     'L0_conv_b_dw': (0.0, 0.1),
     'L0_conv_temperature': (1.0, 0.6),
     'L0_conv_b_out': (0.0, 0.1)}
    factors = {}
    for name, (base, spread) in spreads.items():
        noise = np.random.default_rng([zlib.crc32(name.encode()), seed]).standard_normal(out[name].shape)
        drawn = base * np.exp(spread * noise) if base else spread * noise
        out[name] = jnp.asarray(drawn.astype(out[name].dtype))
    for name, factor in factors.items():
        out[name] = (out[name] * factor).astype(out[name].dtype)
    return out
```

```python
from contextlib import ExitStack

import concourse.bass as bass
from concourse import mybir

ALU = mybir.AluOpType
ACT = mybir.ActivationFunctionType
X = mybir.AxisListType.X
F32 = mybir.dt.float32
F16 = mybir.dt.float16
BF16 = mybir.dt.bfloat16
I32 = mybir.dt.int32
U32 = mybir.dt.uint32

P = 128
B, H, W, C = 2, 128, 128, 96
HEADS = 4
HC = C // HEADS
CV = C + 1
GN = 32
GC = C // GN
TAPS = [(dy, dx) for dy in range(3) for dx in range(3)]
WSCALE = 1024.0
PLANE = W * C
MG = 16
MC = 8
KK = 9
MR = MC * KK
HM, WM = W - 2, C - 2
ROUND = 1.5 * 2.0 ** 23
BIG = 1.0e30
PADW = W + 2
XCR = C + 6
QROWS = 32
NQ = H // QROWS


def by_planes(d):
    return d.rearrange("y (x c) -> x y c", c=C)


class Count:

    def __init__(self, eng, sem):
        self.eng, self.sem, self.n = eng, sem, 0

    def done(self, ins):
        self.n += 1
        ins.then_inc(self.sem, 1)
        return self.n

    def then_wait(self, ins):
        self.eng.wait_ge(self.sem, self.done(ins))


def chunk_stats(nc, img, row, stats, q, groups):
    for g in groups:
        last = nc.vector.bn_stats(stats[:, g, bass.ds(q, 1), :].rearrange("p a s -> p (a s)"),
                                  img[:, bass.ds(row, QROWS), GC * g:GC * g + GC])
    return last


def group_stats_local(nc, c, stats, part, dev):
    parts = stats[:].rearrange("p g q (e s) -> p g (q e) s", s=3)
    m, v = parts[:, :, :, 1], parts[:, :, :, 2]
    c.then_wait(nc.vector.tensor_reduce(part[:, 0, :], m, X, ALU.add))
    nc.vector.tensor_reduce(part[:, 1, :], v, X, ALU.add)
    c.then_wait(nc.vector.tensor_scalar(part[:, 0, :], part[:, 0, :], 0.5 / NQ, None, ALU.mult))
    c.then_wait(nc.vector.tensor_tensor(dev[:], m, part[:, 0, :].unsqueeze(2).to_broadcast([P, GN, 2 * NQ]),
                                        ALU.subtract))
    c.then_wait(nc.vector.tensor_tensor(dev[:], dev[:], dev[:], ALU.mult))
    c.then_wait(nc.vector.tensor_reduce(part[:, 2, :], dev[:], X, ALU.add))
    c.then_wait(nc.vector.scalar_tensor_tensor(part[:, 1, :], part[:, 2, :], float(QROWS * GC // 2),
                                               part[:, 1, :], ALU.mult, ALU.add))
    c.then_wait(nc.vector.tensor_scalar(part[:, 1, :], part[:, 1, :], 1.0 / (H * GC), None, ALU.mult))


def group_stats(nc, dve, c, stats, dev, part, ps, mom, ready, summed, rooted):
    group_stats_local(nc, c, stats, part, dev)
    c.then_wait(nc.vector.tensor_copy(part[:, 3, :], part[:, 0, :]))
    dve.sem_inc(ready, 1)
    dve.wait_ge(summed, 1)
    c.then_wait(nc.vector.tensor_copy(mom[:, 0, :], ps[:, 0, :]))
    c.then_wait(nc.vector.tensor_tensor(part[:, 0, :], part[:, 0, :], mom[:, 0, :], ALU.subtract))
    c.then_wait(nc.vector.tensor_tensor(part[:, 0, :], part[:, 0, :], part[:, 0, :], ALU.mult))
    c.then_wait(nc.vector.tensor_tensor(part[:, 1, :], part[:, 1, :], part[:, 0, :], ALU.add))
    dve.sem_inc(ready, 1)
    dve.wait_ge(rooted, 1)
    c.then_wait(nc.vector.reciprocal(mom[:, 1, :], mom[:, 1, :]))


def group_stats_sums(nc, pe, k, part, ps, ready, summed):
    for step, line in ((0, 3), (1, 1)):
        pe.wait_ge(ready, step + 1)
        nc.tensor.matmul(ps[:, step, :], k["mean_ones"][:, :], part[:, line, :], start=True,
                         stop=True).then_inc(summed, 1)


def group_stats_root(nc, act, k, ps, mom, summed, rooted):
    act.wait_ge(summed, 2)
    nc.scalar.activation(mom[:, 1, :], ps[:, 1, :], ACT.Sqrt, bias=k["eps"][:, 0:1]).then_inc(rooted, 1)


STACKS = 13


def stack_weights(eng, hi, lo, wa, wb, wc, sem):
    def move(dst, src):
        eng.dma_start(dst, src).then_inc(sem, 16)

    by_dx = lambda t, lines, dx: t[lines].rearrange("p (a b) o -> p a b o", b=3)[:, :, dx, :]
    move(wa[0:C], hi[0:C])
    move(wa[C:P], hi[0:32])
    move(wb[0:C], lo[0:C])
    move(wb[C:P], hi[32:64])
    for dx in range(3):
        move(wc[32 * dx:32 * dx + 32], by_dx(hi, slice(64, C), dx))
        move(wc[C + dx:C + dx + 1], by_dx(hi, slice(C, CV), dx))
        move(wc[C + 3 + dx:C + 4 + dx], by_dx(lo, slice(C, CV), dx))


def prepare(nc, k, ins):
    with ExitStack() as ctx:
        sb = lambda n, s, d: ctx.enter_context(nc.sbuf_tensor(n, s, d))
        sem = lambda n: ctx.enter_context(nc.semaphore(n))
        w_aug = sb("w_aug", [CV, 3 * C], F32)
        dw_all = sb("dw_all", [CV, KK, 3 * C], F32)
        b_dw = sb("b_dw_row", [CV, 3 * C], F32)
        w_full = sb("w_full", [CV, KK, 3 * C], F32)
        wqk_hi = sb("wqk_hi", [CV, KK, 2 * C], F16)
        wqk_lo = sb("wqk_lo", [CV, KK, 2 * C], F16)
        plane_i = sb("plane_i", [P, 1], I32)
        iota_i = sb("iota_i", [P, 32], I32)
        ps_wv = ctx.enter_context(nc.psum_tensor("ps_wv", [C, 2, 512], F32))
        weights_in = sem("weights_in")
        zeroed, pooled, made, rounded, turned, dve_own, split, stacked = (
            sem(n) for n in ("pre_zeroed", "pre_pooled", "pre_made", "pre_rounded", "pre_turned", "pre_dve",
                             "pre_split", "pre_stacked"))
        block = ctx.enter_context(nc.Block())

        @block.sync
        def _(sp):
            sp.dma_start(w_aug[0:C, :], ins["w_qkv"].rearrange("a b c o -> (a b c) o")).then_inc(weights_in, 16)
            sp.dma_start(w_aug[C:CV, :], ins["b_qkv"].rearrange("(a o) -> a o", a=1)).then_inc(weights_in, 16)
            sp.dma_start(dw_all[:].rearrange("p t o -> p (t o)"),
                         ins["w_dw"].rearrange("a b c o -> c (a b o)").to_broadcast([CV, KK * 3 * C])
                         ).then_inc(weights_in, 16)
            sp.dma_start(b_dw[C:CV, :], ins["b_dw"].rearrange("(a o) -> a o", a=1)).then_inc(weights_in, 16)
            sp.dma_start(k["w_out"][:, :], ins["w_out"].rearrange("a b c o -> (a b c) o")).then_inc(weights_in, 16)
            sp.dma_start(k["b_out"][C:CV, :], ins["b_out"].rearrange("(a o) -> a o", a=1)).then_inc(weights_in, 16)
            for h in range(HEADS):
                sp.dma_start(k["temp"][HC * h:HC * h + HC, :],
                             ins["temperature"].rearrange("a h b c -> (a b c) h")[:, h:h + 1]
                             .to_broadcast([HC, 1])).then_inc(weights_in, 16)
            sp.wait_ge(split, 1)
            stack_weights(sp, wqk_hi, wqk_lo, k["wa"], k["wb"], k["wc"], stacked)
            sp.wait_ge(stacked, 16 * STACKS)

        @block.gpsimd
        def _(pool):
            nc.gpsimd.memset(k["ident"][:, :], 0.0)
            nc.gpsimd.memset(k["same_head"][:, :], 0.0)
            nc.gpsimd.memset(k["order"][:, :], 0.0)
            nc.gpsimd.memset(k["same_block"][:, :], 1.0)
            nc.gpsimd.memset(k["mean_ones"][:, :], 1.0 / P)
            nc.gpsimd.memset(k["zeros"][:, :], 0.0)
            nc.gpsimd.memset(k["eps"][:, :], 1e-5)
            nc.gpsimd.memset(k["plus_round"][:, :], ROUND)
            nc.gpsimd.memset(k["minus_round"][:, :], -ROUND)
            nc.gpsimd.memset(k["edge_count"][:, :], 3.0)
            nc.gpsimd.iota(plane_i[:, :], [[0, 1]], base=0, channel_multiplier=1)
            nc.gpsimd.iota(iota_i[:, :], [[1, 32]], base=0, channel_multiplier=0).then_inc(zeroed, 1)
            pool.wait_ge(zeroed, 1)
            for c, v in ((0, 1.0), (1, 2.0), (C - 2, 2.0), (C - 1, 1.0)):
                nc.gpsimd.memset(k["edge_count"][:, c:c + 1], v)
            nc.gpsimd.affine_select(k["ident"][:, :], k["ident"][:, :], [[-1, P]], ALU.not_equal, 1.0,
                                    base=0, channel_multiplier=1)
            nc.gpsimd.affine_select(k["order"][:, :], k["order"][:, :], [[-1, MC], [-MC, 3], [-3 * MC, 3]],
                                    ALU.not_equal, 1.0, base=0, channel_multiplier=1)
            nc.gpsimd.affine_select(k["same_head"][:, :], k["same_head"][:, :], [[-HC, HEADS], [0, HC]],
                                    ALU.is_ge, -BIG, base=0, channel_multiplier=1)
            nc.gpsimd.affine_select(k["same_block"][:, :], k["same_block"][:, :], [[-MC, KK], [0, MC]],
                                    ALU.is_ge, 0.0, base=0, channel_multiplier=1).then_inc(zeroed, 1)
            pool.wait_ge(zeroed, 2)
            nc.gpsimd.affine_select(k["same_head"][:, :], k["same_head"][:, :], [[HC, HEADS], [0, HC]],
                                    ALU.is_ge, -BIG, base=HC - 1, channel_multiplier=-1)
            nc.gpsimd.affine_select(k["same_block"][:, :], k["same_block"][:, :], [[MC, KK], [0, MC]],
                                    ALU.is_ge, 0.0, base=MC - 1, channel_multiplier=-1).then_inc(pooled, 1)

        @block.vector
        def _(dve):
            c = Count(dve, dve_own)
            dve.wait_ge(pooled, 1)
            nc.vector.tensor_scalar(k["minus_ident"][:, :], k["ident"][:, :], -1.0, None, ALU.mult)
            nc.vector.tensor_copy(k["iota"][:, :], iota_i[:, :])
            nc.vector.tensor_scalar(k["group_base"][:, :], plane_i[:, :], float(MC * PLANE), None, ALU.mult)
            nc.vector.tensor_reduce(k["own"][:, :], k["ident"][0:MR, 0:MR].rearrange("p (j d) -> p d j", d=MC), X,
                                    ALU.add)
            c.then_wait(nc.vector.tensor_scalar(plane_i[:, :], plane_i[:, :], MC - 1, None, ALU.bitwise_and))
            plane_f = k["plane_f"]
            c.then_wait(nc.vector.tensor_copy(plane_f[:, :], plane_i[:, :]))
            for s in range(KK):
                nc.vector.tensor_scalar(k["second_block"][:, s:s + 1], plane_f[:, :], float(MC - s), None, ALU.is_ge)
            dve.wait_ge(weights_in, 16 * 10)
            c.then_wait(nc.vector.tensor_tensor(w_full[:], dw_all[:],
                                                w_aug[:].unsqueeze(1).to_broadcast([CV, KK, 3 * C]), ALU.mult))
            c.then_wait(nc.vector.tensor_tensor(w_full[C:CV, 4, :], w_full[C:CV, 4, :], b_dw[C:CV, :], ALU.add))
            dve.sem_inc(made, 1)
            dve.wait_ge(rounded, 1)
            nc.vector.scalar_tensor_tensor(wqk_lo[:], w_full[:, :, 0:2 * C], WSCALE, wqk_hi[:], ALU.mult,
                                           ALU.subtract).then_inc(split, 1)
            dve.wait_ge(turned, 1)
            nc.vector.tensor_copy(k["wv_t"][:, 0:5, :], ps_wv[:, 0, 0:5 * CV].rearrange("p (t c) -> p t c", c=CV))
            c.then_wait(nc.vector.tensor_copy(k["wv_t"][:, 5:9, :],
                                              ps_wv[:, 1, 0:4 * CV].rearrange("p (t c) -> p t c", c=CV)))

        @block.scalar
        def _(act):
            act.wait_ge(made, 1)
            nc.scalar.activation(wqk_hi[:], w_full[:, :, 0:2 * C], ACT.Copy, scale=WSCALE).then_inc(rounded, 1)

        @block.tensor
        def _(pe):
            pe.wait_ge(pooled, 1)
            pe.wait_ge(made, 1)
            for t in range(KK):
                last = nc.tensor.transpose(ps_wv[:, t // 5, (t % 5) * CV:(t % 5) * CV + CV],
                                           w_full[:, t, 2 * C:3 * C], k["ident"][0:CV, 0:CV])
            last.then_inc(turned, 1)


ATT_SEMS = ("stat_ready", "stat_summed", "stat_rooted", "a_dve", "padded", "ones_made", "ones_in", "turned",
            "normed", "hi_done", "lo_done", "mom_row", "mom_col", "conv_done", "qk_hi", "qk_lo", "gram_done",
            "gram_out", "att", "att_pe", "att_act", "wf_split", "wf_in", "outs", "evac") \
    + tuple(f"img_in{q}" for q in range(NQ)) + ("rows_ready0", "rows_ready1", "parts_in0", "parts_in1")


def attention(nc, b, k, x, img, x1_dram, x1_out, sems):
    UNITS = H // 4
    PAIRS = H // 2
    MOVES = 6
    with ExitStack() as ctx:
        sb = lambda n, s, d: ctx.enter_context(nc.sbuf_tensor(f"{n}{b}", s, d))
        psum = lambda n, s: ctx.enter_context(nc.psum_tensor(f"{n}{b}", s, F32))
        xa = sb("xa", [P, H + 2, PADW], F16)
        xb = sb("xb", [P, H + 2, PADW], F16)
        xc = sb("xc", [XCR, H + 2, PADW], F16)
        rows_in = sb("rows_in", [P, 2, 4, C], F32)
        z = sb("z", [C, 2, 4 * W], F32)
        low = sb("low", [C, 2, 4, PADW], F16)
        part = sb("part", [P, 4, GN], F32)
        mom = sb("mom", [P, 2, GN], F32)
        mom_c = sb("mom_c", [1, 2, C], F32)
        mom_t = sb("mom_t", [C, 2], F32)
        qk = sb("qk", [P, 2, 2, 4 * C], F16)
        gram = sb("gram", [C, 7 * C], F32)
        sc = sb("sc", [C, C], F32)
        sq = sb("sq", [C, 2, C], F32)
        small = sb("small", [C, 12], F32)
        probs = sb("probs", [C, C], F32)
        mix = sb("mix", [C, C], F32)
        wf = sb("wf", [CV, KK, C], F32)
        wf_hi = sb("wf_hi", [CV, KK, C], F16)
        wf_lo = sb("wf_lo", [CV, KK, C], F16)
        wfa, wfb = sb("wfa", [P, KK, C], F16), sb("wfb", [P, KK, C], F16)
        wfc = sb("wfc", [XCR, 3, C], F16)
        ps = [psum(f"ps_a{j}_", [P, 512]) for j in range(2)]
        ps_g = [psum(f"ps_g{j}_", [P, 512]) for j in range(2)]
        ps_s = psum("ps_s", [P, 2, GN])
        ps_w = psum("ps_w", [P, 2, 512])
        (stat_ready, stat_summed, stat_rooted, dve_own, padded, ones_made, ones_in, turned, normed, hi_done, lo_done,
         mom_row, mom_col, conv_done, qk_hi, qk_lo, gram_done, gram_out, att, att_pe, att_act, wf_split, wf_in,
         outs, evac) = (
            sems[n] for n in ATT_SEMS[:25])
        img_in = [sems[f"img_in{q}"] for q in range(NQ)]
        rows_ready = [sems[f"rows_ready{j}"] for j in range(2)]
        parts_in = [sems[f"parts_in{j}"] for j in range(2)]
        xcol = x[b].rearrange("y x c -> x y c")
        flat = lambda t: t.rearrange("p y x -> p (y x)")
        block = ctx.enter_context(nc.Block())

        @block.sync
        def _(sp):
            for q in range(NQ):
                rows = slice(QROWS * q, QROWS * q + QROWS)
                sp.dma_start(img[:, rows, :], xcol[:, rows, :]).then_inc(img_in[q], 16)

            def load_rows(u, s, first=False):
                if not first:
                    sp.wait_ge(turned, u - 1)
                sp.dma_start(rows_in[:, s], xcol[:, bass.ds(u * 4, 4), :]).then_inc(rows_ready[s], 16)

            def spread(u, s):
                sp.wait_ge(lo_done, u + 1)
                rows = bass.ds(u * (4 * PADW) + PADW, 4 * PADW)
                lo = lambda c, d: low[32 * c:32 * c + 32, s].rearrange("p y x -> p (y x)")[:, d:4 * PADW]
                sp.dma_start(flat(xb[0:C])[:, rows], flat(xa[0:C])[:, rows]).then_inc(parts_in[s], 16)
                sp.dma_start(flat(xa[C:P])[:, rows], lo(0, 0)).then_inc(parts_in[s], 16)
                sp.dma_start(flat(xb[C:P])[:, rows], lo(1, 0)).then_inc(parts_in[s], 16)
                for dx in range(3):
                    sp.dma_start(flat(xc[32 * dx:32 * dx + 32])[:, bass.ds(u * (4 * PADW) + PADW, 4 * PADW - dx)],
                                 lo(2, dx)).then_inc(parts_in[s], 16)

            load_rows(0, 0, True)
            load_rows(1, 1, True)
            sp.wait_ge(ones_made, 1)
            for j in range(1, 6):
                sp.dma_start(flat(xc[C + j:C + j + 1])[:, 0:(H + 2) * PADW - 2],
                             flat(xc[C:C + 1])[:, j % 3:(H + 2) * PADW - 2 + j % 3]).then_inc(ones_in, 16)
            with sp.Fori(0, UNITS // 2 - 1) as i:
                for s in range(2):
                    load_rows(i * 2 + (s + 2), s)
                    spread(i * 2 + s, s)
            for s in range(2):
                spread(UNITS - 2 + s, s)
            sp.wait_ge(wf_split, 1)
            stack_weights(sp, wf_hi, wf_lo, wfa, wfb, wfc, wf_in)
            for q in range(NQ):
                sp.wait_ge(evac, (q + 1) * (QROWS // 4))
                rows = slice(QROWS * q, QROWS * q + QROWS)
                sp.dma_start(by_planes(x1_dram)[:, rows, :], img[:, rows, :]).then_inc(x1_out, 16)

        @block.gpsimd
        def _(pool):
            nc.gpsimd.memset(low[:].rearrange("p s y x -> p (s y x)").bitcast(U32), 0)
            nc.gpsimd.memset(flat(xc[C:CV]), 0.0).then_inc(padded, 1)
            pool.wait_ge(padded, 1)
            nc.gpsimd.memset(xc[C:CV, 1:H + 1, 1:W + 1], 1.0).then_inc(ones_made, 1)
            pool.wait_ge(ones_made, 1)
            for t, n in ((xa, P), (xb, P), (xc, C)):
                for row in (0, H + 1):
                    last = nc.gpsimd.memset(t[0:n, row, :], 0.0)
            for col in (0, W + 1):
                last = nc.gpsimd.memset(xa[0:C, 1:H + 1, col:col + 1], 0.0)
            last.then_inc(padded, 1)

        @block.vector
        def _(dve):
            c = Count(dve, dve_own)
            for q in range(NQ):
                dve.wait_ge(img_in[q], 16)
                last = chunk_stats(nc, img, QROWS * q, k["stats"], q, range(GN))
            c.then_wait(last)
            group_stats(nc, dve, c, k["stats"], k["dev"], part, ps_s, mom, stat_ready, stat_summed, stat_rooted)
            c.then_wait(nc.vector.tensor_copy(mom_c[0:1].rearrange("p m (g j) -> p m g j", j=GC),
                                              mom[0:1].unsqueeze(3).to_broadcast([1, 2, GN, GC])))
            dve.sem_inc(mom_row, 1)
            dve.wait_ge(mom_col, 1)
            c.then_wait(nc.vector.tensor_copy(mom_t[:, :], ps[0][0:C, 0:2]))
            dve.wait_ge(padded, 2)

            def norm(u, s, first=False):
                dve.wait_ge(turned, u + 1)
                if not first:
                    dve.wait_ge(hi_done, u - 1)
                    dve.wait_ge(lo_done, u - 1)
                nc.vector.tensor_scalar(z[:, s, :], ps_w[0:C, s, :], mom_t[:, 0:1], mom_t[:, 1:2], ALU.subtract,
                                        ALU.mult).then_inc(normed, 1)

            def low_part(u, s, first=False):
                dve.wait_ge(hi_done, u + 1)
                if not first:
                    dve.wait_ge(parts_in[s], (u - s) * (8 * MOVES))
                nc.vector.tensor_tensor(low[:, s, :, 1:W + 1], z[:, s, :].rearrange("p (y x) -> p y x", x=W),
                                        xa[0:C, bass.ds(u * 4 + 1, 4), 1:W + 1], ALU.subtract
                                        ).then_inc(lo_done, 1)

            def qk_low(u, s):
                dve.wait_ge(qk_hi, u + 1)
                nc.vector.tensor_tensor(qk[:, s, :, 2 * C:4 * C],
                                        ps[s][:, 0:4 * C].rearrange("p (r o) -> p r o", r=2),
                                        qk[:, s, :, 0:2 * C], ALU.subtract).then_inc(qk_lo, 1)

            norm(0, 0, True)
            norm(1, 1, True)
            low_part(0, 0, True)
            low_part(1, 1, True)
            with dve.Fori(0, UNITS // 2 - 1) as i:
                for s in range(2):
                    norm(i * 2 + (s + 2), s)
                    low_part(i * 2 + (s + 2), s)
                    qk_low(i * 4 + 2 * s, 0)
                    qk_low(i * 4 + (2 * s + 1), 1)
            for u in range(PAIRS - 4, PAIRS):
                qk_low(u, u % 2)

            dve.wait_ge(gram_out, 1)
            g = lambda j: gram[:, j * C:j * C + C]
            nc.vector.tensor_tensor(sc[:, :], g(0), g(2), ALU.add)
            nc.vector.scalar_tensor_tensor(sq[:, 0, :], g(3), 2.0, g(1), ALU.mult, ALU.add)
            c.then_wait(nc.vector.scalar_tensor_tensor(sq[:, 1, :], g(6), 2.0, g(5), ALU.mult, ALU.add))
            c.then_wait(nc.vector.tensor_tensor(sc[:, :], sc[:, :], g(4), ALU.add))
            c.then_wait(nc.vector.tensor_tensor(sq[:], sq[:], k["ident"][0:C, 0:C].unsqueeze(1)
                                                .to_broadcast([C, 2, C]), ALU.mult))
            c.then_wait(nc.vector.tensor_reduce(small[:, 0:2], sq[:], X, ALU.add))
            dve.sem_inc(att, 1)
            dve.wait_ge(att_act, 1)
            c.then_wait(nc.vector.tensor_scalar(small[:, 2:4], small[:, 2:4], 1e-12 * WSCALE, None, ALU.max))
            c.then_wait(nc.vector.reciprocal(small[:, 4:6], small[:, 2:4]))
            nc.vector.tensor_scalar(sc[:, :], sc[:, :], small[:, 4:5], None, ALU.mult)
            c.then_wait(nc.vector.tensor_tensor(small[:, 6:7], small[:, 5:6], k["temp"][:, :], ALU.mult))
            dve.sem_inc(att, 1)
            dve.wait_ge(att_pe, 1)
            c.then_wait(nc.vector.scalar_tensor_tensor(sc[:, :], ps[0][0:C, 0:C], small[:, 6:7],
                                                       k["same_head"][:, :], ALU.mult, ALU.add))
            c.then_wait(nc.vector.tensor_reduce(small[:, 7:8], sc[:, :], X, ALU.max))
            c.then_wait(nc.vector.tensor_scalar(small[:, 8:9], small[:, 7:8], -1.0, None, ALU.mult))
            dve.sem_inc(att, 1)
            dve.wait_ge(att_act, 2)
            c.then_wait(nc.vector.reciprocal(small[:, 10:11], small[:, 9:10]))
            c.then_wait(nc.vector.tensor_scalar(probs[:, :], probs[:, :], small[:, 10:11], None, ALU.mult))
            dve.sem_inc(att, 1)
            dve.wait_ge(att_act, 4)
            c.then_wait(nc.vector.tensor_tensor(wf[C:CV, 4, :], wf[C:CV, 4, :], k["b_out"][C:CV, :], ALU.add))
            dve.sem_inc(att, 1)
            dve.wait_ge(att_act, 5)
            nc.vector.scalar_tensor_tensor(wf_lo[:], wf[:], WSCALE, wf_hi[:], ALU.mult, ALU.subtract
                                           ).then_inc(wf_split, 1)

            def add_rows(u, s):
                dve.wait_ge(outs, u + 1)
                rows = img[:, bass.ds(u * 4, 4), :]
                nc.vector.scalar_tensor_tensor(rows, ps[s][:, 0:4 * C].rearrange("p (y c) -> p y c", c=C),
                                               1.0 / WSCALE, rows, ALU.mult, ALU.add).then_inc(evac, 1)

            PER = QROWS // 4
            for j in range(PER):
                add_rows(j, j % 2)
            with dve.Fori(1, NQ) as q:
                dve.wait_ge(evac, q * PER)
                for j in range(PER):
                    add_rows(q * PER + j, j % 2)
                    chunk_stats(nc, img, q * QROWS - QROWS, k["stats"], q - 1,
                                range(GN // PER * j, GN // PER * (j + 1)))
            dve.wait_ge(evac, UNITS)
            c.then_wait(chunk_stats(nc, img, H - QROWS, k["stats"], NQ - 1, range(GN)))

        @block.scalar
        def _(act):
            group_stats_root(nc, act, k, ps_s, mom, stat_summed, stat_rooted)
            act.wait_ge(padded, 2)

            def high(u, s):
                act.wait_ge(normed, u + 1)
                nc.scalar.activation(xa[0:C, bass.ds(u * 4 + 1, 4), 1:W + 1],
                                     z[:, s, :].rearrange("p (y x) -> p y x", x=W), ACT.Copy).then_inc(hi_done, 1)

            def qk_high(u, s, first=False):
                act.wait_ge(conv_done, u + 1)
                if not first:
                    act.wait_ge(gram_done, u - 1)
                nc.scalar.activation(qk[:, s, :, 0:2 * C], ps[s][:, 0:4 * C].rearrange("p (r o) -> p r o", r=2),
                                     ACT.Copy).then_inc(qk_hi, 1)

            high(0, 0)
            high(1, 1)
            for s in range(2):
                high(s + 2, s)
                qk_high(2 * s, 0, s == 0)
                qk_high(2 * s + 1, 1, s == 0)
            with act.Fori(1, UNITS // 2 - 1) as i:
                for s in range(2):
                    high(i * 2 + (s + 2), s)
                    qk_high(i * 4 + 2 * s, 0)
                    qk_high(i * 4 + (2 * s + 1), 1)
            for u in range(PAIRS - 4, PAIRS):
                qk_high(u, u % 2)

            act.wait_ge(gram_done, PAIRS + 1)
            nc.scalar.activation(gram[:, 0:4 * C], ps_g[0][0:C, 0:4 * C], ACT.Copy)
            nc.scalar.activation(gram[:, 4 * C:7 * C], ps_g[1][0:C, 0:3 * C], ACT.Copy).then_inc(gram_out, 1)
            act.wait_ge(att, 1)
            nc.scalar.activation(small[:, 2:4], small[:, 0:2], ACT.Sqrt).then_inc(att_act, 1)
            act.wait_ge(att, 3)
            nc.scalar.activation(probs[:, :], sc[:, :], ACT.Exp, bias=small[:, 8:9],
                                 accum_out=small[:, 9:10]).then_inc(att_act, 1)
            act.wait_ge(att_pe, 2)
            nc.scalar.activation(mix[:, :], ps[1][0:C, 0:C], ACT.Copy).then_inc(att_act, 1)
            act.wait_ge(att_pe, 3)
            nc.scalar.activation(wf[:, 0:5, :], ps_w[0:CV, 0, 0:5 * C].rearrange("p (t o) -> p t o", o=C), ACT.Copy)
            nc.scalar.activation(wf[:, 5:9, :], ps_w[0:CV, 1, 0:4 * C].rearrange("p (t o) -> p t o", o=C),
                                 ACT.Copy).then_inc(att_act, 1)
            act.wait_ge(att, 5)
            nc.scalar.activation(wf_hi[:], wf[:], ACT.Copy, scale=WSCALE).then_inc(att_act, 1)

        @block.tensor
        def _(pe):
            group_stats_sums(nc, pe, k, part, ps_s, stat_ready, stat_summed)
            pe.wait_ge(mom_row, 1)
            for j in range(2):
                last = nc.tensor.matmul(ps[0][0:C, j:j + 1], mom_c[0:1, j, :], k["ident"][0:1, 0:1], start=True,
                                        stop=True)
            last.then_inc(mom_col, 1)

            def turn(u, s, first=False):
                pe.wait_ge(rows_ready[s], (u - s) * 8 + 16)
                if not first:
                    pe.wait_ge(normed, u - 1)
                for r in range(4):
                    last = nc.tensor.transpose(ps_w[0:C, s, r * W:r * W + W], rows_in[:, s, r, :], k["ident"][:, :])
                last.then_inc(turned, 1)

            def conv(bank, y, rows, wa, wb, wc, n, sem_):
                for r in range(rows):
                    out = bank[:, r * n:r * n + n]
                    for t, (dy, dx) in enumerate(TAPS):
                        row = y + r + dy
                        nc.tensor.matmul(out, xa[:, row, dx:dx + W], wa[:, t, :], start=(t == 0), stop=False)
                        nc.tensor.matmul(out, xb[:, row, dx:dx + W], wb[:, t, :], start=False, stop=False)
                    for dy in range(3):
                        last = nc.tensor.matmul(out, xc[:, y + r + dy, 0:W], wc[:, dy, :],
                                                start=False, stop=(dy == 2))
                last.then_inc(sem_, 1)

            def conv_qk(u, s, first=False):
                if not first:
                    pe.wait_ge(qk_lo, u - 1)
                conv(ps[s], u * 2, 2, k["wa"], k["wb"], k["wc"], 2 * C, conv_done)

            def grams(u, s):
                pe.wait_ge(qk_lo, u + 1)
                for r in range(2):
                    q = lambda j: qk[:, s, r, j * C:j * C + C]
                    mm = lambda out, a, c_: nc.tensor.matmul(out, a, c_, start=False, stop=False,
                                                             skip_group_check=True)
                    mm(ps_g[0][0:C, 0:4 * C], q(1), qk[:, s, r, :])
                    mm(ps_g[1][0:C, 0:C], q(3), q(0))
                    last = mm(ps_g[1][0:C, C:3 * C], q(0),
                              qk[:, s, r, :].rearrange("p (a o) -> p a o", a=2)[:, :, 0:C])
                last.then_inc(gram_done, 1)

            def rows_spread(u, s):
                pe.wait_ge(parts_in[s], (u - s) * (8 * MOVES) + 16 * MOVES)

            pe.wait_ge(ones_in, 16 * 5)
            turn(0, 0, True)
            turn(1, 1, True)
            for bank in ps_g:
                nc.tensor.matmul(bank[0:C, 0:4 * C], k["zeros"][:, 0:C], k["zeros"][:, 0:4 * C], start=True,
                                 stop=False, skip_group_check=True)
            turn(2, 0)
            rows_spread(0, 0)
            rows_spread(1, 1)
            conv_qk(0, 0, True)
            conv_qk(1, 1, True)
            grams(0, 0)
            turn(3, 1)
            rows_spread(2, 0)
            conv_qk(2, 0)
            grams(1, 1)
            conv_qk(3, 1)
            grams(2, 0)
            for i in range(1, UNITS // 2 - 1):
                for s in range(2):
                    turn(i * 2 + (s + 2), s)
                    rows_spread(i * 2 + (s + 1), 1 - s)
                    conv_qk(i * 4 + 2 * s, 0)
                    grams(i * 4 + (2 * s - 1), 1)
                    conv_qk(i * 4 + (2 * s + 1), 1)
                    grams(i * 4 + 2 * s, 0)
            rows_spread(UNITS - 1, 1)
            for u in range(PAIRS - 4, PAIRS):
                conv_qk(u, u % 2)
                grams(u - 1, (u - 1) % 2)
            grams(PAIRS - 1, 1)
            for bank in ps_g:
                last = nc.tensor.matmul(bank[0:C, 0:4 * C], k["zeros"][:, 0:C], k["zeros"][:, 0:4 * C],
                                        start=False, stop=True, skip_group_check=True)
            last.then_inc(gram_done, 1)

            pe.wait_ge(att, 2)
            nc.tensor.transpose(ps[0][0:C, 0:C], sc[:, :], k["ident"][0:C, 0:C]).then_inc(att_pe, 1)
            pe.wait_ge(att, 4)
            nc.tensor.matmul(ps[1][0:C, 0:C], probs[:, :], k["w_out"][:, :], start=True, stop=True
                             ).then_inc(att_pe, 1)
            pe.wait_ge(att_act, 3)
            for t in range(KK):
                last = nc.tensor.matmul(ps_w[0:CV, t // 5, (t % 5) * C:(t % 5) * C + C], k["wv_t"][:, t, :],
                                        mix[:, :], start=True, stop=True)
            last.then_inc(att_pe, 1)

            def conv_out(u, s, first=False):
                if not first:
                    pe.wait_ge(evac, u - 1)
                conv(ps[s], u * 4, 4, wfa, wfb, wfc, C, outs)

            pe.wait_ge(wf_in, 16 * STACKS)
            conv_out(0, 0, True)
            conv_out(1, 1, True)
            for u in range(2, UNITS):
                conv_out(u, u % 2)


def motif_grams(nc, b, k, img, f_dram, x1_out, pick_dram, att_sems):
    with ExitStack() as ctx:
        sb = lambda n, s, d: ctx.enter_context(nc.sbuf_tensor(f"{n}{b}", s, d))
        psum = lambda n, s: ctx.enter_context(nc.psum_tensor(f"{n}{b}", s, F32))
        sem = lambda n: ctx.enter_context(nc.semaphore(f"{n}{b}"))
        f = sb("f", [P, H, C], F32)
        stage = [sb(f"stage{s}_", [P, 3, MC, C], F32) for s in range(2)]
        patches = [sb(f"patches{s}_", [P, 2, C * 3 * MC], F16) for s in range(2)]
        part = sb("m_part", [P, 4, GN], F32)
        mom = sb("m_mom", [P, 2, GN], F32)
        half = sb("half", [MR, 2, MR], F32)
        g_half = sb("g_half", [MR, MG, MR], F32)
        g_turn = sb("g_turn", [MR, MG, MR], F32)
        g_all = sb("g_all", [MR, MG, MR], F32)
        blk = sb("blk", [MR, MG, MC], F32)
        tmp = sb("tmp", [MR, MG, MC], F32)
        d2 = sb("d2", [MR, MG, MC], F32)
        sqc = sb("sqc", [MR, MG], F32)
        mn = sb("mn", [MR, MG], F32)
        nnt = sb("nnt", [MG, MR], F32)
        eq2 = sb("eq2", [MG, MR], F32)
        sel = sb("sel", [MG, 8, KK], F32)
        offs = sb("offs", [MG, KK], F32)
        ps_a = [psum(f"ps_ga{j}_", [P, 512]) for j in range(2)]
        ps_t = [psum(f"ps_gt{j}_", [P, 512]) for j in range(3)]
        ps_s = psum("ps_gs", [P, 2, GN])
        (ready, summed, rooted, own, sub_done, f_done, hi_done, lo_done, f_out, main_done, half_done,
         a_done, post_pe, post_act, picks, pick_pe, pick_out) = (
            sem(n) for n in ("m_ready", "m_summed", "m_rooted", "m_dve", "m_sub", "m_f", "m_hi", "m_lo", 
                             "f_out", "main_done", "half_done", "a_done", "post_pe", "post_act", "picks", "pick_pe",
                             "pick_out"))
        stage_in = [sem(f"stage_in{s}_") for s in range(2)]
        PER = 6
        Q = 4
        by_shift = lambda t, part_: t[0:HM, part_].rearrange("p (w k c) -> p k c w", k=3, c=MC)
        block = ctx.enter_context(nc.Block())

        @block.sync
        def _(sp):
            if b + 1 < B:
                for s_ in att_sems.values():
                    sp.sem_clear(s_)

            def load(g, s, first=False):
                if not first:
                    sp.wait_ge(lo_done, g - 1)
                for ki in range(3):
                    sp.dma_start(stage[s][0:HM, ki], f[ki:ki + HM, bass.ds(g * MC, MC), :]
                                 ).then_inc(stage_in[s], 16)

            sp.wait_ge(f_done, 1)
            for j in range(4):
                load(j, j % 2, j < 2)
            with sp.Fori(1, Q) as q:
                sp.wait_ge(f_done, q + 1)
                for j in range(4):
                    load(q * 4 + j, j % 2)
            for j in range(2):
                sp.wait_ge(picks, j + 1)
                for half_ in range(2):
                    sp.dma_start(pick_dram[b, j, half_], (offs if j == 0 else sel[:, 7])[:, half_:half_ + MC]
                                 ).then_inc(pick_out, 16)
            sp.wait_ge(pick_out, 16 * 4)
            sp.wait_ge(x1_out, 16 * Q)
            sp.wait_ge(f_out, 16 * Q)

        @block.gpsimd
        def _(pool):
            for q in range(1, Q):
                r = slice(32 * q, 32 * q + 32)
                pool.wait_ge(sub_done, q + 1)
                if q == 1:
                    pool.wait_ge(f_done, 1)
                fg = f[:, r, :].rearrange("p y (g j) -> p y g j", j=GC)
                nc.gpsimd.tensor_tensor(fg, fg, mom[:, 1, :].unsqueeze(1).unsqueeze(3)
                                        .to_broadcast([P, 32, GN, GC]), ALU.mult).then_inc(f_done, 1)

        @block.scalar
        def _(act):
            group_stats_root(nc, act, k, ps_s, mom, summed, rooted)

            def high(i, s, first):
                act.wait_ge(stage_in[s], i * 48 + 48)
                if not first:
                    act.wait_ge(main_done, i * 2 + (s - 1))
                nc.scalar.activation(by_shift(patches[s], 0), stage[s][0:HM], ACT.Copy).then_inc(hi_done, 1)

            def halve(i, s, first):
                act.wait_ge(main_done, i * 2 + (s + 1))
                if not first:
                    act.wait_ge(a_done, i * 2 + (s - 1))
                nc.scalar.activation(half[:, s, :], ps_a[s][0:MR, 0:MR], ACT.Copy, scale=0.5).then_inc(half_done, 1)

            def store(q):
                act.wait_ge(f_done, q + 1)
                r = slice(32 * q, 32 * q + 32)
                act.dma_start(by_planes(f_dram)[:, r, :], f[:, r, :]).then_inc(f_out, 16)

            high(0, 0, True)
            high(0, 1, True)
            store(0)
            for s in range(2):
                halve(0, s, True)
                high(1, s, False)
                store(s + 1)
            store(3)
            with act.Fori(1, MG // 2 - 1) as i:
                for s in range(2):
                    halve(i, s, False)
                    high(i + 1, s, False)
            for s in range(2):
                halve(MG // 2 - 1, s, False)
            for step, dst in enumerate((g_turn, g_all)):
                for j in range(3):
                    n = min(PER, MG - PER * j)
                    act.wait_ge(post_pe, 3 * step + j + 1)
                    nc.scalar.activation(dst[:, PER * j:PER * j + n, :],
                                         ps_t[j][0:MR, 0:n * MR].rearrange("p (g r) -> p g r", r=MR),
                                         ACT.Copy).then_inc(post_act, 1)

        @block.tensor
        def _(pe):
            group_stats_sums(nc, pe, k, part, ps_s, ready, summed)

            def grams(i, s, first):
                pe.wait_ge(lo_done, i * 2 + (s + 1))
                if not first:
                    pe.wait_ge(a_done, i * 2 + (s - 1))
                for w in range(WM):
                    cols = slice(3 * MC * w, 3 * MC * w + MR)
                    last = nc.tensor.matmul(ps_a[s][0:MR, 0:2 * MR], patches[s][0:HM, 0, cols],
                                            patches[s][0:HM, :, cols], start=(w == 0), stop=(w == WM - 1))
                last.then_inc(main_done, 1)

            grams(0, 0, True)
            grams(0, 1, True)
            with pe.Fori(1, MG // 2) as i:
                grams(i, 0, False)
                grams(i, 1, False)
            pe.wait_ge(a_done, MG)
            for g in range(MG):
                last = nc.tensor.matmul(ps_t[g // PER][0:MR, (g % PER) * MR:(g % PER) * MR + MR], g_half[:, g, :],
                                        k["order"][:, :], start=True, stop=True)
                if g % PER == PER - 1 or g == MG - 1:
                    last.then_inc(post_pe, 1)
            for g in range(MG):
                if g % PER == 0:
                    pe.wait_ge(post_act, g // PER + 1)
                out = ps_t[g // PER][0:MR, (g % PER) * MR:(g % PER) * MR + MR]
                nc.tensor.matmul(out, g_turn[:, g, :], k["order"][:, :], start=True, stop=False)
                last = nc.tensor.matmul(out, k["order"][:, :], g_turn[:, g, :], start=False, stop=True)
                if g % PER == PER - 1 or g == MG - 1:
                    last.then_inc(post_pe, 1)
            pe.wait_ge(pick_pe, 1)
            nc.tensor.matmul(ps_a[0][0:MR, 0:MG * MC], k["same_block"][:, :],
                             tmp[:].rearrange("p g d -> p (g d)"), start=True, stop=True).then_inc(post_pe, 1)
            pe.wait_ge(pick_pe, 2)
            nc.tensor.transpose(ps_a[1][0:MG, 0:MR], mn[:, :], k["ident"][0:MR, 0:MR]).then_inc(post_pe, 1)

        @block.vector
        def _(dve):
            c = Count(dve, own)
            group_stats(nc, dve, c, k["stats"], k["dev"], part, ps_s, mom, ready, summed, rooted)
            moment = lambda m: mom[:, m, :].unsqueeze(1).unsqueeze(3).to_broadcast([P, 32, GN, GC])
            for q in range(Q):
                r = slice(32 * q, 32 * q + 32)
                fg = f[:, r, :].rearrange("p y (g j) -> p y g j", j=GC)
                nc.vector.tensor_tensor(fg, img[:, r, :].rearrange("p y (g j) -> p y g j", j=GC), moment(0),
                                        ALU.subtract).then_inc(sub_done, 1)
                if q == 0:
                    dve.wait_ge(sub_done, 1)
                    nc.vector.tensor_tensor(fg, fg, moment(1), ALU.mult).then_inc(f_done, 1)

            def low(i, s):
                dve.wait_ge(hi_done, i * 2 + (s + 1))
                nc.vector.tensor_tensor(by_shift(patches[s], 1), stage[s][0:HM], by_shift(patches[s], 0),
                                        ALU.subtract).then_inc(lo_done, 1)

            def half_gram(i, s):
                dve.wait_ge(half_done, i * 2 + (s + 1))
                nc.vector.tensor_tensor(g_half[:, bass.ds(i * 2 + s, 1), :],
                                        ps_a[s][0:MR, MR:2 * MR].unsqueeze(1), half[:, s, :].unsqueeze(1),
                                        ALU.add).then_inc(a_done, 1)

            low(0, 0)
            low(0, 1)
            with dve.Fori(0, MG // 2 - 1) as i:
                for s in range(2):
                    half_gram(i, s)
                    low(i + 1, s)
            for s in range(2):
                half_gram(MG // 2 - 1, s)

            dve.wait_ge(post_act, 6)
            c.then_wait(nc.vector.tensor_tensor(g_all[:], g_all[:], k["same_block"][:, :].unsqueeze(1)
                                                .to_broadcast([MR, MG, MR]), ALU.mult))
            c.then_wait(nc.vector.tensor_reduce(blk[:], g_all[:].rearrange("p g (j d) -> p g d j", d=MC), X,
                                                ALU.add))
            own8 = k["own"][:, :].unsqueeze(1).to_broadcast([MR, MG, MC])
            iota8 = k["iota"][0:MR, 0:MC].unsqueeze(1).to_broadcast([MR, MG, MC])
            c.then_wait(nc.vector.tensor_tensor(tmp[:], blk[:], own8, ALU.mult))
            c.then_wait(nc.vector.tensor_reduce(sqc[:, :], tmp[:], X, ALU.add))
            dve.sem_inc(pick_pe, 1)
            dve.wait_ge(post_pe, 7)
            c.then_wait(nc.vector.tensor_tensor(d2[:], ps_a[0][0:MR, 0:MG * MC].rearrange("p (g d) -> p g d", d=MC),
                                                sqc[:, :].unsqueeze(2).to_broadcast([MR, MG, MC]), ALU.add))
            c.then_wait(nc.vector.scalar_tensor_tensor(d2[:], blk[:], -2.0, d2[:], ALU.mult, ALU.add))
            c.then_wait(nc.vector.tensor_scalar(tmp[:], own8, BIG, None, ALU.mult))
            c.then_wait(nc.vector.tensor_tensor(d2[:], d2[:], tmp[:], ALU.add))
            c.then_wait(nc.vector.tensor_reduce(mn[:, :], d2[:], X, ALU.min))
            c.then_wait(nc.vector.tensor_tensor(d2[:], d2[:], mn[:, :].unsqueeze(2).to_broadcast([MR, MG, MC]),
                                                ALU.is_equal))
            c.then_wait(nc.vector.tensor_scalar(tmp[:], iota8, -float(MC), None, ALU.add))
            c.then_wait(nc.vector.tensor_tensor(tmp[:], tmp[:], d2[:], ALU.mult))
            c.then_wait(nc.vector.tensor_reduce(mn[:, :], tmp[:], X, ALU.min))
            c.then_wait(nc.vector.tensor_scalar(mn[:, :], mn[:, :], float(MC), None, ALU.add))
            dve.sem_inc(pick_pe, 1)
            dve.wait_ge(post_pe, 8)
            c.then_wait(nc.vector.tensor_copy(nnt[:, :], ps_a[1][0:MG, 0:MR]))
            u, ge, cu, ku, kui, t1, t2, cm = (sel[:, j, :] for j in range(8))
            jj = k["iota"][0:MG, 0:KK]
            c.then_wait(nc.vector.tensor_reduce(u, nnt[:, :].rearrange("p (j d) -> p j d", d=MC), X, ALU.max))
            c.then_wait(nc.vector.tensor_tensor(eq2[:, :].rearrange("p (j d) -> p j d", d=MC),
                                                nnt[:, :].rearrange("p (j d) -> p j d", d=MC),
                                                u.unsqueeze(2).to_broadcast([MG, KK, MC]), ALU.is_equal))
            c.then_wait(nc.vector.tensor_reduce(cm, eq2[:, :].rearrange("p (j d) -> p j d", d=MC), X, ALU.add))
            c.then_wait(nc.vector.tensor_tensor(t1, u, jj, ALU.subtract))
            c.then_wait(nc.vector.tensor_scalar(ge, t1, 0.0, None, ALU.is_ge))
            c.then_wait(nc.vector.tensor_scalar(t1, t1, float(KK), None, ALU.add))
            c.then_wait(nc.vector.scalar_tensor_tensor(ku, ge, -float(KK), t1, ALU.mult, ALU.add))
            c.then_wait(nc.vector.scalar_tensor_tensor(cu, ge, -1.0, jj, ALU.add, ALU.add))
            c.then_wait(nc.vector.tensor_scalar(t1, ku, 3.0, None, ALU.is_ge))
            c.then_wait(nc.vector.tensor_scalar(t2, ku, 6.0, None, ALU.is_ge))
            c.then_wait(nc.vector.tensor_tensor(kui, t1, t2, ALU.add))
            c.then_wait(nc.vector.scalar_tensor_tensor(t1, kui, float(C - 3), ku, ALU.mult, ALU.add))
            c.then_wait(nc.vector.scalar_tensor_tensor(t2, cu, float(PLANE), t1, ALU.mult, ALU.add))
            c.then_wait(nc.vector.tensor_scalar(offs[:, :], t2, k["group_base"][0:MG, :], None,
                                                ALU.add))
            dve.sem_inc(picks, 1)
            c.then_wait(nc.vector.tensor_scalar(cm, cm, 1.0 / MC, None, ALU.mult))
            dve.sem_inc(picks, 1)


def motif_terms(nc, b, k, f_dram, x1_dram, pick_dram, out):
    R = 16
    N = H // R
    SLOTS = 4
    NR = R + 2
    BR = 4
    PRODS, RNDS = 4, 3
    with ExitStack() as ctx:
        sb = lambda n, s, d: ctx.enter_context(nc.sbuf_tensor(f"{n}{b}", s, d))
        sem = lambda n: ctx.enter_context(nc.semaphore(f"{n}{b}"))
        near = sb("near", [P, SLOTS, NR * C], F32)
        near2 = sb("near2", [P, SLOTS, NR * C], F32)
        fc = sb("fc", [P, SLOTS, R * C], F32)
        x1c = sb("x1c", [P, SLOTS, R * C], F32)
        prod = sb("prod", [P, PRODS, R, WM], F32)
        rnd_m = sb("rnd_m", [P, 2, R, WM], F32)
        rnd = sb("rnd", [P, RNDS, R, WM], F32)
        over = sb("over", [P, 2, R, WM], BF16)
        own_sum = sb("own_sum", [P, R * C], F32)
        pick = sb("pick", [P, 4], F32)
        scale = sb("scale", [P, KK], F32)
        index_f = sb("index_f", [P, 2, N], F32)
        index = sb("index", [P, 2, N], I32)
        acc = [ctx.enter_context(nc.psum_tensor(f"acc{s}_{b}", [P, R // BR, 512], F32)) for s in range(2)]
        (pick_in, own, scaled, indexed, edged, prod_v, prod_p, rm_done, rnd_done, over_done, acc_done, out_ready,
         cnt_done, fold) = (
            sem(n) for n in ("pick_in", "t_dve", "scaled", "indexed", "edged", "prod_v", "prod_p", "rm_done",
                             "rnd_done", "over_done", "acc_done", "out_ready", "cnt_done", "fold"))
        stored, near_in, fc_in, x1_in = ([sem(f"{n}{j}_") for j in range(SLOTS)]
                                         for n in ("stored", "near_in", "fc_in", "x1_in"))
        moved = [sem(f"moved{s}_") for s in range(2)]
        steps = [(2 * m + s, sh) for m in range(N // 2) for sh in range(KK) for s in range(2)]
        number = {st: n for n, st in enumerate(steps)}
        on_pool = [sh in (1, 4, 7) for i, sh in steps]
        after = {i: number[(i, KK - 1)] + 1 for i in range(N)}
        first_row = lambda i: max(R * i - 2, 0)
        last_row = lambda i: min(R * i + R - 1, HM - 1)

        def product_made(eng, n):
            eng.wait_ge(prod_p if on_pool[n] else prod_v, sum(p == on_pool[n] for p in on_pool[:n + 1]))

        def product_inputs(eng, n):
            i, sh = steps[n]
            s = i % SLOTS
            if sh == 0:
                eng.wait_ge(near_in[s], 32 * (i // SLOTS + 1))
                eng.wait_ge(fc_in[s], 16 * (i // SLOTS + 1))
                eng.wait_ge(edged, 2 if i == N - 1 else 1)
            else:
                eng.wait_ge(moved[i % 2], 16 * (8 * (i // 2) + sh))
            if n >= PRODS:
                eng.wait_ge(over_done, n - PRODS + 1)

        def product(vec, n):
            i, sh = steps[n]
            s, (dy, dx) = i % SLOTS, TAPS[sh]
            fv = fc[:, s, :].rearrange("p (r c) -> p r c", c=C)[:, :, dx:dx + WM]
            nv = near[:, s, :].rearrange("p (r c) -> p r c", c=C)[:, 2 - dy:2 - dy + R, 0:WM]
            return vec.tensor_tensor(prod[:, n % PRODS], fv, nv, ALU.mult)

        def run(i):
            a = (first_row(i) - (R * i - 2)) * C
            return slice(a, a + (last_row(i) - first_row(i)) * C + WM)

        out_p = out[b].rearrange("y x c -> y (x c)")
        block = ctx.enter_context(nc.Block())

        @block.sync
        def _(sp):
            def load_rows(dst, src, i, sem_):
                sp.dma_start(dst[:, i % SLOTS, :], src[:, R * i * C:(R * i + R) * C]).then_inc(sem_[i % SLOTS], 16)

            for j in range(2):
                for half_ in range(2):
                    sp.dma_start(pick[:, 2 * j + half_:2 * j + half_ + 1],
                                 pick_dram[b, j, half_].rearrange("g (c o) -> (g c) o", o=1)
                                 ).then_inc(pick_in, 16)

            def store(i):
                sp.wait_ge(out_ready, i + 1)
                sp.dma_start(out_p[:, R * i * C:(R * i + R) * C], x1c[:, i % SLOTS, :]
                             ).then_inc(stored[i % SLOTS], 16)

            for i in range(2):
                load_rows(fc, f_dram, i, fc_in)
            for i in range(2):
                load_rows(x1c, x1_dram, i, x1_in)
            for n, (i, sh) in enumerate(steps):
                if sh >= 1:
                    if sh == 1:
                        sp.wait_ge(near_in[i % SLOTS], 32 * (i // SLOTS + 1))
                    product_made(sp, n - 2)
                    sp.dma_start(near[MC - sh:P:MC, i % SLOTS, run(i)], near2[MC - sh:P:MC, i % SLOTS, run(i)]
                                 ).then_inc(moved[i % 2], 16)
                if sh == 1 and i + 2 < N:
                    if i >= 2:
                        product_made(sp, number[(i - 2, KK - 1)])
                        product_made(sp, number[(i - 2, KK - 2)])
                        if b == 1:
                            sp.wait_ge(cnt_done, i - 1)
                    load_rows(fc, f_dram, i + 2, fc_in)
                if i >= 2 and sh == 2:
                    store(i - 2)
                if sh == 5 and i + 2 < N:
                    if i >= 2:
                        sp.wait_ge(stored[(i + 2) % SLOTS], 16 * ((i + 2) // SLOTS))
                    load_rows(x1c, x1_dram, i + 2, x1_in)
            for i in range(N - 2, N):
                store(i)
            for j in range(SLOTS):
                sp.wait_ge(stored[j], 16 * (N // SLOTS))

        @block.gpsimd
        def _(pool):
            def gather(i):
                s = i % SLOTS
                for t, src in ((near, 0), (near2, 1)):
                    pool.indirect_dma_start(
                        t[:, s, run(i)], None, f_dram.rearrange("y (e o) -> (y e) o", o=1),
                        bass.IndirectOffsetOnAxis(ap=index[:, src, i:i + 1], axis=0)).then_inc(near_in[s], 16)

            def own_patches(i):
                s = i % SLOTS
                v = own_sum[:].rearrange("p (r c) -> p r c", c=C)
                pool.wait_ge(cnt_done, i + 1)
                nc.gpsimd.tensor_tensor(v, v, k["edge_count"][:, :].unsqueeze(1).to_broadcast([P, R, C]),
                                        ALU.mult).then_inc(fold, 1)
                pool.wait_ge(fold, 2 * i + 1)
                pool.wait_ge(x1_in[s], 16 * (i // SLOTS + 1))
                nc.gpsimd.tensor_tensor(x1c[:, s, :], x1c[:, s, :], own_sum[:], ALU.add).then_inc(fold, 1)

            nc.gpsimd.memset(near[:, 0, 0:2 * C], 0.0).then_inc(edged, 1)
            pool.wait_ge(indexed, 1)
            gather(0)
            gather(1)
            for n, (i, sh) in enumerate(steps):
                if sh == 0 and 2 <= i + 2 < N:
                    if i >= 2:
                        product_made(pool, number[(i - 2, KK - 1)])
                        product_made(pool, number[(i - 2, KK - 2)])
                    if i + 2 == N - 1:
                        nc.gpsimd.memset(near[:, (i + 2) % SLOTS, R * C:NR * C], 0.0).then_inc(edged, 1)
                    gather(i + 2)
                if sh == 3 and b == 1:
                    own_patches(i)
                if on_pool[n]:
                    product_inputs(pool, n)
                    product(nc.gpsimd, n).then_inc(prod_p, 1)

        @block.vector
        def _(dve):
            c = Count(dve, own)
            dve.wait_ge(pick_in, 64)
            for i in range(N):
                last = nc.vector.tensor_scalar(index_f[:, :, i], pick[:, 0:2], float(first_row(i) * C), None,
                                               ALU.add)
            c.then_wait(last)
            nc.vector.tensor_copy(index[:], index_f[:]).then_inc(indexed, 1)
            nc.vector.tensor_scalar(scale[:, :], k["second_block"][:, :], pick[:, 3:4], None, ALU.mult)
            c.then_wait(nc.vector.tensor_scalar(k["first_part"][:, :], k["second_block"][:, :], -1.0, 1.0, ALU.mult,
                                                ALU.add))
            nc.vector.scalar_tensor_tensor(scale[:, :], k["first_part"][:, :], pick[:, 2:3], scale[:, :],
                                           ALU.mult, ALU.add).then_inc(scaled, 1)
            dve.wait_ge(scaled, 1)

            def overshoot(n):
                sh = steps[n][1]
                dve.wait_ge(rnd_done, n + 1)
                if n >= 2:
                    dve.wait_ge(acc_done, n - 1)
                nc.vector.scalar_tensor_tensor(over[:, n % 2], prod[:, n % PRODS], scale[:, sh:sh + 1],
                                               rnd[:, n % RNDS], ALU.mult, ALU.is_lt).then_inc(over_done, 1)

            def finish(i):
                dve.wait_ge(acc_done, after[i])
                dve.wait_ge(x1_in[i % SLOTS], 16 * (i // SLOTS + 1))
                if b == 1:
                    dve.wait_ge(fold, 2 * i + 2)
                v = x1c[:, i % SLOTS, :].rearrange("p (m c) -> p m c", c=BR * C)
                nc.vector.tensor_tensor(v, v, acc[i % 2][:, :, 0:BR * C], ALU.add).then_inc(out_ready, 1)

            LAG = 2
            for n in range(len(steps) + LAG):
                if n < len(steps) and not on_pool[n]:
                    product_inputs(dve, n)
                    product(nc.vector, n).then_inc(prod_v, 1)
                if n >= LAG:
                    overshoot(n - LAG)
                    i, sh = steps[n - LAG]
                    if i >= 2 and i % 2 == 0 and sh == 0:
                        finish(i - 2)
                    if i >= 2 and i % 2 == 1 and sh == 0:
                        finish(i - 2)
            finish(N - 2)
            finish(N - 1)

        @block.scalar
        def _(act):
            def count_rows(i):
                s = i % SLOTS
                act.wait_ge(fc_in[s], 16 * (i // SLOTS + 1))
                if i >= 1:
                    act.wait_ge(fold, 2 * i)
                parts = [(0, R, 3.0)]
                if i == 0:
                    parts = [(0, 1, 1.0), (1, 2, 2.0), (2, R, 3.0)]
                if i == N - 1:
                    parts = [(0, R - 2, 3.0), (R - 2, R - 1, 2.0), (R - 1, R, 1.0)]
                for a, e, v in parts:
                    last = nc.scalar.activation(own_sum[:, a * C:e * C], fc[:, s, a * C:e * C], ACT.Copy, scale=v)
                last.then_inc(cnt_done, 1)

            act.wait_ge(scaled, 1)
            for n, (i, sh) in enumerate(steps):
                product_made(act, n)
                if n >= 2:
                    act.wait_ge(rnd_done, n - 1)
                nc.scalar.activation(rnd_m[:, n % 2], prod[:, n % PRODS], ACT.Identity,
                                     bias=k["plus_round"][:, 0:1], scale=scale[:, sh:sh + 1]).then_inc(rm_done, 1)
                act.wait_ge(rm_done, n + 1)
                if n >= RNDS:
                    act.wait_ge(acc_done, n - RNDS + 1)
                nc.scalar.activation(rnd[:, n % RNDS], rnd_m[:, n % 2], ACT.Identity,
                                     bias=k["minus_round"][:, 0:1]).then_inc(rnd_done, 1)
                if b == 1 and sh == 2:
                    count_rows(i)

        @block.tensor
        def _(pe):
            for n, (i, sh) in enumerate(steps):
                dx = TAPS[sh][1]
                bank = acc[i % 2]
                if sh == 0:
                    if i >= 2:
                        pe.wait_ge(out_ready, i - 1)
                    for m in range(R // BR):
                        nc.tensor.matmul(bank[:, m, 0:BR * C], k["zeros"][:, 0:P], k["zeros"][:, 0:BR * C],
                                         start=True, stop=False, skip_group_check=True)
                o = lambda m: bank[:, m, 0:BR * C].rearrange("p (r c) -> p r c", c=C)[:, :, dx:dx + WM]
                pe.wait_ge(rnd_done, n + 1)
                for m in range(R // BR):
                    nc.tensor.matmul(o(m), k["ident"][:, :], rnd[:, n % RNDS, BR * m:BR * m + BR, :], start=False,
                                     stop=False, skip_group_check=True)
                pe.wait_ge(over_done, n + 1)
                for m in range(R // BR):
                    last = nc.tensor.matmul(o(m), k["minus_ident"][:, :], over[:, n % 2, BR * m:BR * m + BR, :],
                                            start=False, stop=(sh == KK - 1), skip_group_check=True)
                last.then_inc(acc_done, 1)


def build(nc, x, w_qkv, b_qkv, w_dw, b_dw, temperature, w_out, b_out, out):
    f_dram = [nc.dram_tensor(f"f_planes{b}", (H, PLANE), F32).ap() for b in range(B)]
    x1_dram = [nc.dram_tensor(f"x1_planes{b}", (H, PLANE), F32).ap() for b in range(B)]
    pick_dram = nc.dram_tensor("picks_dram", (B, 2, 2, MG, MC), F32).ap()
    ins = dict(w_qkv=w_qkv, b_qkv=b_qkv, w_dw=w_dw, b_dw=b_dw, temperature=temperature, w_out=w_out, b_out=b_out)
    with ExitStack() as ctx:
        sb = lambda n, s, d: ctx.enter_context(nc.sbuf_tensor(n, s, d))
        k = dict(
            ident=sb("ident", [P, P], F32), minus_ident=sb("minus_ident", [P, P], BF16),
            zeros=sb("zeros_k", [P, 4 * C], BF16), mean_ones=sb("mean_ones", [P, P], F32),
            eps=sb("eps", [P, 1], F32), plus_round=sb("plus_round", [P, 1], F32),
            minus_round=sb("minus_round", [P, 1], F32), edge_count=sb("edge_count", [P, C], F32),
            same_head=sb("same_head", [C, C], F32), same_block=sb("same_block", [MR, MR], F32),
            order=sb("order", [MR, MR], F32), own=sb("own8", [MR, MC], F32), iota=sb("iota", [P, 32], F32),
            group_base=sb("group_base", [P, 1], F32), plane_f=sb("plane_f", [P, 1], F32),
            second_block=sb("second_block", [P, KK], F32), first_part=sb("first_part", [P, KK], F32),
            temp=sb("temp", [C, 1], F32), w_out=sb("w_out_s", [C, C], F32), b_out=sb("b_out_s", [CV, C], F32),
            wa=sb("wa", [P, KK, 2 * C], F16), wb=sb("wb", [P, KK, 2 * C], F16), wc=sb("wc", [XCR, 3, 2 * C], F16),
            stats=sb("stats", [P, GN, NQ, 6], F32), dev=sb("dev", [P, GN, 2 * NQ], F32),
            wv_t=sb("wv_t", [C, KK, CV], F32),
        )
        x1_out = [ctx.enter_context(nc.semaphore(f"x1_out{b}")) for b in range(B)]
        att_sems = {n: ctx.enter_context(nc.semaphore(n)) for n in ATT_SEMS}
        prepare(nc, k, ins)
        for b in range(B):
            with nc.sbuf_tensor(f"img{b}", [P, H, C], F32) as img:
                attention(nc, b, k, x, img, x1_dram[b], x1_out[b], att_sems)
                motif_grams(nc, b, k, img, f_dram[b], x1_out[b], pick_dram, att_sems)
            motif_terms(nc, b, k, f_dram[b], x1_dram[b], pick_dram, out)


_INS = ["x", "L0_conv_w_qkv", "L0_conv_b_qkv", "L0_conv_w_dw", "L0_conv_b_dw", "L0_conv_temperature",
        "L0_conv_w_out", "L0_conv_b_out"]


def kernel(**inputs):
    import numpy as np
    import concourse.bacc as bacc
    from concourse import mybir as my
    from concourse.bass_utils import run_bass_kernel_spmd

    nc = bacc.Bacc("TRN2", target_bir_lowering=False, num_devices=1)
    arrays, args = {}, []
    for name in _INS:
        a = np.ascontiguousarray(inputs[name])
        arrays[f"in_{name}"] = a
        args.append(nc.dram_tensor(f"in_{name}", a.shape, my.dt.from_np(a.dtype), kind="ExternalInput").ap())
    out = nc.dram_tensor("out_0", (B, H, W, C), F32, kind="ExternalOutput").ap()
    build(nc, *args, out)
    r = run_bass_kernel_spmd(nc, [arrays], core_ids=[0])
    return r.results[0]["out_0"]
```

```python
from contextlib import ExitStack

import concourse.bass as bass
from concourse import mybir

ALU = mybir.AluOpType
ACT = mybir.ActivationFunctionType
X = mybir.AxisListType.X
F32 = mybir.dt.float32
F16 = mybir.dt.float16
BF16 = mybir.dt.bfloat16
I32 = mybir.dt.int32
U32 = mybir.dt.uint32

P = 128
B, H, W, C = 2, 128, 128, 96
HEADS = 4
HC = C // HEADS
CV = C + 1
GN = 32
GC = C // GN
TAPS = [(dy, dx) for dy in range(3) for dx in range(3)]
WSCALE = 1024.0
PLANE = W * C
MG = 16
MC = 8
KK = 9
MR = MC * KK
HM, WM = W - 2, C - 2
ROUND = 1.5 * 2.0 ** 23
BIG = 1.0e30
TWO_ONES = 0x3C003C00
PADW = W + 2
XCR = C + 6
QROWS = 32
NQ = H // QROWS


def by_planes(d):
    return d.rearrange("y (x c) -> x y c", c=C)


class Count:

    def __init__(self, eng, sem):
        self.eng, self.sem, self.n = eng, sem, 0

    def done(self, ins):
        self.n += 1
        ins.then_inc(self.sem, 1)
        return self.n

    def then_wait(self, ins):
        self.eng.wait_ge(self.sem, self.done(ins))


def chunk_stats(nc, img, row, stats, q, groups):
    for g in groups:
        last = nc.vector.bn_stats(stats[:, g, bass.ds(q, 1), :].rearrange("p a s -> p (a s)"),
                                  img[:, bass.ds(row, QROWS), GC * g:GC * g + GC])
    return last


def group_stats_local(nc, c, stats, part, dev):
    parts = stats[:].rearrange("p g q (e s) -> p g (q e) s", s=3)
    m, v = parts[:, :, :, 1], parts[:, :, :, 2]
    c.then_wait(nc.vector.tensor_reduce(part[:, 0, :], m, X, ALU.add))
    nc.vector.tensor_reduce(part[:, 1, :], v, X, ALU.add)
    c.then_wait(nc.vector.tensor_scalar(part[:, 0, :], part[:, 0, :], 0.5 / NQ, None, ALU.mult))
    c.then_wait(nc.vector.tensor_tensor(dev[:], m, part[:, 0, :].unsqueeze(2).to_broadcast([P, GN, 2 * NQ]),
                                        ALU.subtract))
    c.then_wait(nc.vector.tensor_tensor(dev[:], dev[:], dev[:], ALU.mult))
    c.then_wait(nc.vector.tensor_reduce(part[:, 2, :], dev[:], X, ALU.add))
    c.then_wait(nc.vector.scalar_tensor_tensor(part[:, 1, :], part[:, 2, :], float(QROWS * GC // 2),
                                               part[:, 1, :], ALU.mult, ALU.add))
    c.then_wait(nc.vector.tensor_scalar(part[:, 1, :], part[:, 1, :], 1.0 / (H * GC), None, ALU.mult))


def group_stats(nc, dve, c, stats, dev, part, ps, mom, ready, summed, rooted):
    group_stats_local(nc, c, stats, part, dev)
    c.then_wait(nc.vector.tensor_copy(part[:, 3, :], part[:, 0, :]))
    dve.sem_inc(ready, 1)
    dve.wait_ge(summed, 1)
    c.then_wait(nc.vector.tensor_copy(mom[:, 0, :], ps[:, 0, :]))
    c.then_wait(nc.vector.tensor_tensor(part[:, 0, :], part[:, 0, :], mom[:, 0, :], ALU.subtract))
    c.then_wait(nc.vector.tensor_tensor(part[:, 0, :], part[:, 0, :], part[:, 0, :], ALU.mult))
    c.then_wait(nc.vector.tensor_tensor(part[:, 1, :], part[:, 1, :], part[:, 0, :], ALU.add))
    dve.sem_inc(ready, 1)
    dve.wait_ge(rooted, 1)
    c.then_wait(nc.vector.reciprocal(mom[:, 1, :], mom[:, 1, :]))


def group_stats_sums(nc, pe, k, part, ps, ready, summed):
    for step, line in ((0, 3), (1, 1)):
        pe.wait_ge(ready, step + 1)
        nc.tensor.matmul(ps[:, step, :], k["mean_ones"][:, :], part[:, line, :], start=True,
                         stop=True).then_inc(summed, 1)


def group_stats_root(nc, act, k, ps, mom, summed, rooted):
    act.wait_ge(summed, 2)
    nc.scalar.activation(mom[:, 1, :], ps[:, 1, :], ACT.Sqrt, bias=k["eps"][:, 0:1]).then_inc(rooted, 1)


STACKS = 13


def stack_weights(eng, hi, lo, wa, wb, wc, sem):
    def move(dst, src):
        eng.dma_start(dst, src).then_inc(sem, 16)

    by_dx = lambda t, lines, dx: t[lines].rearrange("p (a b) o -> p a b o", b=3)[:, :, dx, :]
    move(wa[0:C], hi[0:C])
    move(wa[C:P], hi[0:32])
    move(wb[0:C], lo[0:C])
    move(wb[C:P], hi[32:64])
    for dx in range(3):
        move(wc[32 * dx:32 * dx + 32], by_dx(hi, slice(64, C), dx))
        move(wc[C + dx:C + dx + 1], by_dx(hi, slice(C, CV), dx))
        move(wc[C + 3 + dx:C + 4 + dx], by_dx(lo, slice(C, CV), dx))


def load_image(eng, x_image, img, loaded, chunks=range(NQ)):
    for q in chunks:
        rows = slice(QROWS * q, QROWS * q + QROWS)
        eng.dma_start(img[:, rows, :], x_image.rearrange("y x c -> x y c")[:, rows, :]).then_inc(loaded[q], 16)


def prepare(nc, k, ins, x, img, img_in):
    with ExitStack() as ctx:
        sb = lambda n, s, d: ctx.enter_context(nc.sbuf_tensor(n, s, d))
        sem = lambda n: ctx.enter_context(nc.semaphore(n))
        w_aug = sb("w_aug", [CV, 3 * C], F32)
        dw_all = sb("dw_all", [CV, KK, 3 * C], F32)
        b_dw = sb("b_dw_row", [CV, 3 * C], F32)
        w_full = sb("w_full", [CV, KK, 3 * C], F32)
        wqk_hi = sb("wqk_hi", [CV, KK, 2 * C], F16)
        wqk_lo = sb("wqk_lo", [CV, KK, 2 * C], F16)
        plane_i = sb("plane_i", [P, 1], I32)
        iota_i = sb("iota_i", [P, 32], I32)
        ps_wv = ctx.enter_context(nc.psum_tensor("ps_wv", [C, 2, 512], F32))
        weights_in = sem("weights_in")
        zeroed, pooled, made, rounded, turned, dve_own, split, stacked = (
            sem(n) for n in ("pre_zeroed", "pre_pooled", "pre_made", "pre_rounded", "pre_turned", "pre_dve",
                             "pre_split", "pre_stacked"))
        block = ctx.enter_context(nc.Block())

        @block.sync
        def _(sp):
            sp.dma_start(w_aug[0:C, :], ins["w_qkv"].rearrange("a b c o -> (a b c) o")).then_inc(weights_in, 16)
            sp.dma_start(w_aug[C:CV, :], ins["b_qkv"].rearrange("(a o) -> a o", a=1)).then_inc(weights_in, 16)
            sp.dma_start(dw_all[:].rearrange("p t o -> p (t o)"),
                         ins["w_dw"].rearrange("a b c o -> c (a b o)").to_broadcast([CV, KK * 3 * C])
                         ).then_inc(weights_in, 16)
            sp.dma_start(b_dw[C:CV, :], ins["b_dw"].rearrange("(a o) -> a o", a=1)).then_inc(weights_in, 16)
            sp.dma_start(k["w_out"][:, :], ins["w_out"].rearrange("a b c o -> (a b c) o")).then_inc(weights_in, 16)
            sp.dma_start(k["b_out"][C:CV, :], ins["b_out"].rearrange("(a o) -> a o", a=1)).then_inc(weights_in, 16)
            for h in range(HEADS):
                sp.dma_start(k["temp"][HC * h:HC * h + HC, :],
                             ins["temperature"].rearrange("a h b c -> (a b c) h")[:, h:h + 1]
                             .to_broadcast([HC, 1])).then_inc(weights_in, 16)
            load_image(sp, x[0], img, img_in, range(NQ // 2))
            sp.wait_ge(split, 1)
            stack_weights(sp, wqk_hi, wqk_lo, k["wa"], k["wb"], k["wc"], stacked)
            load_image(sp, x[0], img, img_in, range(NQ // 2, NQ))
            sp.wait_ge(stacked, 16 * STACKS)

        @block.gpsimd
        def _(pool):
            nc.gpsimd.memset(k["ident"][:, :], 0.0)
            nc.gpsimd.memset(k["same_head"][:, :], 0.0)
            nc.gpsimd.memset(k["order"][:, :], 0.0)
            nc.gpsimd.memset(k["same_block"][:, :], 1.0)
            nc.gpsimd.memset(k["mean_ones"][:, :], 1.0 / P)
            nc.gpsimd.memset(k["zeros"][:, :], 0.0)
            nc.gpsimd.memset(k["eps"][:, :], 1e-5)
            nc.gpsimd.memset(k["plus_round"][:, :], ROUND)
            nc.gpsimd.memset(k["minus_round"][:, :], -ROUND)
            nc.gpsimd.iota(plane_i[:, :], [[0, 1]], base=0, channel_multiplier=1)
            nc.gpsimd.iota(iota_i[:, :], [[1, 32]], base=0, channel_multiplier=0).then_inc(zeroed, 1)
            pool.wait_ge(zeroed, 1)
            nc.gpsimd.affine_select(k["ident"][:, :], k["ident"][:, :], [[-1, P]], ALU.not_equal, 1.0,
                                    base=0, channel_multiplier=1)
            nc.gpsimd.affine_select(k["order"][:, :], k["order"][:, :], [[-1, MC], [-MC, 3], [-3 * MC, 3]],
                                    ALU.not_equal, 1.0, base=0, channel_multiplier=1)
            nc.gpsimd.affine_select(k["same_head"][:, :], k["same_head"][:, :], [[-HC, HEADS], [0, HC]],
                                    ALU.is_ge, -BIG, base=0, channel_multiplier=1)
            nc.gpsimd.affine_select(k["same_block"][:, :], k["same_block"][:, :], [[-MC, KK], [0, MC]],
                                    ALU.is_ge, 0.0, base=0, channel_multiplier=1).then_inc(zeroed, 1)
            pool.wait_ge(zeroed, 2)
            nc.gpsimd.affine_select(k["same_head"][:, :], k["same_head"][:, :], [[HC, HEADS], [0, HC]],
                                    ALU.is_ge, -BIG, base=HC - 1, channel_multiplier=-1)
            nc.gpsimd.affine_select(k["same_block"][:, :], k["same_block"][:, :], [[MC, KK], [0, MC]],
                                    ALU.is_ge, 0.0, base=MC - 1, channel_multiplier=-1).then_inc(pooled, 1)

        @block.vector
        def _(dve):
            c = Count(dve, dve_own)
            dve.wait_ge(pooled, 1)
            nc.vector.tensor_scalar(k["minus_ident"][:, :], k["ident"][:, :], -1.0, None, ALU.mult)
            nc.vector.tensor_copy(k["iota"][:, :], iota_i[:, :])
            nc.vector.tensor_scalar(k["group_base"][:, :], plane_i[:, :], float(MC * PLANE), None, ALU.mult)
            nc.vector.tensor_reduce(k["own"][:, :], k["ident"][0:MR, 0:MR].rearrange("p (j d) -> p d j", d=MC), X,
                                    ALU.add)
            c.then_wait(nc.vector.tensor_scalar(plane_i[:, :], plane_i[:, :], MC - 1, None, ALU.bitwise_and))
            plane_f = k["plane_f"]
            c.then_wait(nc.vector.tensor_copy(plane_f[:, :], plane_i[:, :]))
            for s in range(KK):
                nc.vector.tensor_scalar(k["second_block"][:, s:s + 1], plane_f[:, :], float(MC - s), None, ALU.is_ge)
            dve.wait_ge(weights_in, 16 * 10)
            c.then_wait(nc.vector.tensor_tensor(w_full[:], dw_all[:],
                                                w_aug[:].unsqueeze(1).to_broadcast([CV, KK, 3 * C]), ALU.mult))
            c.then_wait(nc.vector.tensor_tensor(w_full[C:CV, 4, :], w_full[C:CV, 4, :], b_dw[C:CV, :], ALU.add))
            dve.sem_inc(made, 1)
            dve.wait_ge(rounded, 1)
            nc.vector.scalar_tensor_tensor(wqk_lo[:], w_full[:, :, 0:2 * C], WSCALE, wqk_hi[:], ALU.mult,
                                           ALU.subtract).then_inc(split, 1)
            dve.wait_ge(turned, 1)
            nc.vector.tensor_copy(k["wv_t"][:, 0:5, :], ps_wv[:, 0, 0:5 * CV].rearrange("p (t c) -> p t c", c=CV))
            c.then_wait(nc.vector.tensor_copy(k["wv_t"][:, 5:9, :],
                                              ps_wv[:, 1, 0:4 * CV].rearrange("p (t c) -> p t c", c=CV)))

        @block.scalar
        def _(act):
            act.wait_ge(made, 1)
            nc.scalar.activation(wqk_hi[:], w_full[:, :, 0:2 * C], ACT.Copy, scale=WSCALE).then_inc(rounded, 1)

        @block.tensor
        def _(pe):
            pe.wait_ge(pooled, 1)
            pe.wait_ge(made, 1)
            for t in range(KK):
                last = nc.tensor.transpose(ps_wv[:, t // 5, (t % 5) * CV:(t % 5) * CV + CV],
                                           w_full[:, t, 2 * C:3 * C], k["ident"][0:CV, 0:CV])
            last.then_inc(turned, 1)


ATT_SEMS = ("stat_ready", "stat_summed", "stat_rooted", "a_dve", "padded", "ones_made", "ones_in", "turned",
            "normed", "hi_done", "lo_done", "mom_row", "mom_col", "conv_done", "qk_hi", "qk_lo", "gram_done",
            "gram_out", "att", "att_pe", "att_act", "wf_split", "wf_in", "outs", "evac") \
    + tuple(f"img_in{q}" for q in range(NQ)) + ("rows_ready0", "rows_ready1", "parts_in0", "parts_in1")


def attention(nc, b, k, x, img, x1_dram, x1_out, sems):
    UNITS = H // 4
    PAIRS = H // 2
    MOVES = 6
    with ExitStack() as ctx:
        sb = lambda n, s, d: ctx.enter_context(nc.sbuf_tensor(f"{n}{b}", s, d))
        psum = lambda n, s: ctx.enter_context(nc.psum_tensor(f"{n}{b}", s, F32))
        xa = sb("xa", [P, H + 2, PADW], F16)
        xb = sb("xb", [P, H + 2, PADW], F16)
        xc = sb("xc", [XCR, H + 2, PADW], F16)
        z = sb("z", [C, 2, 4 * W], F32)
        low = sb("low", [C, 2, 4, PADW], F16)
        part = sb("part", [P, 4, GN], F32)
        mom = sb("mom", [P, 2, GN], F32)
        mom_c = sb("mom_c", [1, 2, C], F32)
        mom_t = sb("mom_t", [C, 2], F32)
        qk = sb("qk", [P, 2, 2, 4 * C], F16)
        gram = sb("gram", [C, 7 * C], F32)
        sc = sb("sc", [C, C], F32)
        sq = sb("sq", [C, 2, C], F32)
        small = sb("small", [C, 12], F32)
        probs = sb("probs", [C, C], F32)
        mix = sb("mix", [C, C], F32)
        wf = sb("wf", [CV, KK, C], F32)
        wf_hi = sb("wf_hi", [CV, KK, C], F16)
        wf_lo = sb("wf_lo", [CV, KK, C], F16)
        wfa, wfb = sb("wfa", [P, KK, C], F16), sb("wfb", [P, KK, C], F16)
        wfc = sb("wfc", [XCR, 3, C], F16)
        ps = [psum(f"ps_a{j}_", [P, 512]) for j in range(2)]
        ps_g = [psum(f"ps_g{j}_", [P, 512]) for j in range(2)]
        ps_s = psum("ps_s", [P, 2, GN])
        ps_w = psum("ps_w", [P, 2, 512])
        (stat_ready, stat_summed, stat_rooted, dve_own, padded, ones_made, ones_in, turned, normed, hi_done, lo_done,
         mom_row, mom_col, conv_done, qk_hi, qk_lo, gram_done, gram_out, att, att_pe, att_act, wf_split, wf_in,
         outs, evac) = (
            sems[n] for n in ATT_SEMS[:25])
        img_in = [sems[f"img_in{q}"] for q in range(NQ)]
        rows_ready = [sems[f"rows_ready{j}"] for j in range(2)]
        parts_in = [sems[f"parts_in{j}"] for j in range(2)]
        xcol = x[b].rearrange("y x c -> x y c")
        flat = lambda t: t.rearrange("p y x -> p (y x)")
        block = ctx.enter_context(nc.Block())

        @block.sync
        def _(sp):
            def load_rows(u, s, first=False):
                if b > 0:
                    if not first:
                        sp.wait_ge(turned, u - 1)
                    sp.dma_start(img[:, bass.ds(u * 4, 4), :], xcol[:, bass.ds(u * 4, 4), :]
                                 ).then_inc(rows_ready[s], 16)

            def spread(u, s):
                sp.wait_ge(lo_done, u + 1)
                rows = bass.ds(u * (4 * PADW) + PADW, 4 * PADW)
                lo = lambda c, d: low[32 * c:32 * c + 32, s].rearrange("p y x -> p (y x)")[:, d:4 * PADW]
                sp.dma_start(flat(xb[0:C])[:, rows], flat(xa[0:C])[:, rows]).then_inc(parts_in[s], 16)
                sp.dma_start(flat(xa[C:P])[:, rows], lo(0, 0)).then_inc(parts_in[s], 16)
                sp.dma_start(flat(xb[C:P])[:, rows], lo(1, 0)).then_inc(parts_in[s], 16)
                for dx in range(3):
                    sp.dma_start(flat(xc[32 * dx:32 * dx + 32])[:, bass.ds(u * (4 * PADW) + PADW, 4 * PADW - dx)],
                                 lo(2, dx)).then_inc(parts_in[s], 16)

            load_rows(0, 0, True)
            load_rows(1, 1, True)
            sp.wait_ge(ones_made, 3)
            for j in range(1, 6):
                sp.dma_start(flat(xc[C + j:C + j + 1])[:, 0:(H + 2) * PADW - 2],
                             flat(xc[C:C + 1])[:, j % 3:(H + 2) * PADW - 2 + j % 3]).then_inc(ones_in, 16)
            sp.wait_ge(padded, 1)
            with sp.Fori(0, UNITS // 2 - 1) as i:
                for s in range(2):
                    load_rows(i * 2 + (s + 2), s)
                    spread(i * 2 + s, s)
            for s in range(2):
                spread(UNITS - 2 + s, s)
            sp.wait_ge(wf_split, 1)
            stack_weights(sp, wf_hi, wf_lo, wfa, wfb, wfc, wf_in)
            for q in range(NQ):
                sp.wait_ge(evac, (q + 1) * (QROWS // 4))
                rows = slice(QROWS * q, QROWS * q + QROWS)
                sp.dma_start(by_planes(x1_dram)[:, rows, :], img[:, rows, :]).then_inc(x1_out, 16)

        @block.gpsimd
        def _(pool):
            nc.gpsimd.memset(low[:].rearrange("p s y x -> p (s y x)").bitcast(U32), 0).then_inc(ones_made, 1)
            pool.wait_ge(ones_made, 1)
            nc.gpsimd.memset(flat(xc[C:CV]).bitcast(U32), TWO_ONES).then_inc(ones_made, 1)
            pool.wait_ge(ones_made, 2)
            for border in (xc[C:CV, 0, :], xc[C:CV, H + 1, :], xc[C:CV, 1:H + 1, 0:1], xc[C:CV, 1:H + 1, W + 1:W + 2]):
                last = nc.gpsimd.memset(border, 0.0)
            last.then_inc(ones_made, 1)
            pool.wait_ge(ones_made, 3)
            for t, n in ((xa, P), (xb, P), (xc, C)):
                for row in (0, H + 1):
                    last = nc.gpsimd.memset(t[0:n, row, :], 0.0)
            for col in (0, W + 1):
                last = nc.gpsimd.memset(xa[0:C, 1:H + 1, col:col + 1], 0.0)
            last.then_inc(padded, 1)

        @block.vector
        def _(dve):
            c = Count(dve, dve_own)
            if b == 0:
                for q in range(NQ):
                    dve.wait_ge(img_in[q], 16)
                    last = chunk_stats(nc, img, QROWS * q, k["stats"], q, range(GN))
                c.then_wait(last)
            group_stats(nc, dve, c, k["stats"], k["dev"], part, ps_s, mom, stat_ready, stat_summed, stat_rooted)
            c.then_wait(nc.vector.tensor_copy(mom_c[0:1].rearrange("p m (g j) -> p m g j", j=GC),
                                              mom[0:1].unsqueeze(3).to_broadcast([1, 2, GN, GC])))
            dve.sem_inc(mom_row, 1)
            dve.wait_ge(mom_col, 1)
            c.then_wait(nc.vector.tensor_copy(mom_t[:, :], ps[0][0:C, 0:2]))
            dve.wait_ge(ones_made, 1)

            def norm(u, s, first=False):
                dve.wait_ge(turned, u + 1)
                if not first:
                    dve.wait_ge(hi_done, u - 1)
                    dve.wait_ge(lo_done, u - 1)
                nc.vector.tensor_scalar(z[:, s, :], ps_w[0:C, s, :], mom_t[:, 0:1], mom_t[:, 1:2], ALU.subtract,
                                        ALU.mult).then_inc(normed, 1)

            def low_part(u, s, first=False):
                dve.wait_ge(hi_done, u + 1)
                if not first:
                    dve.wait_ge(parts_in[s], (u - s) * (8 * MOVES))
                nc.vector.tensor_tensor(low[:, s, :, 1:W + 1], z[:, s, :].rearrange("p (y x) -> p y x", x=W),
                                        xa[0:C, bass.ds(u * 4 + 1, 4), 1:W + 1], ALU.subtract
                                        ).then_inc(lo_done, 1)

            def qk_low(u, s):
                dve.wait_ge(qk_hi, u + 1)
                nc.vector.tensor_tensor(qk[:, s, :, 2 * C:4 * C],
                                        ps[s][:, 0:4 * C].rearrange("p (r o) -> p r o", r=2),
                                        qk[:, s, :, 0:2 * C], ALU.subtract).then_inc(qk_lo, 1)

            norm(0, 0, True)
            norm(1, 1, True)
            low_part(0, 0, True)
            low_part(1, 1, True)
            with dve.Fori(0, UNITS // 2 - 1) as i:
                for s in range(2):
                    norm(i * 2 + (s + 2), s)
                    low_part(i * 2 + (s + 2), s)
                    qk_low(i * 4 + 2 * s, 0)
                    qk_low(i * 4 + (2 * s + 1), 1)
            for u in range(PAIRS - 4, PAIRS):
                qk_low(u, u % 2)

            dve.wait_ge(gram_out, 1)
            g = lambda j: gram[:, j * C:j * C + C]
            nc.vector.tensor_tensor(sc[:, :], g(0), g(2), ALU.add)
            nc.vector.scalar_tensor_tensor(sq[:, 0, :], g(3), 2.0, g(1), ALU.mult, ALU.add)
            c.then_wait(nc.vector.scalar_tensor_tensor(sq[:, 1, :], g(6), 2.0, g(5), ALU.mult, ALU.add))
            c.then_wait(nc.vector.tensor_tensor(sc[:, :], sc[:, :], g(4), ALU.add))
            c.then_wait(nc.vector.tensor_tensor(sq[:], sq[:], k["ident"][0:C, 0:C].unsqueeze(1)
                                                .to_broadcast([C, 2, C]), ALU.mult))
            c.then_wait(nc.vector.tensor_reduce(small[:, 0:2], sq[:], X, ALU.add))
            dve.sem_inc(att, 1)
            dve.wait_ge(att_act, 1)
            c.then_wait(nc.vector.tensor_scalar(small[:, 2:4], small[:, 2:4], 1e-12 * WSCALE, None, ALU.max))
            c.then_wait(nc.vector.reciprocal(small[:, 4:6], small[:, 2:4]))
            nc.vector.tensor_scalar(sc[:, :], sc[:, :], small[:, 4:5], None, ALU.mult)
            c.then_wait(nc.vector.tensor_tensor(small[:, 6:7], small[:, 5:6], k["temp"][:, :], ALU.mult))
            dve.sem_inc(att, 1)
            dve.wait_ge(att_pe, 1)
            c.then_wait(nc.vector.scalar_tensor_tensor(sc[:, :], ps[0][0:C, 0:C], small[:, 6:7],
                                                       k["same_head"][:, :], ALU.mult, ALU.add))
            c.then_wait(nc.vector.tensor_reduce(small[:, 7:8], sc[:, :], X, ALU.max))
            c.then_wait(nc.vector.tensor_scalar(small[:, 8:9], small[:, 7:8], -1.0, None, ALU.mult))
            dve.sem_inc(att, 1)
            dve.wait_ge(att_act, 2)
            c.then_wait(nc.vector.reciprocal(small[:, 10:11], small[:, 9:10]))
            c.then_wait(nc.vector.tensor_scalar(probs[:, :], probs[:, :], small[:, 10:11], None, ALU.mult))
            dve.sem_inc(att, 1)
            dve.wait_ge(att_act, 4)
            c.then_wait(nc.vector.tensor_tensor(wf[C:CV, 4, :], wf[C:CV, 4, :], k["b_out"][C:CV, :], ALU.add))
            dve.sem_inc(att, 1)
            dve.wait_ge(att_act, 5)
            nc.vector.scalar_tensor_tensor(wf_lo[:], wf[:], WSCALE, wf_hi[:], ALU.mult, ALU.subtract
                                           ).then_inc(wf_split, 1)

            def add_rows(u, s):
                dve.wait_ge(outs, u + 1)
                rows = img[:, bass.ds(u * 4, 4), :]
                nc.vector.scalar_tensor_tensor(rows, ps[s][:, 0:4 * C].rearrange("p (y c) -> p y c", c=C),
                                               1.0 / WSCALE, rows, ALU.mult, ALU.add).then_inc(evac, 1)

            PER = QROWS // 4
            for j in range(PER):
                add_rows(j, j % 2)
            with dve.Fori(1, NQ) as q:
                dve.wait_ge(evac, q * PER)
                for j in range(PER):
                    add_rows(q * PER + j, j % 2)
                    chunk_stats(nc, img, q * QROWS - QROWS, k["stats"], q - 1,
                                range(GN // PER * j, GN // PER * (j + 1)))
            dve.wait_ge(evac, UNITS)
            c.then_wait(chunk_stats(nc, img, H - QROWS, k["stats"], NQ - 1, range(GN)))

        @block.scalar
        def _(act):
            group_stats_root(nc, act, k, ps_s, mom, stat_summed, stat_rooted)

            def high(u, s):
                act.wait_ge(normed, u + 1)
                nc.scalar.activation(xa[0:C, bass.ds(u * 4 + 1, 4), 1:W + 1],
                                     z[:, s, :].rearrange("p (y x) -> p y x", x=W), ACT.Copy).then_inc(hi_done, 1)

            def qk_high(u, s, first=False):
                act.wait_ge(conv_done, u + 1)
                if not first:
                    act.wait_ge(gram_done, u - 1)
                nc.scalar.activation(qk[:, s, :, 0:2 * C], ps[s][:, 0:4 * C].rearrange("p (r o) -> p r o", r=2),
                                     ACT.Copy).then_inc(qk_hi, 1)

            high(0, 0)
            high(1, 1)
            for s in range(2):
                high(s + 2, s)
                qk_high(2 * s, 0, s == 0)
                qk_high(2 * s + 1, 1, s == 0)
            with act.Fori(1, UNITS // 2 - 1) as i:
                for s in range(2):
                    high(i * 2 + (s + 2), s)
                    qk_high(i * 4 + 2 * s, 0)
                    qk_high(i * 4 + (2 * s + 1), 1)
            for u in range(PAIRS - 4, PAIRS):
                qk_high(u, u % 2)

            act.wait_ge(gram_done, PAIRS + 1)
            nc.scalar.activation(gram[:, 0:4 * C], ps_g[0][0:C, 0:4 * C], ACT.Copy)
            nc.scalar.activation(gram[:, 4 * C:7 * C], ps_g[1][0:C, 0:3 * C], ACT.Copy).then_inc(gram_out, 1)
            act.wait_ge(att, 1)
            nc.scalar.activation(small[:, 2:4], small[:, 0:2], ACT.Sqrt).then_inc(att_act, 1)
            act.wait_ge(att, 3)
            nc.scalar.activation(probs[:, :], sc[:, :], ACT.Exp, bias=small[:, 8:9],
                                 accum_out=small[:, 9:10]).then_inc(att_act, 1)
            act.wait_ge(att_pe, 2)
            nc.scalar.activation(mix[:, :], ps[1][0:C, 0:C], ACT.Copy).then_inc(att_act, 1)
            act.wait_ge(att_pe, 3)
            nc.scalar.activation(wf[:, 0:5, :], ps_w[0:CV, 0, 0:5 * C].rearrange("p (t o) -> p t o", o=C), ACT.Copy)
            nc.scalar.activation(wf[:, 5:9, :], ps_w[0:CV, 1, 0:4 * C].rearrange("p (t o) -> p t o", o=C),
                                 ACT.Copy).then_inc(att_act, 1)
            act.wait_ge(att, 5)
            nc.scalar.activation(wf_hi[:], wf[:], ACT.Copy, scale=WSCALE).then_inc(att_act, 1)

        @block.tensor
        def _(pe):
            group_stats_sums(nc, pe, k, part, ps_s, stat_ready, stat_summed)
            pe.wait_ge(mom_row, 1)
            for j in range(2):
                last = nc.tensor.matmul(ps[0][0:C, j:j + 1], mom_c[0:1, j, :], k["ident"][0:1, 0:1], start=True,
                                        stop=True)
            last.then_inc(mom_col, 1)

            def turn(u, s, first=False):
                if b > 0:
                    pe.wait_ge(rows_ready[s], (u - s) * 8 + 16)
                elif u % (QROWS // 4) == 0:
                    pe.wait_ge(img_in[u // (QROWS // 4)], 16)
                if not first:
                    pe.wait_ge(normed, u - 1)
                for r in range(4):
                    last = nc.tensor.transpose(ps_w[0:C, s, r * W:r * W + W], img[:, 4 * u + r, :], k["ident"][:, :])
                last.then_inc(turned, 1)

            def conv(bank, y, rows, wa, wb, wc, n, sem_):
                for r in range(rows):
                    out = bank[:, r * n:r * n + n]
                    for t, (dy, dx) in enumerate(TAPS):
                        row = y + r + dy
                        nc.tensor.matmul(out, xa[:, row, dx:dx + W], wa[:, t, :], start=(t == 0), stop=False)
                        nc.tensor.matmul(out, xb[:, row, dx:dx + W], wb[:, t, :], start=False, stop=False)
                    for dy in range(3):
                        last = nc.tensor.matmul(out, xc[:, y + r + dy, 0:W], wc[:, dy, :],
                                                start=False, stop=(dy == 2))
                last.then_inc(sem_, 1)

            def conv_qk(u, s, first=False):
                if not first:
                    pe.wait_ge(qk_lo, u - 1)
                conv(ps[s], u * 2, 2, k["wa"], k["wb"], k["wc"], 2 * C, conv_done)

            def grams(u, s):
                pe.wait_ge(qk_lo, u + 1)
                for r in range(2):
                    q = lambda j: qk[:, s, r, j * C:j * C + C]
                    mm = lambda out, a, c_: nc.tensor.matmul(out, a, c_, start=False, stop=False,
                                                             skip_group_check=True)
                    mm(ps_g[0][0:C, 0:4 * C], q(1), qk[:, s, r, :])
                    mm(ps_g[1][0:C, 0:C], q(3), q(0))
                    last = mm(ps_g[1][0:C, C:3 * C], q(0),
                              qk[:, s, r, :].rearrange("p (a o) -> p a o", a=2)[:, :, 0:C])
                last.then_inc(gram_done, 1)

            def rows_spread(u, s):
                pe.wait_ge(parts_in[s], (u - s) * (8 * MOVES) + 16 * MOVES)

            turn(0, 0, True)
            turn(1, 1, True)
            for bank in ps_g:
                nc.tensor.matmul(bank[0:C, 0:4 * C], k["zeros"][:, 0:C], k["zeros"][:, 0:4 * C], start=True,
                                 stop=False, skip_group_check=True)
            turn(2, 0)
            pe.wait_ge(padded, 1)
            pe.wait_ge(ones_in, 16 * 5)
            rows_spread(0, 0)
            conv_qk(0, 0, True)
            rows_spread(1, 1)
            conv_qk(1, 1, True)
            grams(0, 0)
            turn(3, 1)
            rows_spread(2, 0)
            conv_qk(2, 0)
            grams(1, 1)
            conv_qk(3, 1)
            grams(2, 0)
            for i in range(1, UNITS // 2 - 1):
                for s in range(2):
                    turn(i * 2 + (s + 2), s)
                    rows_spread(i * 2 + (s + 1), 1 - s)
                    conv_qk(i * 4 + 2 * s, 0)
                    grams(i * 4 + (2 * s - 1), 1)
                    conv_qk(i * 4 + (2 * s + 1), 1)
                    grams(i * 4 + 2 * s, 0)
            rows_spread(UNITS - 1, 1)
            for u in range(PAIRS - 4, PAIRS):
                conv_qk(u, u % 2)
                grams(u - 1, (u - 1) % 2)
            grams(PAIRS - 1, 1)
            for bank in ps_g:
                last = nc.tensor.matmul(bank[0:C, 0:4 * C], k["zeros"][:, 0:C], k["zeros"][:, 0:4 * C],
                                        start=False, stop=True, skip_group_check=True)
            last.then_inc(gram_done, 1)

            pe.wait_ge(att, 2)
            nc.tensor.transpose(ps[0][0:C, 0:C], sc[:, :], k["ident"][0:C, 0:C]).then_inc(att_pe, 1)
            pe.wait_ge(att, 4)
            nc.tensor.matmul(ps[1][0:C, 0:C], probs[:, :], k["w_out"][:, :], start=True, stop=True
                             ).then_inc(att_pe, 1)
            pe.wait_ge(att_act, 3)
            for t in range(KK):
                last = nc.tensor.matmul(ps_w[0:CV, t // 5, (t % 5) * C:(t % 5) * C + C], k["wv_t"][:, t, :],
                                        mix[:, :], start=True, stop=True)
            last.then_inc(att_pe, 1)

            def conv_out(u, s, first=False):
                if not first:
                    pe.wait_ge(evac, u - 1)
                conv(ps[s], u * 4, 4, wfa, wfb, wfc, C, outs)

            pe.wait_ge(wf_in, 16 * STACKS)
            conv_out(0, 0, True)
            conv_out(1, 1, True)
            for u in range(2, UNITS):
                conv_out(u, u % 2)


def motif_grams(nc, b, k, img, f_dram, x1_out, pick_dram, att_sems):
    with ExitStack() as ctx:
        sb = lambda n, s, d: ctx.enter_context(nc.sbuf_tensor(f"{n}{b}", s, d))
        psum = lambda n, s: ctx.enter_context(nc.psum_tensor(f"{n}{b}", s, F32))
        sem = lambda n: ctx.enter_context(nc.semaphore(f"{n}{b}"))
        f = sb("f", [P, H, C], F32)
        stage = [sb(f"stage{s}_", [P, 3, MC, C], F32) for s in range(2)]
        patches = [sb(f"patches{s}_", [P, 2, C * 3 * MC], F16) for s in range(2)]
        part = sb("m_part", [P, 4, GN], F32)
        mom = sb("m_mom", [P, 2, GN], F32)
        half = sb("half", [MR, 2, MR], F32)
        g_half = sb("g_half", [MR, MG, MR], F32)
        g_turn = sb("g_turn", [MR, MG, MR], F32)
        g_all = sb("g_all", [MR, MG, MR], F32)
        blk = sb("blk", [MR, MG, MC], F32)
        tmp = sb("tmp", [MR, MG, MC], F32)
        d2 = sb("d2", [MR, MG, MC], F32)
        sqc = sb("sqc", [MR, MG], F32)
        mn = sb("mn", [MR, MG], F32)
        nnt = sb("nnt", [MG, MR], F32)
        eq2 = sb("eq2", [MG, MR], F32)
        sel = sb("sel", [MG, 8, KK], F32)
        offs = sb("offs", [MG, KK], F32)
        ps_a = [psum(f"ps_ga{j}_", [P, 512]) for j in range(2)]
        ps_t = [psum(f"ps_gt{j}_", [P, 512]) for j in range(3)]
        ps_s = psum("ps_gs", [P, 2, GN])
        (ready, summed, rooted, own, sub_done, f_done, hi_done, lo_done, f_out, main_done, half_done,
         a_done, post_pe, post_act, picks, pick_pe, pick_out) = (
            sem(n) for n in ("m_ready", "m_summed", "m_rooted", "m_dve", "m_sub", "m_f", "m_hi", "m_lo", 
                             "f_out", "main_done", "half_done", "a_done", "post_pe", "post_act", "picks", "pick_pe",
                             "pick_out"))
        stage_in = [sem(f"stage_in{s}_") for s in range(2)]
        PER = 6
        PIECES = (MC, MC, 2 * MC, 4 * MC, 4 * MC, 4 * MC)
        starts = [sum(PIECES[:j]) for j in range(len(PIECES))]
        ON_DVE = 2
        by_shift = lambda t, part_: t[0:HM, part_].rearrange("p (w k c) -> p k c w", k=3, c=MC)
        block = ctx.enter_context(nc.Block())

        @block.sync
        def _(sp):
            if b + 1 < B:
                for s_ in att_sems.values():
                    sp.sem_clear(s_)

            def load(g, s, first=False):
                if not first:
                    sp.wait_ge(lo_done, g - 1)
                for ki in range(3):
                    sp.dma_start(stage[s][0:HM, ki], f[ki:ki + HM, bass.ds(g * MC, MC), :]
                                 ).then_inc(stage_in[s], 16)

            for j in range(4):
                sp.wait_ge(f_done, min(j, 2) + 1)
                load(j, j % 2, j < 2)
            with sp.Fori(1, MG // 4) as q:
                sp.wait_ge(f_done, q + 3)
                for j in range(4):
                    load(q * 4 + j, j % 2)
            for j in range(2):
                sp.wait_ge(picks, j + 1)
                for half_ in range(2):
                    sp.dma_start(pick_dram[b, j, half_], (offs if j == 0 else sel[:, 7])[:, half_:half_ + MC]
                                 ).then_inc(pick_out, 16)
            sp.wait_ge(pick_out, 16 * 4)
            sp.wait_ge(x1_out, 16 * NQ)
            sp.wait_ge(f_out, 16 * MG)

        @block.gpsimd
        def _(pool):
            pool.wait_ge(f_done, ON_DVE)
            for j in range(ON_DVE, len(PIECES)):
                pool.wait_ge(sub_done, j + 1)
                fg = f[:, starts[j]:starts[j] + PIECES[j], :].rearrange("p y (g j) -> p y g j", j=GC)
                nc.gpsimd.tensor_tensor(fg, fg, mom[:, 1, :].unsqueeze(1).unsqueeze(3)
                                        .to_broadcast([P, PIECES[j], GN, GC]), ALU.mult).then_inc(f_done, 1)

        @block.scalar
        def _(act):
            group_stats_root(nc, act, k, ps_s, mom, summed, rooted)

            def high(i, s, first):
                act.wait_ge(stage_in[s], i * 48 + 48)
                if not first:
                    act.wait_ge(main_done, i * 2 + (s - 1))
                nc.scalar.activation(by_shift(patches[s], 0), stage[s][0:HM], ACT.Copy).then_inc(hi_done, 1)

            def halve(i, s, first):
                act.wait_ge(main_done, i * 2 + (s + 1))
                if not first:
                    act.wait_ge(a_done, i * 2 + (s - 1))
                nc.scalar.activation(half[:, s, :], ps_a[s][0:MR, 0:MR], ACT.Copy, scale=0.5).then_inc(half_done, 1)

            def store(g):
                planes = bass.ds(g * MC, MC)
                act.dma_start(by_planes(f_dram)[:, planes, :], f[:, planes, :]).then_inc(f_out, 16)

            for s in range(2):
                high(0, s, True)
                store(s)
            for s in range(2):
                halve(0, s, True)
                high(1, s, False)
                store(2 + s)
            with act.Fori(1, MG // 2 - 1) as i:
                for s in range(2):
                    halve(i, s, False)
                    high(i + 1, s, False)
                    store(i * 2 + (2 + s))
            for s in range(2):
                halve(MG // 2 - 1, s, False)
            for step, dst in enumerate((g_turn, g_all)):
                for j in range(3):
                    n = min(PER, MG - PER * j)
                    act.wait_ge(post_pe, 3 * step + j + 1)
                    nc.scalar.activation(dst[:, PER * j:PER * j + n, :],
                                         ps_t[j][0:MR, 0:n * MR].rearrange("p (g r) -> p g r", r=MR),
                                         ACT.Copy).then_inc(post_act, 1)

        @block.tensor
        def _(pe):
            group_stats_sums(nc, pe, k, part, ps_s, ready, summed)

            def grams(i, s, first):
                pe.wait_ge(lo_done, i * 2 + (s + 1))
                if not first:
                    pe.wait_ge(a_done, i * 2 + (s - 1))
                for w in range(WM):
                    cols = slice(3 * MC * w, 3 * MC * w + MR)
                    last = nc.tensor.matmul(ps_a[s][0:MR, 0:2 * MR], patches[s][0:HM, 0, cols],
                                            patches[s][0:HM, :, cols], start=(w == 0), stop=(w == WM - 1))
                last.then_inc(main_done, 1)

            grams(0, 0, True)
            grams(0, 1, True)
            with pe.Fori(1, MG // 2) as i:
                grams(i, 0, False)
                grams(i, 1, False)
            pe.wait_ge(a_done, MG)
            for g in range(MG):
                last = nc.tensor.matmul(ps_t[g // PER][0:MR, (g % PER) * MR:(g % PER) * MR + MR], g_half[:, g, :],
                                        k["order"][:, :], start=True, stop=True)
                if g % PER == PER - 1 or g == MG - 1:
                    last.then_inc(post_pe, 1)
            for g in range(MG):
                if g % PER == 0:
                    pe.wait_ge(post_act, g // PER + 1)
                out = ps_t[g // PER][0:MR, (g % PER) * MR:(g % PER) * MR + MR]
                nc.tensor.matmul(out, g_turn[:, g, :], k["order"][:, :], start=True, stop=False)
                last = nc.tensor.matmul(out, k["order"][:, :], g_turn[:, g, :], start=False, stop=True)
                if g % PER == PER - 1 or g == MG - 1:
                    last.then_inc(post_pe, 1)
            pe.wait_ge(pick_pe, 1)
            nc.tensor.matmul(ps_a[0][0:MR, 0:MG * MC], k["same_block"][:, :],
                             tmp[:].rearrange("p g d -> p (g d)"), start=True, stop=True).then_inc(post_pe, 1)
            pe.wait_ge(pick_pe, 2)
            nc.tensor.transpose(ps_a[1][0:MG, 0:MR], mn[:, :], k["ident"][0:MR, 0:MR]).then_inc(post_pe, 1)

        @block.vector
        def _(dve):
            c = Count(dve, own)
            group_stats(nc, dve, c, k["stats"], k["dev"], part, ps_s, mom, ready, summed, rooted)
            def center(j):
                planes = slice(starts[j], starts[j] + PIECES[j])
                fg = f[:, planes, :].rearrange("p y (g j) -> p y g j", j=GC)
                moment = lambda m: mom[:, m, :].unsqueeze(1).unsqueeze(3).to_broadcast([P, PIECES[j], GN, GC])
                nc.vector.tensor_tensor(fg, img[:, planes, :].rearrange("p y (g j) -> p y g j", j=GC), moment(0),
                                        ALU.subtract).then_inc(sub_done, 1)
                if j < ON_DVE:
                    dve.wait_ge(sub_done, j + 1)
                    nc.vector.tensor_tensor(fg, fg, moment(1), ALU.mult).then_inc(f_done, 1)

            def low(i, s):
                dve.wait_ge(hi_done, i * 2 + (s + 1))
                nc.vector.tensor_tensor(by_shift(patches[s], 1), stage[s][0:HM], by_shift(patches[s], 0),
                                        ALU.subtract).then_inc(lo_done, 1)

            def half_gram(i, s):
                dve.wait_ge(half_done, i * 2 + (s + 1))
                nc.vector.tensor_tensor(g_half[:, bass.ds(i * 2 + s, 1), :],
                                        ps_a[s][0:MR, MR:2 * MR].unsqueeze(1), half[:, s, :].unsqueeze(1),
                                        ALU.add).then_inc(a_done, 1)

            for j in range(4):
                center(j)
            low(0, 0)
            low(0, 1)
            for j in range(4, len(PIECES)):
                center(j)
            with dve.Fori(0, MG // 2 - 1) as i:
                for s in range(2):
                    half_gram(i, s)
                    low(i + 1, s)
            for s in range(2):
                half_gram(MG // 2 - 1, s)

            dve.wait_ge(post_act, 6)
            c.then_wait(nc.vector.tensor_tensor(g_all[:], g_all[:], k["same_block"][:, :].unsqueeze(1)
                                                .to_broadcast([MR, MG, MR]), ALU.mult))
            c.then_wait(nc.vector.tensor_reduce(blk[:], g_all[:].rearrange("p g (j d) -> p g d j", d=MC), X,
                                                ALU.add))
            own8 = k["own"][:, :].unsqueeze(1).to_broadcast([MR, MG, MC])
            iota8 = k["iota"][0:MR, 0:MC].unsqueeze(1).to_broadcast([MR, MG, MC])
            c.then_wait(nc.vector.tensor_tensor(tmp[:], blk[:], own8, ALU.mult))
            c.then_wait(nc.vector.tensor_reduce(sqc[:, :], tmp[:], X, ALU.add))
            dve.sem_inc(pick_pe, 1)
            dve.wait_ge(post_pe, 7)
            c.then_wait(nc.vector.tensor_tensor(d2[:], ps_a[0][0:MR, 0:MG * MC].rearrange("p (g d) -> p g d", d=MC),
                                                sqc[:, :].unsqueeze(2).to_broadcast([MR, MG, MC]), ALU.add))
            c.then_wait(nc.vector.scalar_tensor_tensor(d2[:], blk[:], -2.0, d2[:], ALU.mult, ALU.add))
            c.then_wait(nc.vector.tensor_scalar(tmp[:], own8, BIG, None, ALU.mult))
            c.then_wait(nc.vector.tensor_tensor(d2[:], d2[:], tmp[:], ALU.add))
            c.then_wait(nc.vector.tensor_reduce(mn[:, :], d2[:], X, ALU.min))
            c.then_wait(nc.vector.tensor_tensor(d2[:], d2[:], mn[:, :].unsqueeze(2).to_broadcast([MR, MG, MC]),
                                                ALU.is_equal))
            c.then_wait(nc.vector.tensor_scalar(tmp[:], iota8, -float(MC), None, ALU.add))
            c.then_wait(nc.vector.tensor_tensor(tmp[:], tmp[:], d2[:], ALU.mult))
            c.then_wait(nc.vector.tensor_reduce(mn[:, :], tmp[:], X, ALU.min))
            c.then_wait(nc.vector.tensor_scalar(mn[:, :], mn[:, :], float(MC), None, ALU.add))
            dve.sem_inc(pick_pe, 1)
            dve.wait_ge(post_pe, 8)
            c.then_wait(nc.vector.tensor_copy(nnt[:, :], ps_a[1][0:MG, 0:MR]))
            u, ge, cu, ku, kui, t1, t2, cm = (sel[:, j, :] for j in range(8))
            jj = k["iota"][0:MG, 0:KK]
            c.then_wait(nc.vector.tensor_reduce(u, nnt[:, :].rearrange("p (j d) -> p j d", d=MC), X, ALU.max))
            c.then_wait(nc.vector.tensor_tensor(eq2[:, :].rearrange("p (j d) -> p j d", d=MC),
                                                nnt[:, :].rearrange("p (j d) -> p j d", d=MC),
                                                u.unsqueeze(2).to_broadcast([MG, KK, MC]), ALU.is_equal))
            c.then_wait(nc.vector.tensor_reduce(cm, eq2[:, :].rearrange("p (j d) -> p j d", d=MC), X, ALU.add))
            c.then_wait(nc.vector.tensor_tensor(t1, u, jj, ALU.subtract))
            c.then_wait(nc.vector.tensor_scalar(ge, t1, 0.0, None, ALU.is_ge))
            c.then_wait(nc.vector.tensor_scalar(t1, t1, float(KK), None, ALU.add))
            c.then_wait(nc.vector.scalar_tensor_tensor(ku, ge, -float(KK), t1, ALU.mult, ALU.add))
            c.then_wait(nc.vector.scalar_tensor_tensor(cu, ge, -1.0, jj, ALU.add, ALU.add))
            c.then_wait(nc.vector.tensor_scalar(t1, ku, 3.0, None, ALU.is_ge))
            c.then_wait(nc.vector.tensor_scalar(t2, ku, 6.0, None, ALU.is_ge))
            c.then_wait(nc.vector.tensor_tensor(kui, t1, t2, ALU.add))
            c.then_wait(nc.vector.scalar_tensor_tensor(t1, kui, float(C - 3), ku, ALU.mult, ALU.add))
            c.then_wait(nc.vector.scalar_tensor_tensor(t2, cu, float(PLANE), t1, ALU.mult, ALU.add))
            c.then_wait(nc.vector.tensor_scalar(offs[:, :], t2, k["group_base"][0:MG, :], None,
                                                ALU.add))
            dve.sem_inc(picks, 1)
            c.then_wait(nc.vector.tensor_scalar(cm, cm, 1.0 / MC, None, ALU.mult))
            dve.sem_inc(picks, 1)


def motif_terms(nc, b, k, x, f_dram, x1_dram, pick_dram, out):
    R = 16
    N = H // R
    SLOTS = 4
    NR = R + 2
    BR = 4
    PRODS, RNDS = 4, 3
    with ExitStack() as ctx:
        sb = lambda n, s, d: ctx.enter_context(nc.sbuf_tensor(f"{n}{b}", s, d))
        sem = lambda n: ctx.enter_context(nc.semaphore(f"{n}{b}"))
        near = sb("near", [P, SLOTS, NR * C], F32)
        near2 = sb("near2", [P, SLOTS, NR * C], F32)
        fc = sb("fc", [P, SLOTS, R * C], F32)
        x1c = sb("x1c", [P, SLOTS, R * C], F32)
        prod = sb("prod", [P, PRODS, R, WM], F32)
        rnd_m = sb("rnd_m", [P, 2, R, WM], F32)
        rnd = sb("rnd", [P, RNDS, R, WM], F32)
        over = sb("over", [P, 2, R, WM], BF16)
        if b + 1 < B:
            x_next = sb("x_next", [P, 2 * QROWS, C], F32)
            next_in = [sem(f"next_in{j}_") for j in range(2)]
            next_stats = sem("next_stats")
        pick = sb("pick", [P, 4], F32)
        scale = sb("scale", [P, KK], F32)
        index_f = sb("index_f", [P, 2, N], F32)
        index = sb("index", [P, 2, N], I32)
        acc = [ctx.enter_context(nc.psum_tensor(f"acc{s}_{b}", [P, R // BR, 512], F32)) for s in range(2)]
        (pick_in, own, scaled, indexed, edged, prod_v, prod_p, rm_done, rnd_done, over_done, acc_done, out_ready,
         fold) = (
            sem(n) for n in ("pick_in", "t_dve", "scaled", "indexed", "edged", "prod_v", "prod_p", "rm_done",
                             "rnd_done", "over_done", "acc_done", "out_ready", "fold"))
        stored, near_in, near2_in, fc_in, x1_in = ([sem(f"{n}{j}_") for j in range(SLOTS)]
                                                   for n in ("stored", "near_in", "near2_in", "fc_in", "x1_in"))
        moved = [sem(f"moved{s}_") for s in range(2)]
        steps = [(2 * m + s, sh) for m in range(N // 2) for sh in range(KK) for s in range(2)]
        number = {st: n for n, st in enumerate(steps)}
        on_pool = [i % 2 == 1 for i, sh in steps]
        STATS_PER, STATS_AT, LOAD_AT = 13, 19, 6
        after = {i: number[(i, KK - 1)] + 1 for i in range(N)}
        first_row = lambda i: max(R * i - 2, 0)
        last_row = lambda i: min(R * i + R - 1, HM - 1)

        def product_made(eng, n):
            eng.wait_ge(prod_p if on_pool[n] else prod_v, sum(p == on_pool[n] for p in on_pool[:n + 1]))

        def product_inputs(eng, n):
            i, sh = steps[n]
            s = i % SLOTS
            if sh == 0:
                eng.wait_ge(near_in[s], 16 * (i // SLOTS + 1))
                eng.wait_ge(fc_in[s], 16 * (i // SLOTS + 1))
                eng.wait_ge(edged, 2 if i == N - 1 else 1)
            else:
                eng.wait_ge(moved[i % 2], 16 * (8 * (i // 2) + sh))
            if n >= PRODS:
                eng.wait_ge(over_done, n - PRODS + 1)

        def product(vec, n):
            i, sh = steps[n]
            s, (dy, dx) = i % SLOTS, TAPS[sh]
            fv = fc[:, s, :].rearrange("p (r c) -> p r c", c=C)[:, :, dx:dx + WM]
            nv = near[:, s, :].rearrange("p (r c) -> p r c", c=C)[:, 2 - dy:2 - dy + R, 0:WM]
            return vec.tensor_tensor(prod[:, n % PRODS], fv, nv, ALU.mult)

        def run(i):
            a = (first_row(i) - (R * i - 2)) * C
            return slice(a, a + (last_row(i) - first_row(i)) * C + WM)

        out_p = out[b].rearrange("y x c -> y (x c)")
        block = ctx.enter_context(nc.Block())

        @block.sync
        def _(sp):
            def load_rows(dst, src, i, sem_):
                sp.dma_start(dst[:, i % SLOTS, :], src[:, R * i * C:(R * i + R) * C]).then_inc(sem_[i % SLOTS], 16)

            for j in range(2):
                for half_ in range(2):
                    sp.dma_start(pick[:, 2 * j + half_:2 * j + half_ + 1],
                                 pick_dram[b, j, half_].rearrange("g (c o) -> (g c) o", o=1)
                                 ).then_inc(pick_in, 16)

            def load_next(q, piece):
                rows, slot = QROWS // 4, QROWS * (q % 2)
                if q >= 2 and piece == 0:
                    sp.wait_ge(next_stats, q - 1)
                sp.dma_start(x_next[:, slot + rows * piece:slot + rows * (piece + 1), :],
                             x[b + 1].rearrange("y x c -> x y c")[:, QROWS * q + rows * piece:
                                                                  QROWS * q + rows * (piece + 1), :]
                             ).then_inc(next_in[q % 2], 16)

            def store(i):
                sp.wait_ge(out_ready, i + 1)
                sp.dma_start(out_p[:, R * i * C:(R * i + R) * C], x1c[:, i % SLOTS, :]
                             ).then_inc(stored[i % SLOTS], 16)

            for i in range(2):
                load_rows(fc, f_dram, i, fc_in)
            for n, (i, sh) in enumerate(steps):
                if sh >= 1:
                    if sh == 1:
                        sp.wait_ge(near2_in[i % SLOTS], 16 * (i // SLOTS + 1))
                    product_made(sp, n - 2)
                    sp.dma_start(near[MC - sh:P:MC, i % SLOTS, run(i)], near2[MC - sh:P:MC, i % SLOTS, run(i)]
                                 ).then_inc(moved[i % 2], 16)
                if sh == 5 and i + 2 < N:
                    if i >= 2:
                        product_made(sp, number[(i - 2, KK - 1)])
                        product_made(sp, number[(i - 2, KK - 2)])
                        if b == 1:
                            sp.wait_ge(fold, i - 1)
                    load_rows(fc, f_dram, i + 2, fc_in)
                if i >= 2 and sh == 2:
                    store(i - 2)
                if sh == 1 and i < 2:
                    load_rows(x1c, x1_dram, i, x1_in)
                q, part = (n - LOAD_AT) // STATS_PER, (n - LOAD_AT) % STATS_PER
                if b + 1 < B and 0 <= q < NQ and part in (0, 3, 6, 9):
                    load_next(q, part // 3)
                if sh == 4 and i + 2 < N:
                    if i >= 2:
                        sp.wait_ge(stored[(i + 2) % SLOTS], 16 * ((i + 2) // SLOTS))
                    load_rows(x1c, x1_dram, i + 2, x1_in)
            for i in range(N - 2, N):
                store(i)
            for j in range(SLOTS):
                sp.wait_ge(stored[j], 16 * (N // SLOTS))

        @block.gpsimd
        def _(pool):
            def gather(i, second):
                s = i % SLOTS
                pool.indirect_dma_start(
                    (near2 if second else near)[:, s, run(i)], None, f_dram.rearrange("y (e o) -> (y e) o", o=1),
                    bass.IndirectOffsetOnAxis(ap=index[:, second, i:i + 1], axis=0)
                ).then_inc((near2_in if second else near_in)[s], 16)

            nc.gpsimd.memset(near[:, 0, 0:2 * C], 0.0).then_inc(edged, 1)
            pool.wait_ge(indexed, 1)
            for second in range(2):
                gather(0, second)
                gather(1, second)
            for n, (i, sh) in enumerate(steps):
                if sh in (1, 3) and i + 2 < N:
                    if sh == 1 and i >= 2:
                        product_made(pool, number[(i - 2, KK - 1)])
                        product_made(pool, number[(i - 2, KK - 2)])
                    if sh == 1 and i + 2 == N - 1:
                        nc.gpsimd.memset(near[:, (i + 2) % SLOTS, R * C:NR * C], 0.0).then_inc(edged, 1)
                    gather(i + 2, sh // 2)
                if on_pool[n]:
                    product_inputs(pool, n)
                    product(nc.gpsimd, n).then_inc(prod_p, 1)

        @block.vector
        def _(dve):
            c = Count(dve, own)
            dve.wait_ge(pick_in, 64)
            for i in range(N):
                last = nc.vector.tensor_scalar(index_f[:, :, i], pick[:, 0:2], float(first_row(i) * C), None,
                                               ALU.add)
            c.then_wait(last)
            nc.vector.tensor_copy(index[:], index_f[:]).then_inc(indexed, 1)
            nc.vector.tensor_scalar(scale[:, :], k["second_block"][:, :], pick[:, 3:4], None, ALU.mult)
            c.then_wait(nc.vector.tensor_scalar(k["first_part"][:, :], k["second_block"][:, :], -1.0, 1.0, ALU.mult,
                                                ALU.add))
            nc.vector.scalar_tensor_tensor(scale[:, :], k["first_part"][:, :], pick[:, 2:3], scale[:, :],
                                           ALU.mult, ALU.add).then_inc(scaled, 1)
            dve.wait_ge(scaled, 1)

            def overshoot(n):
                sh = steps[n][1]
                dve.wait_ge(rnd_done, n + 1)
                if n >= 2:
                    dve.wait_ge(acc_done, n - 1)
                nc.vector.scalar_tensor_tensor(over[:, n % 2], prod[:, n % PRODS], scale[:, sh:sh + 1],
                                               rnd[:, n % RNDS], ALU.mult, ALU.is_lt).then_inc(over_done, 1)

            def finish(i):
                dve.wait_ge(acc_done, after[i])
                dve.wait_ge(x1_in[i % SLOTS], 16 * (i // SLOTS + 1))
                if b == 1:
                    dve.wait_ge(fold, i + 1)
                v = x1c[:, i % SLOTS, :].rearrange("p (m c) -> p m c", c=BR * C)
                nc.vector.tensor_tensor(v, v, acc[i % 2][:, :, 0:BR * C], ALU.add).then_inc(out_ready, 1)

            def own_patches(i):
                s = i % SLOTS
                dve.wait_ge(fc_in[s], 16 * (i // SLOTS + 1))
                dve.wait_ge(x1_in[s], 16 * (i // SLOTS + 1))
                fv = fc[:, s, :].rearrange("p (r c) -> p r c", c=C)
                xv = x1c[:, s, :].rearrange("p (r c) -> p r c", c=C)
                top, end = (2 if i == 0 else 0), (R - 2 if i == N - 1 else R)
                rows = [(slice(top, end), 3.0)]
                rows += [(slice(r, r + 1), r + 1.0) for r in range(top)]
                rows += [(slice(r, r + 1), float(R - r)) for r in range(end, R)]
                for r, in_rows in rows:
                    for cols, in_cols in ((slice(2, C - 2), 3.0), (slice(0, C, C - 1), 1.0),
                                          (slice(1, C - 1, C - 3), 2.0)):
                        last = nc.vector.scalar_tensor_tensor(xv[:, r, cols], fv[:, r, cols], in_rows * in_cols,
                                                              xv[:, r, cols], ALU.mult, ALU.add)
                last.then_inc(fold, 1)

            def stats_share(n):
                q, part = (n - STATS_AT) // STATS_PER, (n - STATS_AT) % STATS_PER
                if 0 <= q < NQ:
                    if part == 0:
                        dve.wait_ge(next_in[q % 2], 64 * (q // 2 + 1))
                    groups = range(GN * part // STATS_PER, GN * (part + 1) // STATS_PER)
                    last = chunk_stats(nc, x_next, QROWS * (q % 2), k["stats"], q, groups)
                    if part == STATS_PER - 1:
                        last.then_inc(next_stats, 1)

            LAG = 2
            for n in range(len(steps) + LAG):
                if n < len(steps) and not on_pool[n]:
                    product_inputs(dve, n)
                    product(nc.vector, n).then_inc(prod_v, 1)
                if n >= LAG:
                    overshoot(n - LAG)
                    i, sh = steps[n - LAG]
                    if i >= 2 and sh == 0:
                        finish(i - 2)
                    if b == 1 and sh == 3:
                        own_patches(i)
                if b + 1 < B and n < len(steps):
                    stats_share(n)
            finish(N - 2)
            finish(N - 1)
            if b + 1 < B:
                dve.wait_ge(next_stats, NQ)

        @block.scalar
        def _(act):
            act.wait_ge(scaled, 1)
            for n, (i, sh) in enumerate(steps):
                product_made(act, n)
                if n >= 2:
                    act.wait_ge(rnd_done, n - 1)
                nc.scalar.activation(rnd_m[:, n % 2], prod[:, n % PRODS], ACT.Identity,
                                     bias=k["plus_round"][:, 0:1], scale=scale[:, sh:sh + 1]).then_inc(rm_done, 1)
                act.wait_ge(rm_done, n + 1)
                if n >= RNDS:
                    act.wait_ge(acc_done, n - RNDS + 1)
                nc.scalar.activation(rnd[:, n % RNDS], rnd_m[:, n % 2], ACT.Identity,
                                     bias=k["minus_round"][:, 0:1]).then_inc(rnd_done, 1)

        @block.tensor
        def _(pe):
            for n, (i, sh) in enumerate(steps):
                dx = TAPS[sh][1]
                bank = acc[i % 2]
                if sh == 0:
                    if i >= 2:
                        pe.wait_ge(out_ready, i - 1)
                    for m in range(R // BR):
                        nc.tensor.matmul(bank[:, m, 0:BR * C], k["zeros"][:, 0:P], k["zeros"][:, 0:BR * C],
                                         start=True, stop=False, skip_group_check=True)
                o = lambda m: bank[:, m, 0:BR * C].rearrange("p (r c) -> p r c", c=C)[:, :, dx:dx + WM]
                pe.wait_ge(rnd_done, n + 1)
                for m in range(R // BR):
                    nc.tensor.matmul(o(m), k["ident"][:, :], rnd[:, n % RNDS, BR * m:BR * m + BR, :], start=False,
                                     stop=False, skip_group_check=True)
                pe.wait_ge(over_done, n + 1)
                for m in range(R // BR):
                    last = nc.tensor.matmul(o(m), k["minus_ident"][:, :], over[:, n % 2, BR * m:BR * m + BR, :],
                                            start=False, stop=(sh == KK - 1), skip_group_check=True)
                last.then_inc(acc_done, 1)


def build(nc, x, w_qkv, b_qkv, w_dw, b_dw, temperature, w_out, b_out, out):
    f_dram = [nc.dram_tensor(f"f_planes{b}", (H, PLANE), F32).ap() for b in range(B)]
    x1_dram = [nc.dram_tensor(f"x1_planes{b}", (H, PLANE), F32).ap() for b in range(B)]
    pick_dram = nc.dram_tensor("picks_dram", (B, 2, 2, MG, MC), F32).ap()
    ins = dict(w_qkv=w_qkv, b_qkv=b_qkv, w_dw=w_dw, b_dw=b_dw, temperature=temperature, w_out=w_out, b_out=b_out)
    with ExitStack() as ctx:
        sb = lambda n, s, d: ctx.enter_context(nc.sbuf_tensor(n, s, d))
        k = dict(
            ident=sb("ident", [P, P], F32), minus_ident=sb("minus_ident", [P, P], BF16),
            zeros=sb("zeros_k", [P, 4 * C], BF16), mean_ones=sb("mean_ones", [P, P], F32),
            eps=sb("eps", [P, 1], F32), plus_round=sb("plus_round", [P, 1], F32),
            minus_round=sb("minus_round", [P, 1], F32),
            same_head=sb("same_head", [C, C], F32), same_block=sb("same_block", [MR, MR], F32),
            order=sb("order", [MR, MR], F32), own=sb("own8", [MR, MC], F32), iota=sb("iota", [P, 32], F32),
            group_base=sb("group_base", [P, 1], F32), plane_f=sb("plane_f", [P, 1], F32),
            second_block=sb("second_block", [P, KK], F32), first_part=sb("first_part", [P, KK], F32),
            temp=sb("temp", [C, 1], F32), w_out=sb("w_out_s", [C, C], F32), b_out=sb("b_out_s", [CV, C], F32),
            wa=sb("wa", [P, KK, 2 * C], F16), wb=sb("wb", [P, KK, 2 * C], F16), wc=sb("wc", [XCR, 3, 2 * C], F16),
            stats=sb("stats", [P, GN, NQ, 6], F32), dev=sb("dev", [P, GN, 2 * NQ], F32),
            wv_t=sb("wv_t", [C, KK, CV], F32),
        )
        x1_out = [ctx.enter_context(nc.semaphore(f"x1_out{b}")) for b in range(B)]
        att_sems = {n: ctx.enter_context(nc.semaphore(n)) for n in ATT_SEMS}
        for b in range(B):
            with nc.sbuf_tensor(f"img{b}", [P, H, C], F32) as img:
                if b == 0:
                    prepare(nc, k, ins, x, img, [att_sems[f"img_in{q}"] for q in range(NQ)])
                attention(nc, b, k, x, img, x1_dram[b], x1_out[b], att_sems)
                motif_grams(nc, b, k, img, f_dram[b], x1_out[b], pick_dram, att_sems)
            motif_terms(nc, b, k, x, f_dram[b], x1_dram[b], pick_dram, out)


_INS = ["x", "L0_conv_w_qkv", "L0_conv_b_qkv", "L0_conv_w_dw", "L0_conv_b_dw", "L0_conv_temperature",
        "L0_conv_w_out", "L0_conv_b_out"]


def kernel(**inputs):
    import numpy as np
    import concourse.bacc as bacc
    from concourse import mybir as my
    from concourse.bass_utils import run_bass_kernel_spmd

    nc = bacc.Bacc("TRN2", target_bir_lowering=False, num_devices=1)
    arrays, args = {}, []
    for name in _INS:
        a = np.ascontiguousarray(inputs[name])
        arrays[f"in_{name}"] = a
        args.append(nc.dram_tensor(f"in_{name}", a.shape, my.dt.from_np(a.dtype), kind="ExternalInput").ap())
    out = nc.dram_tensor("out_0", (B, H, W, C), F32, kind="ExternalOutput").ap()
    build(nc, *args, out)
    r = run_bass_kernel_spmd(nc, [arrays], core_ids=[0])
    return r.results[0]["out_0"]
```

```python
from contextlib import ExitStack

import concourse.bass as bass
from concourse import mybir

ALU = mybir.AluOpType
ACT = mybir.ActivationFunctionType
X = mybir.AxisListType.X
F32 = mybir.dt.float32
F16 = mybir.dt.float16
BF16 = mybir.dt.bfloat16
I32 = mybir.dt.int32
U32 = mybir.dt.uint32

P = 128
B, H, W, C = 2, 128, 128, 96
HEADS = 4
HC = C // HEADS
CV = C + 1
GN = 32
GC = C // GN
TAPS = [(dy, dx) for dy in range(3) for dx in range(3)]
WSCALE = 1024.0
PLANE = W * C
MG = 16
MC = 8
KK = 9
MR = MC * KK
HM, WM = W - 2, C - 2
ROUND = 1.5 * 2.0 ** 23
BIG = 1.0e30
TWO_ONES = 0x3C003C00
PADW = W + 2
XCR = C + 6
QROWS = 32
NQ = H // QROWS


def by_planes(d):
    return d.rearrange("y (x c) -> x y c", c=C)


class Count:

    def __init__(self, eng, sem):
        self.eng, self.sem, self.n = eng, sem, 0

    def done(self, ins):
        self.n += 1
        ins.then_inc(self.sem, 1)
        return self.n

    def then_wait(self, ins):
        self.eng.wait_ge(self.sem, self.done(ins))


def chunk_stats(nc, img, row, stats, q, groups):
    for g in groups:
        last = nc.vector.bn_stats(stats[:, g, bass.ds(q, 1), :].rearrange("p a s -> p (a s)"),
                                  img[:, bass.ds(row, QROWS), GC * g:GC * g + GC])
    return last


def group_stats_local(nc, c, stats, part, dev):
    parts = stats[:].rearrange("p g q (e s) -> p g (q e) s", s=3)
    m, v = parts[:, :, :, 1], parts[:, :, :, 2]
    c.then_wait(nc.vector.tensor_reduce(part[:, 0, :], m, X, ALU.add))
    nc.vector.tensor_reduce(part[:, 1, :], v, X, ALU.add)
    c.then_wait(nc.vector.tensor_scalar(part[:, 0, :], part[:, 0, :], 0.5 / NQ, None, ALU.mult))
    c.then_wait(nc.vector.tensor_tensor(dev[:], m, part[:, 0, :].unsqueeze(2).to_broadcast([P, GN, 2 * NQ]),
                                        ALU.subtract))
    c.then_wait(nc.vector.tensor_tensor(dev[:], dev[:], dev[:], ALU.mult))
    c.then_wait(nc.vector.tensor_reduce(part[:, 2, :], dev[:], X, ALU.add))
    c.then_wait(nc.vector.scalar_tensor_tensor(part[:, 1, :], part[:, 2, :], float(QROWS * GC // 2),
                                               part[:, 1, :], ALU.mult, ALU.add))
    c.then_wait(nc.vector.tensor_scalar(part[:, 1, :], part[:, 1, :], 1.0 / (H * GC), None, ALU.mult))


def group_stats(nc, dve, c, stats, dev, part, ps, mom, ready, summed, rooted):
    group_stats_local(nc, c, stats, part, dev)
    c.then_wait(nc.vector.tensor_copy(part[:, 3, :], part[:, 0, :]))
    dve.sem_inc(ready, 1)
    dve.wait_ge(summed, 1)
    c.then_wait(nc.vector.tensor_copy(mom[:, 0, :], ps[:, 0, :]))
    c.then_wait(nc.vector.tensor_tensor(part[:, 0, :], part[:, 0, :], mom[:, 0, :], ALU.subtract))
    c.then_wait(nc.vector.tensor_tensor(part[:, 0, :], part[:, 0, :], part[:, 0, :], ALU.mult))
    c.then_wait(nc.vector.tensor_tensor(part[:, 1, :], part[:, 1, :], part[:, 0, :], ALU.add))
    dve.sem_inc(ready, 1)
    dve.wait_ge(rooted, 1)
    c.then_wait(nc.vector.reciprocal(mom[:, 1, :], mom[:, 1, :]))


def group_stats_sums(nc, pe, k, part, ps, ready, summed):
    for step, line in ((0, 3), (1, 1)):
        pe.wait_ge(ready, step + 1)
        nc.tensor.matmul(ps[:, step, :], k["mean_ones"][:, :], part[:, line, :], start=True,
                         stop=True).then_inc(summed, 1)


def group_stats_root(nc, act, k, ps, mom, summed, rooted):
    act.wait_ge(summed, 2)
    nc.scalar.activation(mom[:, 1, :], ps[:, 1, :], ACT.Sqrt, bias=k["eps"][:, 0:1]).then_inc(rooted, 1)


STACKS, STACKS_C = 4, 9


def stack_weights(eng, hi, lo, wa, wb, wc, sem, sem_c):
    def move(dst, src, sem):
        eng.dma_start(dst, src).then_inc(sem, 16)

    by_dx = lambda t, lines, dx: t[lines].rearrange("p (a b) o -> p a b o", b=3)[:, :, dx, :]
    move(wa[0:C], hi[0:C], sem)
    move(wa[C:P], hi[0:32], sem)
    move(wb[0:C], lo[0:C], sem)
    move(wb[C:P], hi[32:64], sem)
    for dx in range(3):
        move(wc[32 * dx:32 * dx + 32], by_dx(hi, slice(64, C), dx), sem_c)
        move(wc[C + dx:C + dx + 1], by_dx(hi, slice(C, CV), dx), sem_c)
        move(wc[C + 3 + dx:C + 4 + dx], by_dx(lo, slice(C, CV), dx), sem_c)


def prepare(nc, k, ins, x):
    with ExitStack() as ctx:
        sb = lambda n, s, d: ctx.enter_context(nc.sbuf_tensor(n, s, d))
        sem = lambda n: ctx.enter_context(nc.semaphore(n))
        w_aug = sb("w_aug", [CV, 3 * C], F32)
        dw_all = sb("dw_all", [CV, KK, 3 * C], F32)
        b_dw = sb("b_dw_row", [CV, 3 * C], F32)
        w_full = sb("w_full", [CV, KK, 3 * C], F32)
        wqk_hi = sb("wqk_hi", [CV, KK, 2 * C], F16)
        wqk_lo = sb("wqk_lo", [CV, KK, 2 * C], F16)
        plane_i = sb("plane_i", [P, 1], I32)
        iota_i = sb("iota_i", [P, 32], I32)
        ps_wv = ctx.enter_context(nc.psum_tensor("ps_wv", [C, 2, 512], F32))
        x_rows = sb("x_rows", [P, W, C], F32)
        weights_in = sem("weights_in")
        x_in = [sem(f"x_in{q}") for q in range(NQ)]
        zeroed, pooled, made, rounded, turned, dve_own, split, stacked, stacked_c = (
            sem(n) for n in ("pre_zeroed", "pre_pooled", "pre_made", "pre_rounded", "pre_turned", "pre_dve",
                             "pre_split", "pre_stacked", "pre_stacked_c"))
        block = ctx.enter_context(nc.Block())

        @block.sync
        def _(sp):
            sp.dma_start(w_aug[0:C, :], ins["w_qkv"].rearrange("a b c o -> (a b c) o")).then_inc(weights_in, 16)
            sp.dma_start(w_aug[C:CV, :], ins["b_qkv"].rearrange("(a o) -> a o", a=1)).then_inc(weights_in, 16)
            sp.dma_start(dw_all[:].rearrange("p t o -> p (t o)"),
                         ins["w_dw"].rearrange("a b c o -> c (a b o)").to_broadcast([CV, KK * 3 * C])
                         ).then_inc(weights_in, 16)
            sp.dma_start(b_dw[C:CV, :], ins["b_dw"].rearrange("(a o) -> a o", a=1)).then_inc(weights_in, 16)
            sp.dma_start(k["w_out"][:, :], ins["w_out"].rearrange("a b c o -> (a b c) o")).then_inc(weights_in, 16)
            sp.dma_start(k["b_out"][C:CV, :], ins["b_out"].rearrange("(a o) -> a o", a=1)).then_inc(weights_in, 16)
            for h in range(HEADS):
                sp.dma_start(k["temp"][HC * h:HC * h + HC, :],
                             ins["temperature"].rearrange("a h b c -> (a b c) h")[:, h:h + 1]
                             .to_broadcast([HC, 1])).then_inc(weights_in, 16)
            for q in range(NQ):
                sp.dma_start(x_rows[:, QROWS * q:QROWS * (q + 1), :], x[0][:, QROWS * q:QROWS * (q + 1), :]
                             ).then_inc(x_in[q], 16)
            sp.wait_ge(split, 1)
            stack_weights(sp, wqk_hi, wqk_lo, k["wa"], k["wb"], k["wc"], stacked, stacked_c)
            sp.wait_ge(stacked, 16 * STACKS)
            sp.wait_ge(stacked_c, 16 * STACKS_C)

        @block.gpsimd
        def _(pool):
            nc.gpsimd.memset(k["ident"][:, :], 0.0)
            nc.gpsimd.memset(k["same_head"][:, :], 0.0)
            nc.gpsimd.memset(k["order"][:, :], 0.0)
            nc.gpsimd.memset(k["same_block"][:, :], 1.0)
            nc.gpsimd.memset(k["group_planes"][:, :], 1.0)
            nc.gpsimd.memset(k["mean_ones"][:, :], 1.0 / P)
            nc.gpsimd.memset(k["zeros"][:, :], 0.0)
            nc.gpsimd.memset(k["eps"][:, :], 1e-5)
            nc.gpsimd.memset(k["plus_round"][:, :], ROUND)
            nc.gpsimd.memset(k["minus_round"][:, :], -ROUND)
            nc.gpsimd.iota(plane_i[:, :], [[0, 1]], base=0, channel_multiplier=1)
            nc.gpsimd.iota(iota_i[:, :], [[1, 32]], base=0, channel_multiplier=0).then_inc(zeroed, 1)
            pool.wait_ge(zeroed, 1)
            nc.gpsimd.affine_select(k["ident"][:, :], k["ident"][:, :], [[-1, P]], ALU.not_equal, 1.0,
                                    base=0, channel_multiplier=1)
            nc.gpsimd.affine_select(k["order"][:, :], k["order"][:, :], [[-1, MC], [-MC, 3], [-3 * MC, 3]],
                                    ALU.not_equal, 1.0, base=0, channel_multiplier=1)
            nc.gpsimd.affine_select(k["same_head"][:, :], k["same_head"][:, :], [[-HC, HEADS], [0, HC]],
                                    ALU.is_ge, -BIG, base=0, channel_multiplier=1)
            nc.gpsimd.affine_select(k["same_block"][:, :], k["same_block"][:, :], [[-MC, KK], [0, MC]],
                                    ALU.is_ge, 0.0, base=0, channel_multiplier=1)
            nc.gpsimd.affine_select(k["group_planes"][:, :], k["group_planes"][:, :], [[1, P]],
                                    ALU.is_ge, 0.0, base=0, channel_multiplier=-MC).then_inc(zeroed, 1)
            pool.wait_ge(zeroed, 2)
            nc.gpsimd.affine_select(k["group_planes"][:, :], k["group_planes"][:, :], [[-1, P]],
                                    ALU.is_ge, 0.0, base=MC - 1, channel_multiplier=MC)
            nc.gpsimd.affine_select(k["same_head"][:, :], k["same_head"][:, :], [[HC, HEADS], [0, HC]],
                                    ALU.is_ge, -BIG, base=HC - 1, channel_multiplier=-1)
            nc.gpsimd.affine_select(k["same_block"][:, :], k["same_block"][:, :], [[MC, KK], [0, MC]],
                                    ALU.is_ge, 0.0, base=MC - 1, channel_multiplier=-1).then_inc(pooled, 1)

        @block.vector
        def _(dve):
            c = Count(dve, dve_own)
            dve.wait_ge(pooled, 1)
            nc.vector.tensor_scalar(k["minus_ident"][:, :], k["ident"][:, :], -1.0, None, ALU.mult)
            nc.vector.tensor_copy(k["iota"][:, :], iota_i[:, :])
            nc.vector.tensor_copy(k["group_base"][:, :], plane_i[:, :])
            nc.vector.tensor_reduce(k["own"][:, :], k["ident"][0:MR, 0:MR].rearrange("p (j d) -> p d j", d=MC), X,
                                    ALU.add)
            c.then_wait(nc.vector.tensor_scalar(plane_i[:, :], plane_i[:, :], MC - 1, None, ALU.bitwise_and))
            plane_f = k["plane_f"]
            c.then_wait(nc.vector.tensor_copy(plane_f[:, :], plane_i[:, :]))
            nc.vector.tensor_scalar(k["group_base"][:, :], k["group_base"][:, :], plane_f[:, :], float(PLANE),
                                    ALU.subtract, ALU.mult)
            for half_ in range(2):
                nc.vector.tensor_scalar(k["own_block"][:, half_, :], k["iota"][:, 0:KK], -float(half_),
                                        plane_f[:, :], ALU.add, ALU.is_equal)
            for s in range(KK):
                last = nc.vector.tensor_scalar(k["second_block"][:, s:s + 1], plane_f[:, :], float(MC - s), None,
                                               ALU.is_ge)
            c.then_wait(last)
            nc.vector.tensor_scalar(k["first_part"][:, :], k["second_block"][:, :], -1.0, 1.0, ALU.mult, ALU.add)
            dve.wait_ge(weights_in, 16 * 10)
            c.then_wait(nc.vector.tensor_tensor(w_full[:], dw_all[:],
                                                w_aug[:].unsqueeze(1).to_broadcast([CV, KK, 3 * C]), ALU.mult))
            c.then_wait(nc.vector.tensor_tensor(w_full[C:CV, 4, :], w_full[C:CV, 4, :], b_dw[C:CV, :], ALU.add))
            dve.sem_inc(made, 1)
            dve.wait_ge(rounded, 1)
            nc.vector.scalar_tensor_tensor(wqk_lo[:], w_full[:, :, 0:2 * C], WSCALE, wqk_hi[:], ALU.mult,
                                           ALU.subtract).then_inc(split, 1)
            dve.wait_ge(turned, 1)
            nc.vector.tensor_copy(k["wv_t"][:, 0:5, :], ps_wv[:, 0, 0:5 * CV].rearrange("p (t c) -> p t c", c=CV))
            nc.vector.tensor_copy(k["wv_t"][:, 5:9, :], ps_wv[:, 1, 0:4 * CV].rearrange("p (t c) -> p t c", c=CV))
            for q in range(NQ):
                dve.wait_ge(x_in[q], 16)
                last = chunk_stats(nc, x_rows, QROWS * q, k["stats"], q, range(GN))
            c.then_wait(last)

        @block.scalar
        def _(act):
            act.wait_ge(made, 1)
            nc.scalar.activation(wqk_hi[:], w_full[:, :, 0:2 * C], ACT.Copy, scale=WSCALE).then_inc(rounded, 1)

        @block.tensor
        def _(pe):
            pe.wait_ge(pooled, 1)
            pe.wait_ge(made, 1)
            for t in range(KK):
                last = nc.tensor.transpose(ps_wv[:, t // 5, (t % 5) * CV:(t % 5) * CV + CV],
                                           w_full[:, t, 2 * C:3 * C], k["ident"][0:CV, 0:CV])
            last.then_inc(turned, 1)


ATT_SEMS = ("stat_ready", "stat_summed", "stat_rooted", "a_dve", "padded", "ones_made", "ones_in", "turned",
            "normed", "hi_done", "lo_done", "mom_row", "mom_col", "conv_done", "qk_lo", "gram_done",
            "gram_out", "att", "att_pe", "att_act", "wf_split", "wf_in", "outs", "evac",
            "sq_made", "sq_added", "ones_below", "wfc_in") \
    + ("rows_ready0", "rows_ready1", "parts_in0", "parts_in1")


def attention(nc, b, k, x, img, x1_dram, x1_out, sems):
    UNITS = H // 4
    PAIRS = H // 2
    TOP = 12
    MOVES = 6
    with ExitStack() as ctx:
        sb = lambda n, s, d: ctx.enter_context(nc.sbuf_tensor(f"{n}{b}", s, d))
        psum = lambda n, s: ctx.enter_context(nc.psum_tensor(f"{n}{b}", s, F32))
        xa = sb("xa", [P, H + 2, PADW], F16)
        xb = sb("xb", [P, H + 2, PADW], F16)
        xc = sb("xc", [XCR, H + 2, PADW], F16)
        z = sb("z", [C, 2, 4 * W], F32)
        low = sb("low", [C, 2, 4, PADW], F16)
        part = sb("part", [P, 4, GN], F32)
        mom = sb("mom", [P, 2, GN], F32)
        mom_c = sb("mom_c", [1, 2, C], F32)
        mom_t = sb("mom_t", [C, 2], F32)
        qk = sb("qk", [P, 2, 2, 4 * C], F16)
        squares = sb("squares", [P, 2, 4 * C], F32)
        sq_sum = sb("sq_sum", [P, 4 * C], F32)
        gram = sb("gram", [C, 3 * C], F32)
        sc = sb("sc", [C, C], F32)
        small = sb("small", [C, 12], F32)
        probs = sb("probs", [C, C], F32)
        mix = sb("mix", [C, C], F32)
        wf = sb("wf", [CV, KK, C], F32)
        wf_hi = sb("wf_hi", [CV, KK, C], F16)
        wf_lo = sb("wf_lo", [CV, KK, C], F16)
        wfa, wfb = sb("wfa", [P, KK, C], F16), sb("wfb", [P, KK, C], F16)
        wfc = sb("wfc", [XCR, 3, C], F16)
        ps = [psum(f"ps_a{j}_", [P, 512]) for j in range(2)]
        ps_g = [psum(f"ps_g{j}_", [P, 512]) for j in range(2)]
        ps_s = psum("ps_s", [P, 2, GN])
        ps_w = psum("ps_w", [P, 2, 512])
        (stat_ready, stat_summed, stat_rooted, dve_own, padded, ones_made, ones_in, turned, normed, hi_done, lo_done,
         mom_row, mom_col, conv_done, qk_lo, gram_done, gram_out, att, att_pe, att_act, wf_split, wf_in,
         outs, evac, sq_made, sq_added,
         ones_below, wfc_in) = (
            sems[n] for n in ATT_SEMS[:28])
        rows_ready = [sems[f"rows_ready{j}"] for j in range(2)]
        parts_in = [sems[f"parts_in{j}"] for j in range(2)]
        xcol = x[b].rearrange("y x c -> x y c")
        flat = lambda t: t.rearrange("p y x -> p (y x)")
        block = ctx.enter_context(nc.Block())

        @block.sync
        def _(sp):
            def load_rows(u, s, first=False):
                if not first:
                    sp.wait_ge(turned, u - 1)
                sp.dma_start(img[:, bass.ds(u * 4, 4), :], xcol[:, bass.ds(u * 4, 4), :]
                             ).then_inc(rows_ready[s], 16)

            def spread(u, s):
                sp.wait_ge(lo_done, u + 1)
                rows = bass.ds(u * (4 * PADW) + PADW, 4 * PADW)
                lo = lambda c, d: low[32 * c:32 * c + 32, s].rearrange("p y x -> p (y x)")[:, d:4 * PADW]
                sp.dma_start(flat(xb[0:C])[:, rows], flat(xa[0:C])[:, rows]).then_inc(parts_in[s], 16)
                sp.dma_start(flat(xa[C:P])[:, rows], lo(0, 0)).then_inc(parts_in[s], 16)
                sp.dma_start(flat(xb[C:P])[:, rows], lo(1, 0)).then_inc(parts_in[s], 16)
                for dx in range(3):
                    sp.dma_start(flat(xc[32 * dx:32 * dx + 32])[:, bass.ds(u * (4 * PADW) + PADW, 4 * PADW - dx)],
                                 lo(2, dx)).then_inc(parts_in[s], 16)

            load_rows(0, 0, True)
            load_rows(1, 1, True)
            def shift_ones(first, end, sem_):
                for j in range(1, 6):
                    sp.dma_start(flat(xc[C + j:C + j + 1])[:, first:end],
                                 flat(xc[C:C + 1])[:, first + j % 3:end + j % 3]).then_inc(sem_, 16)

            sp.wait_ge(ones_made, 3)
            shift_ones(0, TOP * PADW - 2, ones_in)
            sp.wait_ge(padded, 1)
            for s in range(2):
                load_rows(s + 2, s)
                spread(s, s)
            sp.wait_ge(ones_made, 5)
            shift_ones(TOP * PADW - 2, (H + 2) * PADW - 2, ones_below)
            with sp.Fori(1, UNITS // 2 - 1) as i:
                for s in range(2):
                    load_rows(i * 2 + (s + 2), s)
                    spread(i * 2 + s, s)
            for s in range(2):
                spread(UNITS - 2 + s, s)
            sp.wait_ge(wf_split, 1)
            stack_weights(sp, wf_hi, wf_lo, wfa, wfb, wfc, wf_in, wfc_in)
            for q in range(NQ):
                sp.wait_ge(evac, (q + 1) * (QROWS // 4))
                rows = slice(QROWS * q, QROWS * q + QROWS)
                sp.dma_start(by_planes(x1_dram)[:, rows, :], img[:, rows, :]).then_inc(x1_out, 16)

        @block.gpsimd
        def _(pool):
            nc.gpsimd.memset(low[:].rearrange("p s y x -> p (s y x)").bitcast(U32), 0).then_inc(ones_made, 1)
            pool.wait_ge(ones_made, 1)

            def ones(first, end, made):
                nc.gpsimd.memset(flat(xc[C:CV])[:, first * PADW:end * PADW].bitcast(U32), TWO_ONES
                                 ).then_inc(ones_made, 1)
                pool.wait_ge(ones_made, made + 1)
                border = xc[C:CV, 0, :] if first == 0 else xc[C:CV, H + 1, :]
                nc.gpsimd.memset(border, 0.0)
                rows = slice(max(first, 1), min(end, H + 1))
                for col in (0, W + 1):
                    last = nc.gpsimd.memset(xc[C:CV, rows, col:col + 1], 0.0)
                last.then_inc(ones_made, 1)

            ones(0, TOP, 1)
            pool.wait_ge(ones_made, 3)
            for t, n in ((xa, P), (xb, P), (xc, C)):
                for row in (0, H + 1):
                    last = nc.gpsimd.memset(t[0:n, row, :], 0.0)
            for col in (0, W + 1):
                last = nc.gpsimd.memset(xa[0:C, 1:H + 1, col:col + 1], 0.0)
            nc.gpsimd.memset(sq_sum[:, :], 0.0).then_inc(padded, 1)

            pool.wait_ge(padded, 1)
            ones(TOP, H + 2, 3)

            def add_squares(u, s, first=False):
                pool.wait_ge(sq_made, u + 1)
                if not first:
                    pool.wait_ge(sq_added, u)
                nc.gpsimd.tensor_tensor(sq_sum[:, :], sq_sum[:, :], squares[:, s, :], ALU.add
                                        ).then_inc(sq_added, 1)

            pool.wait_ge(ones_made, 5)
            add_squares(0, 0, True)
            add_squares(1, 1)
            with pool.Fori(1, PAIRS // 2) as i:
                for s in range(2):
                    add_squares(i * 2 + s, s)

        @block.vector
        def _(dve):
            c = Count(dve, dve_own)
            group_stats(nc, dve, c, k["stats"], k["dev"], part, ps_s, mom, stat_ready, stat_summed, stat_rooted)
            c.then_wait(nc.vector.tensor_copy(mom_c[0:1].rearrange("p m (g j) -> p m g j", j=GC),
                                              mom[0:1].unsqueeze(3).to_broadcast([1, 2, GN, GC])))
            dve.sem_inc(mom_row, 1)
            dve.wait_ge(mom_col, 1)
            c.then_wait(nc.vector.tensor_copy(mom_t[:, :], ps[0][0:C, 0:2]))
            dve.wait_ge(ones_made, 1)

            def norm(u, s, first=False):
                dve.wait_ge(turned, u + 1)
                if not first:
                    dve.wait_ge(hi_done, u - 1)
                    dve.wait_ge(lo_done, u - 1)
                nc.vector.tensor_scalar(z[:, s, :], ps_w[0:C, s, :], mom_t[:, 0:1], mom_t[:, 1:2], ALU.subtract,
                                        ALU.mult).then_inc(normed, 1)

            def low_part(u, s, first=False):
                dve.wait_ge(hi_done, u + 1)
                if not first:
                    dve.wait_ge(parts_in[s], (u - s) * (8 * MOVES))
                nc.vector.tensor_tensor(low[:, s, :, 1:W + 1], z[:, s, :].rearrange("p (y x) -> p y x", x=W),
                                        xa[0:C, bass.ds(u * 4 + 1, 4), 1:W + 1], ALU.subtract
                                        ).then_inc(lo_done, 1)

            def qk_low(u, s):
                dve.wait_ge(sq_made, u + 1)
                nc.vector.tensor_tensor(qk[:, s, :, 2 * C:4 * C],
                                        ps[s][:, 0:4 * C].rearrange("p (r o) -> p r o", r=2),
                                        qk[:, s, :, 0:2 * C], ALU.subtract).then_inc(qk_lo, 1)

            norm(0, 0, True)
            norm(1, 1, True)
            low_part(0, 0, True)
            low_part(1, 1, True)
            with dve.Fori(0, UNITS // 2 - 1) as i:
                for s in range(2):
                    norm(i * 2 + (s + 2), s)
                    low_part(i * 2 + (s + 2), s)
                    qk_low(i * 4 + 2 * s, 0)
                    qk_low(i * 4 + (2 * s + 1), 1)
            for u in range(PAIRS - 4, PAIRS):
                qk_low(u, u % 2)

            dve.wait_ge(gram_out, 1)
            g = lambda j: gram[:, j * C:j * C + C]
            c.then_wait(nc.vector.tensor_tensor(sc[:, :], g(0), g(1), ALU.add))
            c.then_wait(nc.vector.tensor_tensor(sc[:, :], sc[:, :], g(2), ALU.add))
            dve.wait_ge(att_act, 1)
            c.then_wait(nc.vector.tensor_scalar(small[:, 2:4], small[:, 2:4], 1e-12 * WSCALE, None, ALU.max))
            c.then_wait(nc.vector.reciprocal(small[:, 4:6], small[:, 2:4]))
            nc.vector.tensor_scalar(sc[:, :], sc[:, :], small[:, 4:5], None, ALU.mult)
            c.then_wait(nc.vector.tensor_tensor(small[:, 6:7], small[:, 5:6], k["temp"][:, :], ALU.mult))
            dve.sem_inc(att, 1)
            dve.wait_ge(att_pe, 1)
            c.then_wait(nc.vector.scalar_tensor_tensor(sc[:, :], ps[0][0:C, 0:C], small[:, 6:7],
                                                       k["same_head"][:, :], ALU.mult, ALU.add))
            c.then_wait(nc.vector.tensor_reduce(small[:, 7:8], sc[:, :], X, ALU.max))
            c.then_wait(nc.vector.tensor_scalar(small[:, 8:9], small[:, 7:8], -1.0, None, ALU.mult))
            dve.sem_inc(att, 1)
            dve.wait_ge(att_act, 2)
            c.then_wait(nc.vector.reciprocal(small[:, 10:11], small[:, 9:10]))
            c.then_wait(nc.vector.tensor_scalar(probs[:, :], probs[:, :], small[:, 10:11], None, ALU.mult))
            dve.sem_inc(att, 1)
            dve.wait_ge(att_act, 4)
            c.then_wait(nc.vector.tensor_tensor(wf[C:CV, 4, :], wf[C:CV, 4, :], k["b_out"][C:CV, :], ALU.add))
            dve.sem_inc(att, 1)
            dve.wait_ge(att_act, 5)
            nc.vector.scalar_tensor_tensor(wf_lo[:], wf[:], WSCALE, wf_hi[:], ALU.mult, ALU.subtract
                                           ).then_inc(wf_split, 1)

            def add_rows(u, s):
                dve.wait_ge(outs, u + 1)
                rows = img[:, bass.ds(u * 4, 4), :]
                nc.vector.scalar_tensor_tensor(rows, ps[s][:, 0:4 * C].rearrange("p (y c) -> p y c", c=C),
                                               1.0 / WSCALE, rows, ALU.mult, ALU.add).then_inc(evac, 1)

            PER = QROWS // 4
            for j in range(PER):
                add_rows(j, j % 2)
            with dve.Fori(1, NQ) as q:
                dve.wait_ge(evac, q * PER)
                for j in range(PER):
                    add_rows(q * PER + j, j % 2)
                    chunk_stats(nc, img, q * QROWS - QROWS, k["stats"], q - 1,
                                range(GN // PER * j, GN // PER * (j + 1)))
            dve.wait_ge(evac, UNITS)
            c.then_wait(chunk_stats(nc, img, H - QROWS, k["stats"], NQ - 1, range(GN)))

        @block.scalar
        def _(act):
            group_stats_root(nc, act, k, ps_s, mom, stat_summed, stat_rooted)

            def high(u, s):
                act.wait_ge(normed, u + 1)
                nc.scalar.activation(xa[0:C, bass.ds(u * 4 + 1, 4), 1:W + 1],
                                     z[:, s, :].rearrange("p (y x) -> p y x", x=W), ACT.Copy).then_inc(hi_done, 1)

            def qk_high(u, s, first=False):
                act.wait_ge(conv_done, u + 1)
                if not first:
                    act.wait_ge(gram_done, u - 1)
                nc.scalar.activation(qk[:, s, :, 0:2 * C], ps[s][:, 0:4 * C].rearrange("p (r o) -> p r o", r=2),
                                     ACT.Copy)
                if not first:
                    act.wait_ge(sq_added, u - 1)
                nc.scalar.activation(squares[:, s, :], ps[s][:, 0:4 * C], ACT.Square).then_inc(sq_made, 1)

            high(0, 0)
            high(1, 1)
            for s in range(2):
                high(s + 2, s)
                qk_high(2 * s, 0, s == 0)
                qk_high(2 * s + 1, 1, s == 0)
            with act.Fori(1, UNITS // 2 - 1) as i:
                for s in range(2):
                    high(i * 2 + (s + 2), s)
                    qk_high(i * 4 + 2 * s, 0)
                    qk_high(i * 4 + (2 * s + 1), 1)
            for u in range(PAIRS - 4, PAIRS):
                qk_high(u, u % 2)

            act.wait_ge(gram_done, PAIRS + 1)
            nc.scalar.activation(gram[:, :], ps_g[0][0:C, 0:3 * C], ACT.Copy).then_inc(gram_out, 1)
            act.wait_ge(gram_done, PAIRS + 2)
            nc.scalar.activation(small[:, 2:4], ps_g[1][0:C, 0:2], ACT.Sqrt, scale=float(P)).then_inc(att_act, 1)
            act.wait_ge(att, 2)
            nc.scalar.activation(probs[:, :], sc[:, :], ACT.Exp, bias=small[:, 8:9],
                                 accum_out=small[:, 9:10]).then_inc(att_act, 1)
            act.wait_ge(att_pe, 2)
            nc.scalar.activation(mix[:, :], ps[1][0:C, 0:C], ACT.Copy).then_inc(att_act, 1)
            act.wait_ge(att_pe, 3)
            nc.scalar.activation(wf[:, 0:5, :], ps_w[0:CV, 0, 0:5 * C].rearrange("p (t o) -> p t o", o=C), ACT.Copy)
            nc.scalar.activation(wf[:, 5:9, :], ps_w[0:CV, 1, 0:4 * C].rearrange("p (t o) -> p t o", o=C),
                                 ACT.Copy).then_inc(att_act, 1)
            act.wait_ge(att, 4)
            nc.scalar.activation(wf_hi[:], wf[:], ACT.Copy, scale=WSCALE).then_inc(att_act, 1)

        @block.tensor
        def _(pe):
            def turn(u, s, first=False):
                pe.wait_ge(rows_ready[s], (u - s) * 8 + 16)
                if not first:
                    pe.wait_ge(normed, u - 1)
                for r in range(4):
                    last = nc.tensor.transpose(ps_w[0:C, s, r * W:r * W + W], img[:, 4 * u + r, :], k["ident"][:, :])
                last.then_inc(turned, 1)

            def conv(bank, y, rows, wa, wb, wc, n, sem_):
                for r in range(rows):
                    out = bank[:, r * n:r * n + n]
                    for t, (dy, dx) in enumerate(TAPS):
                        row = y + r + dy
                        nc.tensor.matmul(out, xa[:, row, dx:dx + W], wa[:, t, :], start=(t == 0), stop=False)
                        nc.tensor.matmul(out, xb[:, row, dx:dx + W], wb[:, t, :], start=False, stop=False)
                    for dy in range(3):
                        last = nc.tensor.matmul(out, xc[:, y + r + dy, 0:W], wc[:, dy, :],
                                                start=False, stop=(dy == 2))
                last.then_inc(sem_, 1)

            def conv_qk(u, s, first=False):
                if not first:
                    pe.wait_ge(qk_lo, u - 1)
                conv(ps[s], u * 2, 2, k["wa"], k["wb"], k["wc"], 2 * C, conv_done)

            def grams(u, s):
                pe.wait_ge(qk_lo, u + 1)
                for r in range(2):
                    q = lambda j: qk[:, s, r, j * C:j * C + C]
                    mm = lambda out, a, c_: nc.tensor.matmul(out, a, c_, start=False, stop=False,
                                                             skip_group_check=True)
                    mm(ps_g[0][0:C, 0:2 * C], q(1), qk[:, s, r, :].rearrange("p (a o) -> p a o", a=2)[:, :, 0:C])
                    last = mm(ps_g[0][0:C, 2 * C:3 * C], q(3), q(0))
                last.then_inc(gram_done, 1)

            def rows_spread(u, s):
                pe.wait_ge(parts_in[s], (u - s) * (8 * MOVES) + 16 * MOVES)

            turn(0, 0, True)
            turn(1, 1, True)
            group_stats_sums(nc, pe, k, part, ps_s, stat_ready, stat_summed)
            pe.wait_ge(mom_row, 1)
            for j in range(2):
                last = nc.tensor.matmul(ps[0][0:C, j:j + 1], mom_c[0:1, j, :], k["ident"][0:1, 0:1], start=True,
                                        stop=True)
            last.then_inc(mom_col, 1)
            nc.tensor.matmul(ps_g[0][0:C, 0:3 * C], k["zeros"][:, 0:C], k["zeros"][:, 0:3 * C], start=True,
                             stop=False, skip_group_check=True)
            turn(2, 0)
            pe.wait_ge(padded, 1)
            pe.wait_ge(ones_in, 16 * 5)
            rows_spread(0, 0)
            conv_qk(0, 0, True)
            rows_spread(1, 1)
            conv_qk(1, 1, True)
            grams(0, 0)
            turn(3, 1)
            conv_qk(2, 0)
            grams(1, 1)
            rows_spread(2, 0)
            conv_qk(3, 1)
            grams(2, 0)
            pe.wait_ge(ones_below, 16 * 5)
            for i in range(1, UNITS // 2 - 1):
                for s in range(2):
                    turn(i * 2 + (s + 2), s)
                    conv_qk(i * 4 + 2 * s, 0)
                    grams(i * 4 + (2 * s - 1), 1)
                    rows_spread(i * 2 + (s + 1), 1 - s)
                    conv_qk(i * 4 + (2 * s + 1), 1)
                    grams(i * 4 + 2 * s, 0)
            for u in range(PAIRS - 4, PAIRS):
                if u == PAIRS - 3:
                    rows_spread(UNITS - 1, 1)
                conv_qk(u, u % 2)
                grams(u - 1, (u - 1) % 2)
            grams(PAIRS - 1, 1)
            nc.tensor.matmul(ps_g[0][0:C, 0:3 * C], k["zeros"][:, 0:C], k["zeros"][:, 0:3 * C], start=False,
                             stop=True, skip_group_check=True).then_inc(gram_done, 1)
            pe.wait_ge(sq_added, PAIRS)
            for j, of in ((0, 1), (1, 0)):
                for r in range(2):
                    last = nc.tensor.matmul(ps_g[1][0:C, j:j + 1], sq_sum[:, (2 * r + of) * C:(2 * r + of + 1) * C],
                                            k["mean_ones"][:, 0:1], start=(r == 0), stop=(r == 1))
            last.then_inc(gram_done, 1)

            pe.wait_ge(att, 1)
            nc.tensor.transpose(ps[0][0:C, 0:C], sc[:, :], k["ident"][0:C, 0:C]).then_inc(att_pe, 1)
            pe.wait_ge(att, 3)
            nc.tensor.matmul(ps[1][0:C, 0:C], probs[:, :], k["w_out"][:, :], start=True, stop=True
                             ).then_inc(att_pe, 1)
            pe.wait_ge(att_act, 3)
            for t in range(KK):
                last = nc.tensor.matmul(ps_w[0:CV, t // 5, (t % 5) * C:(t % 5) * C + C], k["wv_t"][:, t, :],
                                        mix[:, :], start=True, stop=True)
            last.then_inc(att_pe, 1)

            def conv_out(u, s, first=False):
                if not first:
                    pe.wait_ge(evac, u - 1)
                conv(ps[s], u * 4, 4, wfa, wfb, wfc, C, outs)

            nc.tensor.matmul(ps[0][:, 0:4 * C], k["zeros"][:, 0:P], k["zeros"][:, 0:4 * C], start=True, stop=False,
                             skip_group_check=True)
            pe.wait_ge(wf_in, 16 * STACKS)
            mm = lambda r, a, w: nc.tensor.matmul(ps[0][:, r * C:r * C + C], a, w, start=False, stop=False,
                                                  skip_group_check=True)
            for r in range(4):
                for t, (dy, dx) in enumerate(TAPS):
                    mm(r, xa[:, r + dy, dx:dx + W], wfa[:, t, :])
                    mm(r, xb[:, r + dy, dx:dx + W], wfb[:, t, :])
            pe.wait_ge(wfc_in, 16 * STACKS_C)
            for r in range(4):
                for dy in range(3):
                    mm(r, xc[:, r + dy, 0:W], wfc[:, dy, :])
            nc.tensor.matmul(ps[0][:, 0:4 * C], k["zeros"][:, 0:P], k["zeros"][:, 0:4 * C], start=False, stop=True,
                             skip_group_check=True).then_inc(outs, 1)
            conv_out(1, 1, True)
            for u in range(2, UNITS):
                conv_out(u, u % 2)


def motif_grams(nc, b, k, img, f_dram, x1_out, att_sems):
    with ExitStack() as ctx:
        sb = lambda n, s, d: ctx.enter_context(nc.sbuf_tensor(f"{n}{b}", s, d))
        psum = lambda n, s: ctx.enter_context(nc.psum_tensor(f"{n}{b}", s, F32))
        sem = lambda n: ctx.enter_context(nc.semaphore(f"{n}{b}"))
        f = sb("f", [P, H, C], F32)
        stage = [sb(f"stage{s}_", [P, 3, MC, C], F32) for s in range(2)]
        patches = [sb(f"patches{s}_", [P, 2, C * 3 * MC], F16) for s in range(2)]
        part = sb("m_part", [P, 4, GN], F32)
        mom = sb("m_mom", [P, 2, GN], F32)
        half = sb("half", [MR, 2, MR], F32)
        g_half = sb("g_half", [MR, MG, MR], F32)
        g_turn = sb("g_turn", [MR, MG, MR], F32)
        g_all = sb("g_all", [MR, MG, MR], F32)
        blk = sb("blk", [MR, MG, MC], F32)
        tmp = sb("tmp", [MR, MG, MC], F32)
        d2 = sb("d2", [MR, MG, MC], F32)
        sqc = sb("sqc", [MR, MG], F32)
        mn = sb("mn", [MR, MG], F32)
        nnt = sb("nnt", [MG, MR], F32)
        eq2 = sb("eq2", [MG, MR], F32)
        sel = sb("sel", [MG, 6, KK], F32)
        block_picks = sb("block_picks", [MG, 3, KK], F32)
        both = sb("both", [P, 2, 3, KK], F32)
        ps_a = [psum(f"ps_ga{j}_", [P, 512]) for j in range(2)]
        ps_t = [psum(f"ps_gt{j}_", [P, 512]) for j in range(3)]
        ps_s = psum("ps_gs", [P, 2, GN])
        (ready, summed, rooted, own, sub_done, f_done, hi_done, lo_done, f_out, main_done, half_done,
         a_done, post_pe, post_act, picks, picks_spread, pick_pe) = (
            sem(n) for n in ("m_ready", "m_summed", "m_rooted", "m_dve", "m_sub", "m_f", "m_hi", "m_lo", 
                             "f_out", "main_done", "half_done", "a_done", "post_pe", "post_act", "picks",
                             "picks_spread", "pick_pe"))
        stage_in = [sem(f"stage_in{s}_") for s in range(2)]
        PER = 6
        PIECES = (MC, MC, 2 * MC, 4 * MC, 4 * MC, 4 * MC)
        starts = [sum(PIECES[:j]) for j in range(len(PIECES))]
        ON_DVE = 2
        by_shift = lambda t, part_: t[0:HM, part_].rearrange("p (w k c) -> p k c w", k=3, c=MC)
        block = ctx.enter_context(nc.Block())

        @block.sync
        def _(sp):
            if b + 1 < B:
                for s_ in att_sems.values():
                    sp.sem_clear(s_)

            def load(g, s, first=False):
                if not first:
                    sp.wait_ge(lo_done, g - 1)
                for ki in range(3):
                    sp.dma_start(stage[s][0:HM, ki], f[ki:ki + HM, bass.ds(g * MC, MC), :]
                                 ).then_inc(stage_in[s], 16)

            for j in range(4):
                sp.wait_ge(f_done, min(j, 2) + 1)
                load(j, j % 2, j < 2)
            with sp.Fori(1, MG // 4) as q:
                sp.wait_ge(f_done, q + 3)
                for j in range(4):
                    load(q * 4 + j, j % 2)
            sp.wait_ge(x1_out, 16 * NQ)
            sp.wait_ge(f_out, 16 * MG)

        @block.gpsimd
        def _(pool):
            pool.wait_ge(f_done, ON_DVE)
            for j in range(ON_DVE, len(PIECES)):
                pool.wait_ge(sub_done, j + 1)
                fg = f[:, starts[j]:starts[j] + PIECES[j], :].rearrange("p y (g j) -> p y g j", j=GC)
                nc.gpsimd.tensor_tensor(fg, fg, mom[:, 1, :].unsqueeze(1).unsqueeze(3)
                                        .to_broadcast([P, PIECES[j], GN, GC]), ALU.mult).then_inc(f_done, 1)

        @block.scalar
        def _(act):
            group_stats_root(nc, act, k, ps_s, mom, summed, rooted)

            def high(i, s, first):
                act.wait_ge(stage_in[s], i * 48 + 48)
                if not first:
                    act.wait_ge(main_done, i * 2 + (s - 1))
                nc.scalar.activation(by_shift(patches[s], 0), stage[s][0:HM], ACT.Copy).then_inc(hi_done, 1)

            def halve(i, s, first):
                act.wait_ge(main_done, i * 2 + (s + 1))
                if not first:
                    act.wait_ge(a_done, i * 2 + (s - 1))
                nc.scalar.activation(half[:, s, :], ps_a[s][0:MR, 0:MR], ACT.Copy, scale=0.5).then_inc(half_done, 1)

            def store(g):
                planes = bass.ds(g * MC, MC)
                act.dma_start(by_planes(f_dram)[:, planes, :], f[:, planes, :]).then_inc(f_out, 16)

            for s in range(2):
                high(0, s, True)
            for s in range(2):
                halve(0, s, True)
                high(1, s, False)
            with act.Fori(1, MG // 2 - 1) as i:
                for s in range(2):
                    halve(i, s, False)
                    high(i + 1, s, False)
                    store(i * 2 - 2 + s)
            for g in range(MG - 4, MG):
                store(g)
            for s in range(2):
                halve(MG // 2 - 1, s, False)
            for step, dst in enumerate((g_turn, g_all)):
                for j in range(3):
                    n = min(PER, MG - PER * j)
                    act.wait_ge(post_pe, 3 * step + j + 1)
                    nc.scalar.activation(dst[:, PER * j:PER * j + n, :],
                                         ps_t[j][0:MR, 0:n * MR].rearrange("p (g r) -> p g r", r=MR),
                                         ACT.Copy).then_inc(post_act, 1)

        @block.tensor
        def _(pe):
            group_stats_sums(nc, pe, k, part, ps_s, ready, summed)

            def grams(i, s, first):
                pe.wait_ge(lo_done, i * 2 + (s + 1))
                if not first:
                    pe.wait_ge(a_done, i * 2 + (s - 1))
                for w in range(WM):
                    cols = slice(3 * MC * w, 3 * MC * w + MR)
                    last = nc.tensor.matmul(ps_a[s][0:MR, 0:2 * MR], patches[s][0:HM, 0, cols],
                                            patches[s][0:HM, :, cols], start=(w == 0), stop=(w == WM - 1))
                last.then_inc(main_done, 1)

            grams(0, 0, True)
            grams(0, 1, True)
            with pe.Fori(1, MG // 2) as i:
                grams(i, 0, False)
                grams(i, 1, False)
            pe.wait_ge(a_done, MG)
            for g in range(MG):
                last = nc.tensor.matmul(ps_t[g // PER][0:MR, (g % PER) * MR:(g % PER) * MR + MR], g_half[:, g, :],
                                        k["order"][:, :], start=True, stop=True)
                if g % PER == PER - 1 or g == MG - 1:
                    last.then_inc(post_pe, 1)
            for g in range(MG):
                if g % PER == 0:
                    pe.wait_ge(post_act, g // PER + 1)
                out = ps_t[g // PER][0:MR, (g % PER) * MR:(g % PER) * MR + MR]
                nc.tensor.matmul(out, g_turn[:, g, :], k["order"][:, :], start=True, stop=False)
                last = nc.tensor.matmul(out, k["order"][:, :], g_turn[:, g, :], start=False, stop=True)
                if g % PER == PER - 1 or g == MG - 1:
                    last.then_inc(post_pe, 1)
            pe.wait_ge(pick_pe, 1)
            nc.tensor.matmul(ps_a[0][0:MR, 0:MG * MC], k["same_block"][:, :],
                             tmp[:].rearrange("p g d -> p (g d)"), start=True, stop=True).then_inc(post_pe, 1)
            pe.wait_ge(pick_pe, 2)
            nc.tensor.transpose(ps_a[1][0:MG, 0:MR], mn[:, :], k["ident"][0:MR, 0:MR]).then_inc(post_pe, 1)
            pe.wait_ge(picks, 1)
            nc.tensor.matmul(ps_s[:].rearrange("p a g -> p (a g)")[:, 0:3 * KK], k["group_planes"][:, :],
                             block_picks[:].rearrange("g v j -> g (v j)"), start=True, stop=True
                             ).then_inc(picks_spread, 1)

        @block.vector
        def _(dve):
            c = Count(dve, own)
            group_stats(nc, dve, c, k["stats"], k["dev"], part, ps_s, mom, ready, summed, rooted)
            def center(j):
                planes = slice(starts[j], starts[j] + PIECES[j])
                fg = f[:, planes, :].rearrange("p y (g j) -> p y g j", j=GC)
                moment = lambda m: mom[:, m, :].unsqueeze(1).unsqueeze(3).to_broadcast([P, PIECES[j], GN, GC])
                nc.vector.tensor_tensor(fg, img[:, planes, :].rearrange("p y (g j) -> p y g j", j=GC), moment(0),
                                        ALU.subtract).then_inc(sub_done, 1)
                if j < ON_DVE:
                    dve.wait_ge(sub_done, j + 1)
                    nc.vector.tensor_tensor(fg, fg, moment(1), ALU.mult).then_inc(f_done, 1)

            def low(i, s):
                dve.wait_ge(hi_done, i * 2 + (s + 1))
                nc.vector.tensor_tensor(by_shift(patches[s], 1), stage[s][0:HM], by_shift(patches[s], 0),
                                        ALU.subtract).then_inc(lo_done, 1)

            def half_gram(i, s):
                dve.wait_ge(half_done, i * 2 + (s + 1))
                nc.vector.tensor_tensor(g_half[:, bass.ds(i * 2 + s, 1), :],
                                        ps_a[s][0:MR, MR:2 * MR].unsqueeze(1), half[:, s, :].unsqueeze(1),
                                        ALU.add).then_inc(a_done, 1)

            for j in range(4):
                center(j)
            low(0, 0)
            low(0, 1)
            for s in range(2):
                half_gram(0, s)
                low(1, s)
                center(4 + s)
            with dve.Fori(1, MG // 2 - 1) as i:
                for s in range(2):
                    half_gram(i, s)
                    low(i + 1, s)
            for s in range(2):
                half_gram(MG // 2 - 1, s)

            dve.wait_ge(post_act, 6)
            c.then_wait(nc.vector.tensor_tensor(g_all[:], g_all[:], k["same_block"][:, :].unsqueeze(1)
                                                .to_broadcast([MR, MG, MR]), ALU.mult))
            c.then_wait(nc.vector.tensor_reduce(blk[:], g_all[:].rearrange("p g (j d) -> p g d j", d=MC), X,
                                                ALU.add))
            own8 = k["own"][:, :].unsqueeze(1).to_broadcast([MR, MG, MC])
            iota8 = k["iota"][0:MR, 0:MC].unsqueeze(1).to_broadcast([MR, MG, MC])
            c.then_wait(nc.vector.tensor_tensor(tmp[:], blk[:], own8, ALU.mult))
            c.then_wait(nc.vector.tensor_reduce(sqc[:, :], tmp[:], X, ALU.add))
            dve.sem_inc(pick_pe, 1)
            dve.wait_ge(post_pe, 7)
            c.then_wait(nc.vector.tensor_tensor(d2[:], ps_a[0][0:MR, 0:MG * MC].rearrange("p (g d) -> p g d", d=MC),
                                                sqc[:, :].unsqueeze(2).to_broadcast([MR, MG, MC]), ALU.add))
            c.then_wait(nc.vector.scalar_tensor_tensor(d2[:], blk[:], -2.0, d2[:], ALU.mult, ALU.add))
            c.then_wait(nc.vector.tensor_scalar(tmp[:], own8, BIG, None, ALU.mult))
            c.then_wait(nc.vector.tensor_tensor(d2[:], d2[:], tmp[:], ALU.add))
            c.then_wait(nc.vector.tensor_reduce(mn[:, :], d2[:], X, ALU.min))
            c.then_wait(nc.vector.tensor_tensor(d2[:], d2[:], mn[:, :].unsqueeze(2).to_broadcast([MR, MG, MC]),
                                                ALU.is_equal))
            c.then_wait(nc.vector.tensor_scalar(tmp[:], iota8, -float(MC), None, ALU.add))
            c.then_wait(nc.vector.tensor_tensor(tmp[:], tmp[:], d2[:], ALU.mult))
            c.then_wait(nc.vector.tensor_reduce(mn[:, :], tmp[:], X, ALU.min))
            c.then_wait(nc.vector.tensor_scalar(mn[:, :], mn[:, :], float(MC), None, ALU.add))
            dve.sem_inc(pick_pe, 1)
            dve.wait_ge(post_pe, 8)
            c.then_wait(nc.vector.tensor_copy(nnt[:, :], ps_a[1][0:MG, 0:MR]))
            u, ge, ku, kui, t1, t2 = (sel[:, j, :] for j in range(6))
            cu, in_plane, cm = (block_picks[:, j, :] for j in range(3))
            jj = k["iota"][0:MG, 0:KK]
            c.then_wait(nc.vector.tensor_reduce(u, nnt[:, :].rearrange("p (j d) -> p j d", d=MC), X, ALU.max))
            c.then_wait(nc.vector.tensor_tensor(eq2[:, :].rearrange("p (j d) -> p j d", d=MC),
                                                nnt[:, :].rearrange("p (j d) -> p j d", d=MC),
                                                u.unsqueeze(2).to_broadcast([MG, KK, MC]), ALU.is_equal))
            c.then_wait(nc.vector.tensor_reduce(cm, eq2[:, :].rearrange("p (j d) -> p j d", d=MC), X, ALU.add))
            nc.vector.tensor_scalar(cm, cm, 1.0 / MC, None, ALU.mult)
            c.then_wait(nc.vector.tensor_tensor(t1, u, jj, ALU.subtract))
            c.then_wait(nc.vector.tensor_scalar(ge, t1, 0.0, None, ALU.is_ge))
            c.then_wait(nc.vector.tensor_scalar(t1, t1, float(KK), None, ALU.add))
            c.then_wait(nc.vector.scalar_tensor_tensor(ku, ge, -float(KK), t1, ALU.mult, ALU.add))
            c.then_wait(nc.vector.scalar_tensor_tensor(cu, ge, -1.0, jj, ALU.add, ALU.add))
            c.then_wait(nc.vector.tensor_scalar(t1, ku, 3.0, None, ALU.is_ge))
            c.then_wait(nc.vector.tensor_scalar(t2, ku, 6.0, None, ALU.is_ge))
            c.then_wait(nc.vector.tensor_tensor(kui, t1, t2, ALU.add))
            c.then_wait(nc.vector.scalar_tensor_tensor(in_plane, kui, float(C - 3), ku, ALU.mult, ALU.add))
            dve.sem_inc(picks, 1)
            dve.wait_ge(picks_spread, 1)
            c.then_wait(nc.vector.tensor_tensor(
                both[:], ps_s[:].rearrange("p a g -> p (a g)")[:, 0:3 * KK].rearrange("p (v j) -> p v j", j=KK)
                .unsqueeze(1).to_broadcast([P, 2, 3, KK]),
                k["own_block"][:].unsqueeze(2).to_broadcast([P, 2, 3, KK]), ALU.mult))
            c.then_wait(nc.vector.tensor_reduce(k["pick"][:], both[:], X, ALU.add))


def motif_terms(nc, b, k, x, f_dram, x1_dram, out):
    R = 16
    N = H // R
    SLOTS = 4
    NR = R + 2
    BR = 4
    PRODS, RNDS = 4, 3
    with ExitStack() as ctx:
        sb = lambda n, s, d: ctx.enter_context(nc.sbuf_tensor(f"{n}{b}", s, d))
        sem = lambda n: ctx.enter_context(nc.semaphore(f"{n}{b}"))
        near = sb("near", [P, SLOTS, NR * C], F32)
        near2 = sb("near2", [P, SLOTS, NR * C], F32)
        fc = sb("fc", [P, SLOTS, R * C], F32)
        x1c = sb("x1c", [P, SLOTS, R * C], F32)
        prod = sb("prod", [P, PRODS, R, WM], F32)
        rnd_m = sb("rnd_m", [P, 2, R, WM], F32)
        rnd = sb("rnd", [P, RNDS, R, WM], F32)
        over = sb("over", [P, 2, R, WM], BF16)
        if b + 1 < B:
            x_next = sb("x_next", [P, 2 * QROWS, C], F32)
            next_in = [sem(f"next_in{j}_") for j in range(2)]
            next_stats = sem("next_stats")
        offset = sb("offset", [P, 2], F32)
        scale = sb("scale", [P, KK], F32)
        index_f = sb("index_f", [P, 2, N], F32)
        index = sb("index", [P, 2, N], I32)
        acc = [ctx.enter_context(nc.psum_tensor(f"acc{s}_{b}", [P, R // BR, 512], F32)) for s in range(2)]
        (own, scaled, indexed, edged, prod_v, prod_p, rm_done, rnd_done, over_done, acc_done, out_ready,
         fold) = (
            sem(n) for n in ("t_dve", "scaled", "indexed", "edged", "prod_v", "prod_p", "rm_done",
                             "rnd_done", "over_done", "acc_done", "out_ready", "fold"))
        stored, near_in, near2_in, fc_in, x1_in = ([sem(f"{n}{j}_") for j in range(SLOTS)]
                                                   for n in ("stored", "near_in", "near2_in", "fc_in", "x1_in"))
        moved = [sem(f"moved{s}_") for s in range(2)]
        steps = [(2 * m + s, sh) for m in range(N // 2) for sh in range(KK) for s in range(2)]
        number = {st: n for n, st in enumerate(steps)}
        on_pool = [i % 2 == 1 for i, sh in steps]
        STATS_PER, STATS_AT, LOAD_AT = 13, 19, 7
        after = {i: number[(i, KK - 1)] + 1 for i in range(N)}
        first_row = lambda i: max(R * i - 2, 0)
        last_row = lambda i: min(R * i + R - 1, HM - 1)

        def product_made(eng, n):
            eng.wait_ge(prod_p if on_pool[n] else prod_v, sum(p == on_pool[n] for p in on_pool[:n + 1]))

        def product_inputs(eng, n):
            i, sh = steps[n]
            s = i % SLOTS
            if sh == 0:
                eng.wait_ge(near_in[s], 16 * (i // SLOTS + 1))
                eng.wait_ge(fc_in[s], 16 * (i // SLOTS + 1))
                eng.wait_ge(edged, 2 if i == N - 1 else 1)
            else:
                eng.wait_ge(moved[i % 2], 16 * (8 * (i // 2) + sh))
            if n >= PRODS:
                eng.wait_ge(over_done, n - PRODS + 1)

        def product(vec, n):
            i, sh = steps[n]
            s, (dy, dx) = i % SLOTS, TAPS[sh]
            fv = fc[:, s, :].rearrange("p (r c) -> p r c", c=C)[:, :, dx:dx + WM]
            nv = near[:, s, :].rearrange("p (r c) -> p r c", c=C)[:, 2 - dy:2 - dy + R, 0:WM]
            return vec.tensor_tensor(prod[:, n % PRODS], fv, nv, ALU.mult)

        def run(i):
            a = (first_row(i) - (R * i - 2)) * C
            return slice(a, a + (last_row(i) - first_row(i)) * C + WM)

        out_p = out[b].rearrange("y x c -> y (x c)")
        block = ctx.enter_context(nc.Block())

        @block.sync
        def _(sp):
            def load_rows(dst, src, i, sem_):
                sp.dma_start(dst[:, i % SLOTS, :], src[:, R * i * C:(R * i + R) * C]).then_inc(sem_[i % SLOTS], 16)

            def load_next(q, piece):
                cols, slot = QROWS // 4, QROWS * (q % 2)
                if q >= 2 and piece == 0:
                    sp.wait_ge(next_stats, q - 1)
                sp.dma_start(x_next[:, slot + cols * piece:slot + cols * (piece + 1), :],
                             x[b + 1][:, QROWS * q + cols * piece:QROWS * q + cols * (piece + 1), :]
                             ).then_inc(next_in[q % 2], 16)

            def store(i):
                sp.wait_ge(out_ready, i + 1)
                sp.dma_start(out_p[:, R * i * C:(R * i + R) * C], x1c[:, i % SLOTS, :]
                             ).then_inc(stored[i % SLOTS], 16)

            for i in range(2):
                load_rows(fc, f_dram, i, fc_in)
            for n, (i, sh) in enumerate(steps):
                if sh >= 1:
                    if sh == 1:
                        sp.wait_ge(near2_in[i % SLOTS], 16 * (i // SLOTS + 1))
                    product_made(sp, n - 2)
                    sp.dma_start(near[MC - sh:P:MC, i % SLOTS, run(i)], near2[MC - sh:P:MC, i % SLOTS, run(i)]
                                 ).then_inc(moved[i % 2], 16)
                if sh == 5 and i + 2 < N:
                    if i >= 2:
                        product_made(sp, number[(i - 2, KK - 1)])
                        product_made(sp, number[(i - 2, KK - 2)])
                        if b == 1:
                            sp.wait_ge(fold, i - 1)
                    load_rows(fc, f_dram, i + 2, fc_in)
                if i >= 2 and sh == 2:
                    store(i - 2)
                if sh == 1 and i < 2:
                    load_rows(x1c, x1_dram, i, x1_in)
                q, part = (n - LOAD_AT) // STATS_PER, (n - LOAD_AT) % STATS_PER
                if b + 1 < B and 0 <= q < NQ and part in (0, 3, 6, 9):
                    load_next(q, part // 3)
                if sh == 4 and i + 2 < N:
                    if i >= 2:
                        sp.wait_ge(stored[(i + 2) % SLOTS], 16 * ((i + 2) // SLOTS))
                    load_rows(x1c, x1_dram, i + 2, x1_in)
            for i in range(N - 2, N):
                store(i)
            for j in range(SLOTS):
                sp.wait_ge(stored[j], 16 * (N // SLOTS))

        @block.gpsimd
        def _(pool):
            def gather(i, second):
                s = i % SLOTS
                pool.indirect_dma_start(
                    (near2 if second else near)[:, s, run(i)], None, f_dram.rearrange("y (e o) -> (y e) o", o=1),
                    bass.IndirectOffsetOnAxis(ap=index[:, second, i:i + 1], axis=0)
                ).then_inc((near2_in if second else near_in)[s], 16)

            nc.gpsimd.memset(near[:, 0, 0:2 * C], 0.0).then_inc(edged, 1)
            pool.wait_ge(indexed, 1)
            for second in range(2):
                gather(0, second)
                gather(1, second)
            for n, (i, sh) in enumerate(steps):
                if sh in (1, 3) and i + 2 < N:
                    if sh == 1 and i >= 2:
                        product_made(pool, number[(i - 2, KK - 1)])
                        product_made(pool, number[(i - 2, KK - 2)])
                    if sh == 1 and i + 2 == N - 1:
                        nc.gpsimd.memset(near[:, (i + 2) % SLOTS, R * C:NR * C], 0.0).then_inc(edged, 1)
                    gather(i + 2, sh // 2)
                if on_pool[n]:
                    product_inputs(pool, n)
                    product(nc.gpsimd, n).then_inc(prod_p, 1)

        @block.vector
        def _(dve):
            c = Count(dve, own)
            pick = k["pick"]
            c.then_wait(nc.vector.scalar_tensor_tensor(offset[:, :], pick[:, :, 0], float(PLANE), pick[:, :, 1],
                                                       ALU.mult, ALU.add))
            for i in range(N):
                last = nc.vector.tensor_scalar(index_f[:, :, i], offset[:, :], k["group_base"][:, 0:1],
                                               float(first_row(i) * C), ALU.add, ALU.add)
            c.then_wait(last)
            nc.vector.tensor_copy(index[:], index_f[:]).then_inc(indexed, 1)
            c.then_wait(nc.vector.tensor_scalar(scale[:, :], k["second_block"][:, :], pick[:, 1, 2:3], None,
                                                ALU.mult))
            nc.vector.scalar_tensor_tensor(scale[:, :], k["first_part"][:, :], pick[:, 0, 2:3], scale[:, :],
                                           ALU.mult, ALU.add).then_inc(scaled, 1)
            dve.wait_ge(scaled, 1)

            def overshoot(n):
                sh = steps[n][1]
                dve.wait_ge(rnd_done, n + 1)
                if n >= 2:
                    dve.wait_ge(acc_done, n - 1)
                nc.vector.scalar_tensor_tensor(over[:, n % 2], prod[:, n % PRODS], scale[:, sh:sh + 1],
                                               rnd[:, n % RNDS], ALU.mult, ALU.is_lt).then_inc(over_done, 1)

            def finish(i):
                dve.wait_ge(acc_done, after[i])
                dve.wait_ge(x1_in[i % SLOTS], 16 * (i // SLOTS + 1))
                if b == 1:
                    dve.wait_ge(fold, i + 1)
                v = x1c[:, i % SLOTS, :].rearrange("p (m c) -> p m c", c=BR * C)
                nc.vector.tensor_tensor(v, v, acc[i % 2][:, :, 0:BR * C], ALU.add).then_inc(out_ready, 1)

            def own_patches(i):
                s = i % SLOTS
                dve.wait_ge(fc_in[s], 16 * (i // SLOTS + 1))
                dve.wait_ge(x1_in[s], 16 * (i // SLOTS + 1))
                fv = fc[:, s, :].rearrange("p (r c) -> p r c", c=C)
                xv = x1c[:, s, :].rearrange("p (r c) -> p r c", c=C)
                top, end = (2 if i == 0 else 0), (R - 2 if i == N - 1 else R)
                rows = [(slice(top, end), 3.0)]
                rows += [(slice(r, r + 1), r + 1.0) for r in range(top)]
                rows += [(slice(r, r + 1), float(R - r)) for r in range(end, R)]
                for r, in_rows in rows:
                    for cols, in_cols in ((slice(2, C - 2), 3.0), (slice(0, C, C - 1), 1.0),
                                          (slice(1, C - 1, C - 3), 2.0)):
                        last = nc.vector.scalar_tensor_tensor(xv[:, r, cols], fv[:, r, cols], in_rows * in_cols,
                                                              xv[:, r, cols], ALU.mult, ALU.add)
                last.then_inc(fold, 1)

            def stats_share(n):
                q, part = (n - STATS_AT) // STATS_PER, (n - STATS_AT) % STATS_PER
                if 0 <= q < NQ:
                    if part == 0:
                        dve.wait_ge(next_in[q % 2], 64 * (q // 2 + 1))
                    groups = range(GN * part // STATS_PER, GN * (part + 1) // STATS_PER)
                    last = chunk_stats(nc, x_next, QROWS * (q % 2), k["stats"], q, groups)
                    if part == STATS_PER - 1:
                        last.then_inc(next_stats, 1)

            LAG = 2
            for n in range(len(steps) + LAG):
                if n < len(steps) and not on_pool[n]:
                    product_inputs(dve, n)
                    product(nc.vector, n).then_inc(prod_v, 1)
                if n >= LAG:
                    overshoot(n - LAG)
                    i, sh = steps[n - LAG]
                    if i >= 2 and sh == 0:
                        finish(i - 2)
                    if b == 1 and sh == 3:
                        own_patches(i)
                if b + 1 < B and n < len(steps):
                    stats_share(n)
            finish(N - 2)
            finish(N - 1)
            if b + 1 < B:
                dve.wait_ge(next_stats, NQ)

        @block.scalar
        def _(act):
            act.wait_ge(scaled, 1)
            for n, (i, sh) in enumerate(steps):
                product_made(act, n)
                if n >= 2:
                    act.wait_ge(rnd_done, n - 1)
                nc.scalar.activation(rnd_m[:, n % 2], prod[:, n % PRODS], ACT.Identity,
                                     bias=k["plus_round"][:, 0:1], scale=scale[:, sh:sh + 1]).then_inc(rm_done, 1)
                act.wait_ge(rm_done, n + 1)
                if n >= RNDS:
                    act.wait_ge(acc_done, n - RNDS + 1)
                nc.scalar.activation(rnd[:, n % RNDS], rnd_m[:, n % 2], ACT.Identity,
                                     bias=k["minus_round"][:, 0:1]).then_inc(rnd_done, 1)

        @block.tensor
        def _(pe):
            for n, (i, sh) in enumerate(steps):
                dx = TAPS[sh][1]
                bank = acc[i % 2]
                if sh == 0:
                    if i >= 2:
                        pe.wait_ge(out_ready, i - 1)
                    for m in range(R // BR):
                        nc.tensor.matmul(bank[:, m, 0:BR * C], k["zeros"][:, 0:P], k["zeros"][:, 0:BR * C],
                                         start=True, stop=False, skip_group_check=True)
                o = lambda m: bank[:, m, 0:BR * C].rearrange("p (r c) -> p r c", c=C)[:, :, dx:dx + WM]
                pe.wait_ge(rnd_done, n + 1)
                for m in range(R // BR):
                    nc.tensor.matmul(o(m), k["ident"][:, :], rnd[:, n % RNDS, BR * m:BR * m + BR, :], start=False,
                                     stop=False, skip_group_check=True)
                pe.wait_ge(over_done, n + 1)
                for m in range(R // BR):
                    last = nc.tensor.matmul(o(m), k["minus_ident"][:, :], over[:, n % 2, BR * m:BR * m + BR, :],
                                            start=False, stop=(sh == KK - 1), skip_group_check=True)
                last.then_inc(acc_done, 1)


def build(nc, x, w_qkv, b_qkv, w_dw, b_dw, temperature, w_out, b_out, out):
    f_dram = [nc.dram_tensor(f"f_planes{b}", (H, PLANE), F32).ap() for b in range(B)]
    x1_dram = [nc.dram_tensor(f"x1_planes{b}", (H, PLANE), F32).ap() for b in range(B)]
    ins = dict(w_qkv=w_qkv, b_qkv=b_qkv, w_dw=w_dw, b_dw=b_dw, temperature=temperature, w_out=w_out, b_out=b_out)
    with ExitStack() as ctx:
        sb = lambda n, s, d: ctx.enter_context(nc.sbuf_tensor(n, s, d))
        k = dict(
            ident=sb("ident", [P, P], F32), minus_ident=sb("minus_ident", [P, P], BF16),
            zeros=sb("zeros_k", [P, 4 * C], BF16), mean_ones=sb("mean_ones", [P, P], F32),
            eps=sb("eps", [P, 1], F32), plus_round=sb("plus_round", [P, 1], F32),
            minus_round=sb("minus_round", [P, 1], F32), group_planes=sb("group_planes", [MG, P], F32),
            own_block=sb("own_block", [P, 2, KK], F32), pick=sb("pick", [P, 2, 3], F32),
            same_head=sb("same_head", [C, C], F32), same_block=sb("same_block", [MR, MR], F32),
            order=sb("order", [MR, MR], F32), own=sb("own8", [MR, MC], F32), iota=sb("iota", [P, 32], F32),
            group_base=sb("group_base", [P, 1], F32), plane_f=sb("plane_f", [P, 1], F32),
            second_block=sb("second_block", [P, KK], F32), first_part=sb("first_part", [P, KK], F32),
            temp=sb("temp", [C, 1], F32), w_out=sb("w_out_s", [C, C], F32), b_out=sb("b_out_s", [CV, C], F32),
            wa=sb("wa", [P, KK, 2 * C], F16), wb=sb("wb", [P, KK, 2 * C], F16), wc=sb("wc", [XCR, 3, 2 * C], F16),
            stats=sb("stats", [P, GN, NQ, 6], F32), dev=sb("dev", [P, GN, 2 * NQ], F32),
            wv_t=sb("wv_t", [C, KK, CV], F32),
        )
        x1_out = [ctx.enter_context(nc.semaphore(f"x1_out{b}")) for b in range(B)]
        att_sems = {n: ctx.enter_context(nc.semaphore(n)) for n in ATT_SEMS}
        prepare(nc, k, ins, x)
        for b in range(B):
            with nc.sbuf_tensor(f"img{b}", [P, H, C], F32) as img:
                attention(nc, b, k, x, img, x1_dram[b], x1_out[b], att_sems)
                motif_grams(nc, b, k, img, f_dram[b], x1_out[b], att_sems)
            motif_terms(nc, b, k, x, f_dram[b], x1_dram[b], out)


_INS = ["x", "L0_conv_w_qkv", "L0_conv_b_qkv", "L0_conv_w_dw", "L0_conv_b_dw", "L0_conv_temperature",
        "L0_conv_w_out", "L0_conv_b_out"]


def kernel(**inputs):
    import numpy as np
    import concourse.bacc as bacc
    from concourse import mybir as my
    from concourse.bass_utils import run_bass_kernel_spmd

    nc = bacc.Bacc("TRN2", target_bir_lowering=False, num_devices=1)
    arrays, args = {}, []
    for name in _INS:
        a = np.ascontiguousarray(inputs[name])
        arrays[f"in_{name}"] = a
        args.append(nc.dram_tensor(f"in_{name}", a.shape, my.dt.from_np(a.dtype), kind="ExternalInput").ap())
    out = nc.dram_tensor("out_0", (B, H, W, C), F32, kind="ExternalOutput").ap()
    build(nc, *args, out)
    r = run_bass_kernel_spmd(nc, [arrays], core_ids=[0])
    return r.results[0]["out_0"]
```
